# Optimizing a Trainium2 kernel written in Bass

```python
import numpy as np
import jax
import jax.numpy as jnp

def _softmax(x, axis=-1):
    return jax.nn.softmax(x, axis=axis)

def _gelu(x):
    return jax.nn.gelu(x, approximate=True)

def _silu(x):
    return jax.nn.silu(x)

def _sigmoid(x):
    return jax.nn.sigmoid(x)

def _layernorm(x, axis=-1, eps=1e-05):
    m = jnp.mean(x, axis=axis, keepdims=True)
    v = jnp.var(x, axis=axis, keepdims=True)
    return (x - m) / jnp.sqrt(v + eps)

def _scatter_add(tgt, idx, src, axis=0):
    return tgt.at[idx].add(src)

def _segment_sum(src, seg, n):
    return jax.ops.segment_sum(src, seg, n)
kernel_name = 'mk_adaln_d2_jaxref_r8_fae68e'

def setup_inputs(seed: int=0):
    np.random.seed(seed)
    _w = jnp.asarray

    def _L0_attn_setup():
        import jax, jax.numpy as jnp
        import numpy as np
        H = 128
        NH = 16
        L = 4
        B = 4
        N = 256
        EPS_LN = 1e-12

        def gelu(x):
            return jax.nn.gelu(x, approximate=False)

        def layernorm(x, g, b):
            m = jnp.mean(x, axis=-1, keepdims=True)
            v = jnp.mean((x - m) ** 2, axis=-1, keepdims=True)
            return (x - m) / jnp.sqrt(v + EPS_LN) * g + b

        def conv1d_grouped(x, w, b, groups):
            y = jax.lax.conv_general_dilated(x, w, window_strides=(1,), padding=[(2, 2)], dimension_numbers=('NCH', 'OIH', 'NCH'), feature_group_count=groups)
            return y + b[None, :, None]

        def rope(x):
            b, n, c = x.shape
            half = c // 2
            inv = 1.0 / 10000.0 ** (jnp.arange(0, c, 2, dtype=jnp.float32) / c)
            freqs = jnp.arange(n, dtype=jnp.float32)[:, None] * inv[None, :]
            freqs = jnp.repeat(freqs, 2, axis=-1)
            cos, sin = (jnp.cos(freqs), jnp.sin(freqs))
            xp = x.reshape(b, n, half, 2)
            xr = jnp.stack([-xp[..., 1], xp[..., 0]], axis=-1).reshape(b, n, c)
            return x * cos + xr * sin

        def linear_attention(x, Wq, bq, Wk, bk, Wv, bv, g, bb):
            b, n, c = x.shape
            hd = c // NH
            q = gelu(x @ Wq + bq) + 0.21
            k = gelu(x @ Wk + bk) + 0.21
            v = x @ Wv + bv
            q_r = rope(q)
            k_r = rope(k)
            to_h = lambda t: t.reshape(b, n, NH, hd).transpose(0, 2, 1, 3)
            q, k, v, q_r, k_r = map(to_h, (q, k, v, q_r, k_r))
            kmean = jnp.mean(k, axis=2, keepdims=True)
            z = 1.0 / (jnp.einsum('bhnd,bhmd->bhnm', q, kmean) + 1e-06)
            kv = jnp.einsum('bhnd,bhne->bhde', k_r, v) / n
            out = jnp.einsum('bhnd,bhde->bhne', q_r, kv) * z
            out = out.transpose(0, 2, 1, 3).reshape(b, n, c)
            return layernorm(out + x, g, bb)
        key = jax.random.key(seed)
        ks = jax.random.split(key, 10)
        s = 0.02
        r = lambda k, sh: jax.random.normal(k, sh, dtype=jnp.float32) * s
        d = {}
        d['x'] = jax.random.normal(ks[0], (B, N, H), dtype=jnp.float32)
        d['conv1_w'] = r(ks[1], (4 * H, 1, 5))
        d['conv1_b'] = jnp.zeros((4 * H,), jnp.float32)
        d['conv2_w'] = r(ks[2], (H, 4, 5))
        d['conv2_b'] = jnp.zeros((H,), jnp.float32)
        d['ln0_g'] = jnp.ones((H,), jnp.float32)
        d['ln0_b'] = jnp.zeros((H,), jnp.float32)
        d['Wq'] = r(ks[3], (L, H, H))
        d['bq'] = jnp.zeros((L, H), jnp.float32)
        d['Wk'] = r(ks[4], (L, H, H))
        d['bk'] = jnp.zeros((L, H), jnp.float32)
        d['Wv'] = r(ks[5], (L, H, H))
        d['bv'] = jnp.zeros((L, H), jnp.float32)
        d['lnA_g'] = jnp.ones((L, H), jnp.float32)
        d['lnA_b'] = jnp.zeros((L, H), jnp.float32)
        d['W1'] = r(ks[6], (H, 4 * H))
        d['b1'] = jnp.zeros((4 * H,), jnp.float32)
        d['W2'] = r(ks[7], (4 * H, H))
        d['b2'] = jnp.zeros((H,), jnp.float32)
        d['ln2_g'] = jnp.ones((H,), jnp.float32)
        d['ln2_b'] = jnp.zeros((H,), jnp.float32)
        return d
    _L0_attn_in = _L0_attn_setup()

    def _L0_ffn_setup():
        import jax, jax.numpy as jnp
        import numpy as np
        B, L, D = (4, 64, 128)
        E, TOP_K = (16, 4)
        F = 4 * D
        key = jax.random.key(seed)
        ks = jax.random.split(key, 6)
        scale = 0.02
        return {'x': jax.random.normal(ks[0], (B, L, D), jnp.float32), 'keys': jax.random.normal(ks[1], (E, D), jnp.float32), 'w1': jax.random.normal(ks[2], (E, F, D), jnp.float32) * scale, 'b1': jnp.zeros((E, F), jnp.float32), 'w2': jax.random.normal(ks[3], (E, D, F), jnp.float32) * scale, 'b2': jnp.zeros((E, D), jnp.float32), 'rw': jax.random.normal(ks[4], (E, D), jnp.float32) * scale, 'rb': jnp.zeros((E,), jnp.float32)}
    _L0_ffn_in = _L0_ffn_setup()
    _L0_c = _w((lambda *s: np.random.randn(*s).astype(np.float32) * 0.05)(4, 128))
    _L0_wmod = _w((lambda *s: np.random.randn(*s).astype(np.float32) * 0.05)(128, 6 * 128) * 128 ** (-0.5))

    def _L1_attn_setup():
        import jax, jax.numpy as jnp
        import numpy as np
        NEG_FILL = jnp.finfo(jnp.float32).min
        key = jax.random.key(seed)
        k0, k1, k2, k3, k4 = jax.random.split(key, 5)
        B, N, E, D = (4, 512, 128, 32)
        STD = 0.05
        inputs = jax.random.normal(k0, (B, N, E), dtype=jnp.float32)
        Wq = STD * jax.random.normal(k1, (E, D), dtype=jnp.float32)
        Wk = STD * jax.random.normal(k2, (E, D), dtype=jnp.float32)
        Wvdown = STD * jax.random.normal(k3, (E, D), dtype=jnp.float32)
        Wvup = STD * jax.random.normal(k4, (D, E), dtype=jnp.float32)
        return {'inputs': inputs, 'Wq': Wq, 'Wk': Wk, 'Wvdown': Wvdown, 'Wvup': Wvup}
    _L1_attn_in = _L1_attn_setup()

    def _L1_ffn_setup():
        import jax, jax.numpy as jnp
        import numpy as np
        DIM = 128
        DEPTH = 6
        HEADS = 16
        DIM_HEAD = 64
        WINDOW = 32
        INNER = HEADS * DIM_HEAD
        DIM_INNER = int(DIM * 4 * 2 / 3)
        QK_SCALE = 8.0

        def shift_tokens(t):
            a, s = jnp.split(t, 2, -1)
            s = jnp.pad(s, ((0, 0), (1, 0), (0, 0)))[:, :-1]
            return jnp.concatenate([a, s], -1)

        def l2norm(t):
            return t / jnp.maximum(jnp.linalg.norm(t, axis=-1, keepdims=True), 1e-12)

        def rotate_half(x):
            x1, x2 = jnp.split(x, 2, -1)
            return jnp.concatenate([-x2, x1], -1)

        def rotary_tables(n):
            half = jnp.arange(0, DIM_HEAD, 2, dtype=jnp.float32)
            inv_freq = 1.0 / 10000.0 ** (half / DIM_HEAD)
            t = jnp.arange(n, dtype=jnp.float32)
            freqs = t[:, None] * inv_freq[None, :]
            freqs = jnp.concatenate([freqs, freqs], -1)
            base_scale = (half + 0.4 * DIM_HEAD) / (1.4 * DIM_HEAD)
            power = (t - n // 2) / (WINDOW // 2)
            scale = base_scale[None, :] ** power[:, None]
            scale = jnp.concatenate([scale, scale], -1)
            return (freqs, scale)

        def local_attention(q, k, v):
            b, h, n, d = q.shape
            w = WINDOW
            nw = n // w
            bq = q.reshape(b, h, nw, w, d)
            bk = k.reshape(b, h, nw, w, d)
            bv = v.reshape(b, h, nw, w, d)

            def look(t):
                p = jnp.pad(t, ((0, 0), (0, 0), (1, 0), (0, 0), (0, 0)))
                return jnp.concatenate([p[:, :, :nw], p[:, :, 1:]], axis=3)
            bk2, bv2 = (look(bk), look(bv))
            seq = jnp.arange(n).reshape(nw, w)
            seq_p = jnp.pad(seq, ((1, 0), (0, 0)), constant_values=-1)
            jt = jnp.concatenate([seq_p[:nw], seq_p[1:]], axis=1)
            it = seq[:, :, None]
            jb = jt[:, None, :]
            mask = (it < jb) | (it > jb + w) | (jb == -1)
            sim = jnp.einsum('bhwie,bhwje->bhwij', bq, bk2) * QK_SCALE
            sim = jnp.where(mask, -jnp.finfo(sim.dtype).max, sim)
            attn = jax.nn.softmax(sim, -1)
            out = jnp.einsum('bhwij,bhwje->bhwie', attn, bv2)
            return out.reshape(b, h, n, d)

        def attn_layer(x, Wqkv, qs, ksc, Wo):
            b, n, _ = x.shape
            qkv = x @ Wqkv
            q, k, v = jnp.split(qkv, 3, -1)
            sh = lambda t: t.reshape(b, n, HEADS, DIM_HEAD).transpose(0, 2, 1, 3)
            q, k, v = (sh(q), sh(k), sh(v))
            q = l2norm(q) * qs
            k = l2norm(k) * ksc
            freqs, scale = rotary_tables(n)
            cos, sin = (jnp.cos(freqs), jnp.sin(freqs))
            q = q * cos * scale + rotate_half(q) * sin * scale
            inv = 1.0 / scale
            k = k * cos * inv + rotate_half(k) * sin * inv
            out = local_attention(q, k, v)
            out = out.transpose(0, 2, 1, 3).reshape(b, n, INNER)
            return out @ Wo

        def ffn_layer(x, g, bln, W1, b1, W2, b2):
            mu = x.mean(-1, keepdims=True)
            var = ((x - mu) ** 2).mean(-1, keepdims=True)
            xn = (x - mu) / jnp.sqrt(var + 1e-05) * g + bln
            hg = xn @ W1 + b1
            a, gate = jnp.split(hg, 2, -1)
            return a * jax.nn.gelu(gate, approximate=False) @ W2 + b2
        key = jax.random.key(seed)
        ks = jax.random.split(key, 8)
        B, N = (2, 256)
        init = lambda k, shape: jax.random.normal(k, shape, jnp.float32) * 0.02
        return {'x': jax.random.normal(ks[0], (B, N, DIM), jnp.float32), 'Wqkv': init(ks[1], (DEPTH, DIM, 3 * INNER)), 'q_scale': jnp.ones((DEPTH, DIM_HEAD), jnp.float32), 'k_scale': jnp.ones((DEPTH, DIM_HEAD), jnp.float32), 'Wo': init(ks[2], (DEPTH, INNER, DIM)), 'ln_g': jnp.ones((DEPTH, DIM), jnp.float32), 'ln_b': jnp.zeros((DEPTH, DIM), jnp.float32), 'W1': init(ks[3], (DEPTH, DIM, 2 * DIM_INNER)), 'b1': jnp.zeros((DEPTH, 2 * DIM_INNER), jnp.float32), 'W2': init(ks[4], (DEPTH, DIM_INNER, DIM)), 'b2': jnp.zeros((DEPTH, DIM), jnp.float32)}
    _L1_ffn_in = _L1_ffn_setup()
    _L1_c = _w((lambda *s: np.random.randn(*s).astype(np.float32) * 0.05)(4, 128))
    _L1_wmod = _w((lambda *s: np.random.randn(*s).astype(np.float32) * 0.05)(128, 6 * 128) * 128 ** (-0.5))
    _d = {'L0_attn_x': _L0_attn_in['x'], 'L0_attn_conv1_w': _L0_attn_in['conv1_w'], 'L0_attn_conv1_b': _L0_attn_in['conv1_b'], 'L0_attn_conv2_w': _L0_attn_in['conv2_w'], 'L0_attn_conv2_b': _L0_attn_in['conv2_b'], 'L0_attn_ln0_g': _L0_attn_in['ln0_g'], 'L0_attn_ln0_b': _L0_attn_in['ln0_b'], 'L0_attn_Wq': _L0_attn_in['Wq'], 'L0_attn_bq': _L0_attn_in['bq'], 'L0_attn_Wk': _L0_attn_in['Wk'], 'L0_attn_bk': _L0_attn_in['bk'], 'L0_attn_Wv': _L0_attn_in['Wv'], 'L0_attn_bv': _L0_attn_in['bv'], 'L0_attn_lnA_g': _L0_attn_in['lnA_g'], 'L0_attn_lnA_b': _L0_attn_in['lnA_b'], 'L0_attn_W1': _L0_attn_in['W1'], 'L0_attn_b1': _L0_attn_in['b1'], 'L0_attn_W2': _L0_attn_in['W2'], 'L0_attn_b2': _L0_attn_in['b2'], 'L0_attn_ln2_g': _L0_attn_in['ln2_g'], 'L0_attn_ln2_b': _L0_attn_in['ln2_b'], 'L0_ffn_keys': _L0_ffn_in['keys'], 'L0_ffn_w1': _L0_ffn_in['w1'], 'L0_ffn_b1': _L0_ffn_in['b1'], 'L0_ffn_w2': _L0_ffn_in['w2'], 'L0_ffn_b2': _L0_ffn_in['b2'], 'L0_ffn_rw': _L0_ffn_in['rw'], 'L0_ffn_rb': _L0_ffn_in['rb'], 'L0_c': _L0_c, 'L0_wmod': _L0_wmod, 'L1_attn_Wq': _L1_attn_in['Wq'], 'L1_attn_Wk': _L1_attn_in['Wk'], 'L1_attn_Wvdown': _L1_attn_in['Wvdown'], 'L1_attn_Wvup': _L1_attn_in['Wvup'], 'L1_ffn_Wqkv': _L1_ffn_in['Wqkv'], 'L1_ffn_q_scale': _L1_ffn_in['q_scale'], 'L1_ffn_k_scale': _L1_ffn_in['k_scale'], 'L1_ffn_Wo': _L1_ffn_in['Wo'], 'L1_ffn_ln_g': _L1_ffn_in['ln_g'], 'L1_ffn_ln_b': _L1_ffn_in['ln_b'], 'L1_ffn_W1': _L1_ffn_in['W1'], 'L1_ffn_b1': _L1_ffn_in['b1'], 'L1_ffn_W2': _L1_ffn_in['W2'], 'L1_ffn_b2': _L1_ffn_in['b2'], 'L1_c': _L1_c, 'L1_wmod': _L1_wmod}
    _x0 = _d['L0_attn_x']
    _d['L0_attn_x'] = jax.random.normal(jax.random.fold_in(jax.random.key(seed), 1), (4, 512, 128), dtype=_x0.dtype)
    del _x0
    return _d

def reference(L0_attn_x, L0_attn_conv1_w, L0_attn_conv1_b, L0_attn_conv2_w, L0_attn_conv2_b, L0_attn_ln0_g, L0_attn_ln0_b, L0_attn_Wq, L0_attn_bq, L0_attn_Wk, L0_attn_bk, L0_attn_Wv, L0_attn_bv, L0_attn_lnA_g, L0_attn_lnA_b, L0_attn_W1, L0_attn_b1, L0_attn_W2, L0_attn_b2, L0_attn_ln2_g, L0_attn_ln2_b, L0_ffn_keys, L0_ffn_w1, L0_ffn_b1, L0_ffn_w2, L0_ffn_b2, L0_ffn_rw, L0_ffn_rb, L0_c, L0_wmod, L1_attn_Wq, L1_attn_Wk, L1_attn_Wvdown, L1_attn_Wvup, L1_ffn_Wqkv, L1_ffn_q_scale, L1_ffn_k_scale, L1_ffn_Wo, L1_ffn_ln_g, L1_ffn_ln_b, L1_ffn_W1, L1_ffn_b1, L1_ffn_W2, L1_ffn_b2, L1_c, L1_wmod):

    def _L0_attn_ref(x, conv1_w, conv1_b, conv2_w, conv2_b, ln0_g, ln0_b, Wq, bq, Wk, bk, Wv, bv, lnA_g, lnA_b, W1, b1, W2, b2, ln2_g, ln2_b):
        import jax, jax.numpy as jnp
        import numpy as np
        H = 128
        NH = 16
        L = 4
        B = 4
        N = 256
        EPS_LN = 1e-12

        def gelu(x):
            return jax.nn.gelu(x, approximate=False)

        def layernorm(x, g, b):
            m = jnp.mean(x, axis=-1, keepdims=True)
            v = jnp.mean((x - m) ** 2, axis=-1, keepdims=True)
            return (x - m) / jnp.sqrt(v + EPS_LN) * g + b

        def conv1d_grouped(x, w, b, groups):
            y = jax.lax.conv_general_dilated(x, w, window_strides=(1,), padding=[(2, 2)], dimension_numbers=('NCH', 'OIH', 'NCH'), feature_group_count=groups)
            return y + b[None, :, None]

        def rope(x):
            b, n, c = x.shape
            half = c // 2
            inv = 1.0 / 10000.0 ** (jnp.arange(0, c, 2, dtype=jnp.float32) / c)
            freqs = jnp.arange(n, dtype=jnp.float32)[:, None] * inv[None, :]
            freqs = jnp.repeat(freqs, 2, axis=-1)
            cos, sin = (jnp.cos(freqs), jnp.sin(freqs))
            xp = x.reshape(b, n, half, 2)
            xr = jnp.stack([-xp[..., 1], xp[..., 0]], axis=-1).reshape(b, n, c)
            return x * cos + xr * sin

        def linear_attention(x, Wq, bq, Wk, bk, Wv, bv, g, bb):
            b, n, c = x.shape
            hd = c // NH
            q = gelu(x @ Wq + bq) + 0.21
            k = gelu(x @ Wk + bk) + 0.21
            v = x @ Wv + bv
            q_r = rope(q)
            k_r = rope(k)
            to_h = lambda t: t.reshape(b, n, NH, hd).transpose(0, 2, 1, 3)
            q, k, v, q_r, k_r = map(to_h, (q, k, v, q_r, k_r))
            kmean = jnp.mean(k, axis=2, keepdims=True)
            z = 1.0 / (jnp.einsum('bhnd,bhmd->bhnm', q, kmean) + 1e-06)
            kv = jnp.einsum('bhnd,bhne->bhde', k_r, v) / n
            out = jnp.einsum('bhnd,bhde->bhne', q_r, kv) * z
            out = out.transpose(0, 2, 1, 3).reshape(b, n, c)
            return layernorm(out + x, g, bb)
        b, n, c = x.shape
        h = x.transpose(0, 2, 1)
        h = conv1d_grouped(h, conv1_w, conv1_b, c)
        h = gelu(h)
        h = conv1d_grouped(h, conv2_w, conv2_b, c)
        h = h.transpose(0, 2, 1)
        h = layernorm(h + x, ln0_g, ln0_b)
        for i in range(Wq.shape[0]):
            h = linear_attention(h, Wq[i], bq[i], Wk[i], bk[i], Wv[i], bv[i], lnA_g[i], lnA_b[i])
        f = gelu(h @ W1 + b1) @ W2 + b2
        return layernorm(f + h, ln2_g, ln2_b)

    def _L0_ffn_ref(x, keys, w1, b1, w2, b2, rw, rb):
        import jax, jax.numpy as jnp
        import numpy as np
        B, L, D = (4, 64, 128)
        E, TOP_K = (16, 4)
        F = 4 * D
        diff = x[:, :, None, :] - keys
        dist2 = jnp.sum(diff * diff, axis=-1)
        logits = -dist2 + jnp.einsum('bld,ed->ble', x, rw) + rb
        topv, topi = jax.lax.top_k(logits, TOP_K)
        w = jax.nn.softmax(topv, axis=-1)
        hidden = jax.nn.gelu(jnp.einsum('bld,efd->blef', x, w1) + b1, approximate=False)
        exp_out = jnp.einsum('blef,edf->bled', hidden, w2) + b2
        sel = jnp.take_along_axis(exp_out, topi[..., None], axis=2)
        fused = jnp.sum(w[..., None] * sel, axis=2)
        return fused

    def _L1_attn_ref(inputs, Wq, Wk, Wvdown, Wvup):
        import jax, jax.numpy as jnp
        import numpy as np
        NEG_FILL = jnp.finfo(jnp.float32).min
        B, N, E = inputs.shape
        D = Wq.shape[1]
        Q = inputs @ Wq
        K = inputs @ Wk
        score = jnp.einsum('bqd,bkd->bqk', Q, K)
        score = score / jnp.sqrt(jnp.float32(D))
        causal = jnp.tril(jnp.ones((N, N), dtype=bool))
        score = jnp.where(causal, score, 0.0)
        score = jnp.where(score != 0, score, NEG_FILL)
        attn = jax.nn.softmax(score, axis=-1)
        V = inputs @ (Wvdown @ Wvup)
        return attn @ V

    def _L1_ffn_ref(x, Wqkv, q_scale, k_scale, Wo, ln_g, ln_b, W1, b1, W2, b2):
        import jax, jax.numpy as jnp
        import numpy as np
        DIM = 128
        DEPTH = 6
        HEADS = 16
        DIM_HEAD = 64
        WINDOW = 32
        INNER = HEADS * DIM_HEAD
        DIM_INNER = int(DIM * 4 * 2 / 3)
        QK_SCALE = 8.0

        def shift_tokens(t):
            a, s = jnp.split(t, 2, -1)
            s = jnp.pad(s, ((0, 0), (1, 0), (0, 0)))[:, :-1]
            return jnp.concatenate([a, s], -1)

        def l2norm(t):
            return t / jnp.maximum(jnp.linalg.norm(t, axis=-1, keepdims=True), 1e-12)

        def rotate_half(x):
            x1, x2 = jnp.split(x, 2, -1)
            return jnp.concatenate([-x2, x1], -1)

        def rotary_tables(n):
            half = jnp.arange(0, DIM_HEAD, 2, dtype=jnp.float32)
            inv_freq = 1.0 / 10000.0 ** (half / DIM_HEAD)
            t = jnp.arange(n, dtype=jnp.float32)
            freqs = t[:, None] * inv_freq[None, :]
            freqs = jnp.concatenate([freqs, freqs], -1)
            base_scale = (half + 0.4 * DIM_HEAD) / (1.4 * DIM_HEAD)
            power = (t - n // 2) / (WINDOW // 2)
            scale = base_scale[None, :] ** power[:, None]
            scale = jnp.concatenate([scale, scale], -1)
            return (freqs, scale)

        def local_attention(q, k, v):
            b, h, n, d = q.shape
            w = WINDOW
            nw = n // w
            bq = q.reshape(b, h, nw, w, d)
            bk = k.reshape(b, h, nw, w, d)
            bv = v.reshape(b, h, nw, w, d)

            def look(t):
                p = jnp.pad(t, ((0, 0), (0, 0), (1, 0), (0, 0), (0, 0)))
                return jnp.concatenate([p[:, :, :nw], p[:, :, 1:]], axis=3)
            bk2, bv2 = (look(bk), look(bv))
            seq = jnp.arange(n).reshape(nw, w)
            seq_p = jnp.pad(seq, ((1, 0), (0, 0)), constant_values=-1)
            jt = jnp.concatenate([seq_p[:nw], seq_p[1:]], axis=1)
            it = seq[:, :, None]
            jb = jt[:, None, :]
            mask = (it < jb) | (it > jb + w) | (jb == -1)
            sim = jnp.einsum('bhwie,bhwje->bhwij', bq, bk2) * QK_SCALE
            sim = jnp.where(mask, -jnp.finfo(sim.dtype).max, sim)
            attn = jax.nn.softmax(sim, -1)
            out = jnp.einsum('bhwij,bhwje->bhwie', attn, bv2)
            return out.reshape(b, h, n, d)

        def attn_layer(x, Wqkv, qs, ksc, Wo):
            b, n, _ = x.shape
            qkv = x @ Wqkv
            q, k, v = jnp.split(qkv, 3, -1)
            sh = lambda t: t.reshape(b, n, HEADS, DIM_HEAD).transpose(0, 2, 1, 3)
            q, k, v = (sh(q), sh(k), sh(v))
            q = l2norm(q) * qs
            k = l2norm(k) * ksc
            freqs, scale = rotary_tables(n)
            cos, sin = (jnp.cos(freqs), jnp.sin(freqs))
            q = q * cos * scale + rotate_half(q) * sin * scale
            inv = 1.0 / scale
            k = k * cos * inv + rotate_half(k) * sin * inv
            out = local_attention(q, k, v)
            out = out.transpose(0, 2, 1, 3).reshape(b, n, INNER)
            return out @ Wo

        def ffn_layer(x, g, bln, W1, b1, W2, b2):
            mu = x.mean(-1, keepdims=True)
            var = ((x - mu) ** 2).mean(-1, keepdims=True)
            xn = (x - mu) / jnp.sqrt(var + 1e-05) * g + bln
            hg = xn @ W1 + b1
            a, gate = jnp.split(hg, 2, -1)
            return a * jax.nn.gelu(gate, approximate=False) @ W2 + b2
        for i in range(DEPTH):
            x = attn_layer(shift_tokens(x), Wqkv[i], q_scale[i], k_scale[i], Wo[i]) + x
            x = ffn_layer(shift_tokens(x), ln_g[i], ln_b[i], W1[i], b1[i], W2[i], b2[i]) + x
        return x
    x = L0_attn_x
    mod = (_silu(L0_c) @ L0_wmod).reshape(L0_c.shape[0], 6, 1, -1)
    sa, ca, ga, sb, cb, gb = (mod[:, 0], mod[:, 1], mod[:, 2], mod[:, 3], mod[:, 4], mod[:, 5])
    ga = (2 * (ga >= 0) - 1) * jnp.maximum(jnp.abs(ga), 0.25)
    gb = (2 * (gb >= 0) - 1) * jnp.maximum(jnp.abs(gb), 0.25)
    h = _layernorm(x, axis=-1) * (1 + ca) + sa
    x = x + ga * _L0_attn_ref(h, L0_attn_conv1_w, L0_attn_conv1_b, L0_attn_conv2_w, L0_attn_conv2_b, L0_attn_ln0_g, L0_attn_ln0_b, L0_attn_Wq, L0_attn_bq, L0_attn_Wk, L0_attn_bk, L0_attn_Wv, L0_attn_bv, L0_attn_lnA_g, L0_attn_lnA_b, L0_attn_W1, L0_attn_b1, L0_attn_W2, L0_attn_b2, L0_attn_ln2_g, L0_attn_ln2_b)
    h = _layernorm(x, axis=-1) * (1 + cb) + sb
    x = x + gb * _L0_ffn_ref(h, L0_ffn_keys, L0_ffn_w1, L0_ffn_b1, L0_ffn_w2, L0_ffn_b2, L0_ffn_rw, L0_ffn_rb)
    mod = (_silu(L1_c) @ L1_wmod).reshape(L1_c.shape[0], 6, 1, -1)
    sa, ca, ga, sb, cb, gb = (mod[:, 0], mod[:, 1], mod[:, 2], mod[:, 3], mod[:, 4], mod[:, 5])
    ga = (2 * (ga >= 0) - 1) * jnp.maximum(jnp.abs(ga), 0.25)
    gb = (2 * (gb >= 0) - 1) * jnp.maximum(jnp.abs(gb), 0.25)
    h = _layernorm(x, axis=-1) * (1 + ca) + sa
    x = x + ga * _L1_attn_ref(h, L1_attn_Wq, L1_attn_Wk, L1_attn_Wvdown, L1_attn_Wvup)
    h = _layernorm(x, axis=-1) * (1 + cb) + sb
    x = x + gb * _L1_ffn_ref(h, L1_ffn_Wqkv, L1_ffn_q_scale, L1_ffn_k_scale, L1_ffn_Wo, L1_ffn_ln_g, L1_ffn_ln_b, L1_ffn_W1, L1_ffn_b1, L1_ffn_W2, L1_ffn_b2)
    return x

_drawn_inputs = setup_inputs


def setup_inputs(seed=0):
    import zlib

    import numpy as np

    out = dict(_drawn_inputs(seed))
    spreads = {'L0_attn_conv1_b': (0.0, 0.8),
     'L0_attn_conv2_b': (0.0, 0.313),
     'L0_attn_ln0_g': (1.0, 0.2),
     'L0_attn_ln0_b': (0.0, 0.368),
     'L0_attn_bq': (0.0, 0.8),
     'L0_attn_bk': (0.0, 0.8),
     'L0_attn_bv': (0.0, 0.286),
     'L0_attn_lnA_g': (1.0, 0.2),
     'L0_attn_lnA_b': (0.0, 0.1),
     'L0_attn_b1': (0.0, 0.8),
     'L0_attn_b2': (0.0, 0.287),
     'L0_attn_ln2_g': (1.0, 0.2),
     'L0_attn_ln2_b': (0.0, 0.297),
     'L0_ffn_b1': (0.0, 0.8),
     'L0_ffn_b2': (0.0, 0.336),
     'L0_ffn_rb': (0.0, 0.8),
     'L1_ffn_q_scale': (1.0, 0.6),
     'L1_ffn_k_scale': (1.0, 0.6),
     'L1_ffn_ln_g': (1.0, 0.6),
     'L1_ffn_ln_b': (0.0, 0.8),
     'L1_ffn_b1': (0.0, 0.8),
     'L1_ffn_b2': (0.0, 0.633)}
    factors = {'L0_attn_conv1_w': 8.0,
     'L0_attn_conv2_w': 8.0,
     'L0_attn_Wq': 8.0,
     'L0_attn_Wk': 8.0,
     'L0_attn_Wv': 4.289,
     'L0_attn_W1': 4.238,
     'L0_attn_W2': 3.925,
     'L0_ffn_w1': 4.459,
     'L0_ffn_w2': 4.004,
     'L0_ffn_rw': 8.0,
     'L1_attn_Wq': 8.0,
     'L1_attn_Wk': 8.0,
     'L1_attn_Wvdown': 8.0,
     'L1_attn_Wvup': 8.0,
     'L1_ffn_W1': 7.612,
     'L1_ffn_W2': 7.454}
    for name, (base, spread) in spreads.items():
        noise = np.random.default_rng([zlib.crc32(name.encode()), seed]).standard_normal(out[name].shape)
        drawn = base * np.exp(spread * noise) if base else spread * noise
        out[name] = jnp.asarray(drawn.astype(out[name].dtype))
    for name, factor in factors.items():
        out[name] = (out[name] * factor).astype(out[name].dtype)
    return out
```

```python
from contextlib import ExitStack

import numpy as np

import concourse.bass as bass
from concourse import mybir

F32 = mybir.dt.float32
BF16 = mybir.dt.bfloat16
I32 = mybir.dt.int32
ALU = mybir.AluOpType
ACT = mybir.ActivationFunctionType
AX_X = mybir.AxisListType.X
ds = bass.ds

D = 128
NB, N = 4, 512
T = NB * N
TILES = N // 128
MAGIC = float(0x5F3759DF)


class Chain:

    def __init__(self, eng, sem, per_iteration=0, iteration=0):
        self.eng, self.sem, self.n = eng, sem, 0
        self.per, self.base = per_iteration, per_iteration * iteration

    def inc(self, instruction):
        self.n += 1
        instruction.then_inc(self.sem, 1)
        return self.n

    def wait(self, mark):
        self.eng.wait_ge(self.sem, self.base + mark)

    def link(self, instruction):
        self.wait(self.inc(instruction))

    def end(self):
        assert self.n == self.per, (self.n, self.per)


def rsqrt(dve, ch, y, x, half, tmp, eps):
    ch.link(dve.tensor_scalar(half, x, float(eps), None, ALU.add))
    ch.link(dve.tensor_scalar(y.bitcast(I32), half.bitcast(I32), -0.5, MAGIC, ALU.mult, ALU.add))
    ch.link(dve.tensor_scalar(half, half, -0.5, None, ALU.mult))
    for _ in range(3):
        ch.link(dve.tensor_tensor(tmp, y, y, ALU.mult))
        ch.link(dve.tensor_tensor(tmp, tmp, half, ALU.mult))
        ch.link(dve.scalar_tensor_tensor(out=y, in0=tmp, scalar=1.5, in1=y, op0=ALU.add, op1=ALU.mult))


def norm_tokens(c, dve, ch, out, src, stats, mv, rs, eps):
    marks = [ch.inc(dve.bn_stats(stats[:, t, :], src[:, t, :])) for t in range(TILES)]
    c.wait_apart(dve, ch.sem, ch.base + marks[-1])
    marks = [ch.inc(dve.bn_aggr(mv[:, t, :], stats[:, t, :])) for t in range(TILES)]
    ch.wait(marks[-1])
    rsqrt(dve, ch, rs[:, 0, :], mv[:, :, 1], rs[:, 1, :], rs[:, 2, :], eps)
    for t in range(TILES):
        last = dve.tensor_scalar(out[:, t, :], src[:, t, :], mv[:, t, 0:1], rs[:, 0, t:t + 1],
                                 ALU.subtract, ALU.mult)
        if t < TILES - 1:
            ch.inc(last)
    return last


class Core:

    def __init__(self, nc, ins, stack):
        self.nc, self.ins, self.stack = nc, ins, stack
        self.stage = stack

    def sb(self, name, shape, dt=F32, keep=False):
        return (self.stack if keep else self.stage).enter_context(self.nc.sbuf_tensor(name, shape, dt))

    def ps(self, name, shape=(128, 512), dt=F32):
        return self.stage.enter_context(self.nc.psum_tensor(name, list(shape), dt))

    def wait_apart(self, eng, sem, value):
        wait(eng, sem, value)
        if not isinstance(value, int):
            eng.sem_inc(self.passed)

    def sem(self, name, keep=False):
        return (self.stack if keep else self.stage).enter_context(self.nc.semaphore(name))


def wait(eng, sem, value):
    if not isinstance(value, int) or value > 0:
        eng.wait_ge(sem, value)


def shape_constants():
    out = {}
    inv = (1.0 / 10000.0 ** (np.arange(0, D, 2, dtype=np.float32) / np.float32(D))).astype(np.float32)
    freqs = np.repeat(np.arange(N, dtype=np.float32)[:, None] * inv[None, :], 2, axis=-1)
    cos, sin = np.cos(freqs).astype(np.float32), np.sin(freqs).astype(np.float32)
    by_tile = lambda a: a.reshape(TILES, 128, -1).transpose(1, 0, 2)
    out["cos_tok"], out["sin_tok"] = by_tile(cos), by_tile(sin)
    out["cos_feat"], out["sin_feat"] = cos.T, sin.T
    rot = np.zeros((D, D), np.float32)
    rot[np.arange(0, D, 2), np.arange(1, D, 2)] = -1
    rot[np.arange(1, D, 2), np.arange(0, D, 2)] = 1
    out["rot"], out["rot_t"] = rot, rot.T
    out["ident"] = np.eye(D, dtype=np.float32)
    head = np.kron(np.eye(16), np.ones((8, 8))).astype(np.float32)
    out["headmask"] = np.stack([head, head], axis=1)
    out["ones_n"] = np.full((D, D), 1.0 / N, np.float32)
    out["ones"] = np.ones((D, D), np.float32)
    half = np.arange(0, 64, 2, dtype=np.float32)
    fr = np.arange(N, dtype=np.float32)[:, None] * (1.0 / 10000.0 ** (half / 64)).astype(np.float32)[None, :]
    base = ((half + np.float32(0.4 * 64)) / np.float32(1.4 * 64)).astype(np.float32)
    power = ((np.arange(N, dtype=np.float32) - N // 2) / 16).astype(np.float32)
    scale = (base[None, :] ** power[:, None]).astype(np.float32)
    c1, s1 = np.cos(fr).astype(np.float32), np.sin(fr).astype(np.float32)
    for kind, f in (("q", scale), ("k", (1.0 / scale).astype(np.float32))):
        out["rope_cos_" + kind] = by_tile(np.concatenate([c1 * f, c1 * f], -1))
        out["rope_sin_" + kind] = by_tile(np.concatenate([-s1 * f, s1 * f], -1))
    out["causal"] = by_tile(np.tril(np.ones((N, N), np.float32)))
    qpos, kpos = np.tile(np.arange(64), 2)[:, None], np.arange(-32, 64)[None, :]
    band = (qpos - kpos >= 0) & (qpos - kpos <= 32)
    out["band"] = np.stack([np.tile(np.where(m, 0.0, -1e30), (1, 4)) for m in (band & (kpos >= 0), band)],
                           axis=1).astype(np.float32)
    return {k: np.ascontiguousarray(v, np.float32) for k, v in out.items()}


GROUPS = {
    "all": ("ident", "ones", "band"),
    "L0": ("cos_tok", "sin_tok", "cos_feat", "sin_feat", "rot", "rot_t", "headmask", "ones_n"),
    "L1": ("causal", "rope_cos_q", "rope_sin_q", "rope_cos_k", "rope_sin_k"),
}


def group_array(group):
    tables = shape_constants()
    return np.concatenate([tables[name].reshape(128, -1) for name in GROUPS[group]], 1)


def place_tables(c):
    tables = shape_constants()
    width = {g: sum(tables[name].size // 128 for name in names) for g, names in GROUPS.items()}
    c.tables_all = c.sb("tables_all", [128, width["all"]], keep=True)
    both = c.sb("tables_layer", [128, max(width["L0"], width["L1"])], keep=True)
    c.tables_0, c.tables_1 = both[:, 0:width["L0"]], both[:, 0:width["L1"]]
    views = {}
    for group, buf in (("all", c.tables_all), ("L0", c.tables_0), ("L1", c.tables_1)):
        at = 0
        for name in GROUPS[group]:
            shape = tables[name].shape
            v = buf[:, at:at + tables[name].size // 128]
            at += tables[name].size // 128
            views[name] = v.rearrange("p (a b) -> p a b", a=shape[1]) if len(shape) == 3 else v
    c.ident, c.ones, c.band = (views[name] for name in GROUPS["all"])
    c.cos_tok, c.sin_tok, c.cos_feat, c.sin_feat, c.rot, c.rot_t, c.headmask, c.ones_n = (
        views[name] for name in GROUPS["L0"])
    c.causal, c.rope_cos_q, c.rope_sin_q, c.rope_cos_k, c.rope_sin_k = (views[name] for name in GROUPS["L1"])


def setup(c):
    nc = c.nc
    c.passed = c.sem("passed", keep=True)
    c.adaln_sems = [c.sem("n_s_" + k, keep=True) for k in ("xs", "tr", "yn", "back", "h", "dve")]
    c.X = c.sb("X", [D, T], keep=True)
    c.H = c.sb("H", [D, T], keep=True)
    c.mods = c.sb("mods", [D, 2, 6, NB], keep=True)
    c.ident_bf = c.sb("ident_bf", [D, D], BF16, keep=True)
    c.band_bf = c.sb("band_bf", [D, 2, 384], BF16, keep=True)
    cT = c.sb("m_cT", [D, 2, NB])
    sT = c.sb("m_sT", [D, 2, NB])
    wm = [c.sb(f"m_w{j}", [D, 6 * D]) for j in range(2)]
    ga = c.sb("m_abs", [D, 2, 2, NB])
    gs = c.sb("m_sign", [D, 2, 2, NB])
    ps = c.ps("m_ps")
    s_x, s_c, s_k = c.sem("m_s_x"), c.sem("m_s_c"), c.sem("m_s_tables")
    s_silu, s_mm, s_ch = c.sem("m_s_silu"), c.sem("m_s_mm"), c.sem("m_s_dve")

    with nc.Block() as block:
        @block.sync
        def _(sp):
            sp.dma_start(cT[:, :, :], c.ins["c_cols"]).then_inc(s_c, 16)
            for j in range(2):
                sp.dma_start(wm[j][:, :], c.ins["w_mod"][j]).then_inc(s_c, 16)
            sp.dma_start(c.X[:, :], c.ins["x"]).then_inc(s_x, 16)
            sp.dma_start(c.tables_all[:, :], c.ins["tables_all_in"]).then_inc(s_k, 16)
            sp.dma_start(c.tables_0, c.ins["tables_0_in"]).then_inc(s_k, 16)
            sp.wait_ge(s_x, 16)
            sp.wait_ge(s_k, 32)

        @block.scalar
        def _(act):
            act.wait_ge(s_c, 48)
            act.activation(sT[:, :, :], cT[:, :, :], ACT.Silu).then_inc(s_silu, 1)

        @block.tensor
        def _(pe):
            pe.wait_ge(s_silu, 1)
            for l in range(2):
                for j in range(6):
                    at = (l * 6 + j) * NB
                    last = pe.matmul(ps[:, at:at + NB], wm[l][:, j * D:(j + 1) * D], sT[:, l, :], start=True, stop=True)
            last.then_inc(s_mm, 1)

        @block.vector
        def _(dve):
            ch = Chain(dve, s_ch)
            dve.wait_ge(s_mm, 1)
            ch.link(dve.tensor_copy(c.mods[:, :, :, :], ps[:, 0:48].rearrange("p (l j b) -> p l j b", l=2, j=6)))
            for j in (1, 4):
                ch.inc(dve.tensor_scalar(c.mods[:, :, j, :], c.mods[:, :, j, :], 1.0, None, ALU.add))
            for n, j in enumerate((2, 5)):
                g = c.mods[:, :, j, :]
                ch.link(dve.scalar_tensor_tensor(out=ga[:, n, :, :], in0=g, scalar=-1.0, in1=g, op0=ALU.mult, op1=ALU.max))
                ch.link(dve.tensor_scalar(ga[:, n, :, :], ga[:, n, :, :], 0.25, None, ALU.max))
                ch.link(dve.tensor_scalar(gs[:, n, :, :], g, 0.0, 2.0, ALU.is_ge, ALU.mult))
                ch.link(dve.tensor_scalar(gs[:, n, :, :], gs[:, n, :, :], -1.0, None, ALU.add))
                ch.inc(dve.tensor_tensor(g, ga[:, n, :, :], gs[:, n, :, :], ALU.mult))
            dve.wait_ge(s_k, 32)
            ch.inc(dve.tensor_copy(c.ident_bf[:, :], c.ident[:, :]))
            ch.link(dve.tensor_copy(c.band_bf[:, :, :], c.band[:, :, :]))


def adaln(c, layer, part):
    nc, n = c.nc, f"n{layer}{part}_"
    UN = 2
    xs = [c.sb(n + f"xs{u}", [D, N]) for u in range(UN)]
    yn = [c.sb(n + f"yn{u}", [128, TILES, D]) for u in range(UN)]
    stats = [c.sb(n + f"stats{u}", [128, TILES, 6]) for u in range(UN)]
    mv = [c.sb(n + f"mv{u}", [128, TILES, 2]) for u in range(UN)]
    rs = [c.sb(n + f"rs{u}", [128, 3, TILES]) for u in range(UN)]
    ps = [c.ps(n + f"ps{u}") for u in range(UN)]
    s_xs, s_tr, s_yn, s_bk, s_h, s_ch = c.adaln_sems
    done = (2 * layer + part) * NB
    with nc.Block() as block:
        @block.scalar
        def _(act):
            for pair in range(NB // UN):
                for u in range(UN):
                    wait(act, s_tr, done + pair * UN)
                    act.activation(xs[u][:, :], c.X[:, ds((pair * UN + u) * N, N)], ACT.Copy).then_inc(s_xs, 1)
                for u in range(UN):
                    b = pair * UN + u
                    act.wait_ge(s_bk, done + b + 1)
                    act.activation(c.H[:, ds(b * N, N)], ps[u][:, :], ACT.Identity,
                                   bias=c.mods[:, layer, 3 * part, ds(b, 1)],
                                   scale=c.mods[:, layer, 3 * part + 1, ds(b, 1)]).then_inc(s_h, 1)

        @block.tensor
        def _(pe):
            for pair in range(NB // UN):
                for u in range(UN):
                    pe.wait_ge(s_xs, done + pair * UN + u + 1)
                    wait(pe, s_h, done + pair * UN)
                    for t in range(TILES):
                        tt = slice(128 * t, 128 * t + 128)
                        last = pe.transpose(ps[u][:, tt], xs[u][:, tt], c.ident[:, :])
                    last.then_inc(s_tr, 1)
                for u in range(UN):
                    pe.wait_ge(s_yn, done + pair * UN + u + 1)
                    for t in range(TILES):
                        last = pe.transpose(ps[u][:, 128 * t:128 * t + 128], yn[u][:, t, :], c.ident[:, :])
                    last.then_inc(s_bk, 1)

        @block.vector
        def _(dve):
            for pair in range(NB // UN):
                ch = Chain(dve, s_ch, 46, done // UN + pair)
                for u in range(UN):
                    dve.wait_ge(s_tr, done + pair * UN + u + 1)
                    norm_tokens(c, dve, ch, yn[u], ps[u][:, :].rearrange("p (t c) -> p t c", t=TILES), stats[u], mv[u],
                                rs[u], 1e-5).then_inc(s_yn, 1)
                ch.end()


def convolutions(c):
    nc = c.nc
    UN, O, K = 2, 4, 5
    cols = c.sb("c_cols_sb", [D, 2 * O * K + O + 3])
    w1, w2 = cols[:, 0:O * K], cols[:, O * K:2 * O * K]
    b1 = cols[:, 2 * O * K:2 * O * K + O]
    b2, gain, shift = (cols[:, 2 * O * K + O + j:2 * O * K + O + j + 1] for j in range(3))
    diag = c.sb("c_diag", [D, O * K, D])
    hp = [c.sb(f"c_hp{u}", [D, N + K - 1]) for u in range(UN)]
    hid = [c.sb(f"c_hid{u}", [D, O, N + K - 1]) for u in range(UN)]
    acc = [c.sb(f"c_acc{u}", [D, N]) for u in range(UN)]
    yn = [c.sb(f"c_yn{u}", [128, TILES, D]) for u in range(UN)]
    stats = [c.sb(f"c_stats{u}", [128, TILES, 6]) for u in range(UN)]
    mv = [c.sb(f"c_mv{u}", [128, TILES, 2]) for u in range(UN)]
    rs = [c.sb(f"c_rs{u}", [128, 3, TILES]) for u in range(UN)]
    psC = [c.ps(f"c_psC{j}") for j in range(4)]
    psN = [c.ps(f"c_psN{u}") for u in range(UN)]
    s = {k: c.sem("c_s_" + k) for k in ("w", "z", "dg", "hp", "c1", "hid", "acc", "tr", "yn", "back", "h")}
    s_ch, s_ch0 = c.sem("c_s_dve"), c.sem("c_s_dve0")
    with nc.Block() as block:
        @block.sync
        def _(sp):
            sp.dma_start(cols[:, :], c.ins["cols_conv"]).then_inc(s["w"], 16)

        @block.gpsimd
        def _(pool):
            for u in range(UN):
                pool.memset(hp[u][:, :], 0.0)
                last = pool.memset(hid[u][:, :, :], 0.0)
            last.then_inc(s["z"], 1)

        @block.scalar
        def _(act):
            act.wait_ge(s["w"], 16)
            act.wait_ge(s["z"], 1)
            for pair in range(NB // UN):
                it = pair * UN
                for u in range(UN):
                    wait(act, s["acc"], it)
                    act.activation(hp[u][:, 2:2 + N], c.H[:, ds((it + u) * N, N)], ACT.Copy).then_inc(s["hp"], 1)
                for u in range(UN):
                    for o in range(O):
                        act.wait_ge(s["c1"], (it + u) * O + o + 1)
                        act.activation(hid[u][:, o, 2:2 + N], psC[o][:, :], ACT.Gelu,
                                       bias=b1[:, o:o + 1]).then_inc(s["hid"], 1)
                for u in range(UN):
                    act.wait_ge(s["back"], it + u + 1)
                    act.activation(c.H[:, ds((it + u) * N, N)], psN[u][:, :], ACT.Identity, bias=shift,
                                   scale=gain).then_inc(s["h"], 1)

        @block.tensor
        def _(pe):
            pe.wait_ge(s["dg"], O * K)
            for pair in range(NB // UN):
                it = pair * UN
                for u in range(UN):
                    pe.wait_ge(s["hp"], it + u + 1)
                    for o in range(O):
                        if u:
                            pe.wait_ge(s["hid"], it * O + o + 1)
                        else:
                            wait(pe, s["hid"], it * O)
                        for k in range(K):
                            last = pe.matmul(psC[o][:, :], diag[:, o * K + k, :], hp[u][:, k:k + N],
                                             start=(k == 0), stop=(k == K - 1))
                        last.then_inc(s["c1"], 1)
                for u in range(UN):
                    pe.wait_ge(s["acc"], it + u + 1)
                    wait(pe, s["h"], it)
                    for t in range(TILES):
                        tt = slice(128 * t, 128 * t + 128)
                        last = pe.transpose(psN[u][:, tt], acc[u][:, tt], c.ident[:, :])
                    last.then_inc(s["tr"], 1)
                for u in range(UN):
                    pe.wait_ge(s["yn"], it + u + 1)
                    for t in range(TILES):
                        last = pe.transpose(psN[u][:, 128 * t:128 * t + 128], yn[u][:, t, :], c.ident[:, :])
                    last.then_inc(s["back"], 1)

        @block.vector
        def _(dve):
            dve.wait_ge(s["w"], 16)
            for j in range(O * K):
                dve.tensor_scalar(diag[:, j, :], c.ident[:, :], w1[:, j:j + 1], None, ALU.mult).then_inc(s["dg"], 1)
            for pair in range(NB // UN):
                it = pair * UN
                ch = Chain(dve, s_ch, 46 + 2 * O * K, pair)
                for u in range(UN):
                    a = acc[u][:, :]
                    for o in range(O):
                        dve.wait_ge(s["hid"], (it + u) * O + o + 1)
                        for k in range(K):
                            x, w = hid[u][:, o, k:k + N], w2[:, o * K + k:o * K + k + 1]
                            if o == 0 and k == 0:
                                wait(dve, s["tr"], it)
                                ch.link(dve.tensor_scalar(a, x, w, b2, ALU.mult, ALU.add))
                            else:
                                ch.link(dve.scalar_tensor_tensor(out=a, in0=x, scalar=w, in1=a, op0=ALU.mult, op1=ALU.add))
                    dve.tensor_tensor(a, a, hp[u][:, 2:2 + N], ALU.add).then_inc(s["acc"], 1)
                for u in range(UN):
                    dve.wait_ge(s["tr"], it + u + 1)
                    norm_tokens(c, dve, ch, yn[u], psN[u][:, :].rearrange("p (t c) -> p t c", t=TILES), stats[u], mv[u],
                                rs[u], 1e-12).then_inc(s["yn"], 1)
                ch.end()


def feed_forward(c):
    nc = c.nc
    UN, C = 2, 4
    w1 = c.sb("f_w1", [D, C * D])
    w2 = c.sb("f_w2", [D, C, D])
    cols = c.sb("f_cols", [D, C + 3])
    hh = [c.sb(f"f_hh{u}", [D, C, N]) for u in range(UN)]
    y = [c.sb(f"f_y{u}", [D, N]) for u in range(UN)]
    yn = [c.sb(f"f_yn{u}", [128, TILES, D]) for u in range(UN)]
    ya = [c.sb(f"f_ya{u}", [D, N]) for u in range(UN)]
    stats = [c.sb(f"f_stats{u}", [128, TILES, 6]) for u in range(UN)]
    mv = [c.sb(f"f_mv{u}", [128, TILES, 2]) for u in range(UN)]
    rs = [c.sb(f"f_rs{u}", [128, 3, TILES]) for u in range(UN)]
    psC = [c.ps(f"f_psC{j}") for j in range(2)]
    psY = [c.ps(f"f_psY{u}") for u in range(UN)]
    s = {k: c.sem("f_s_" + k) for k in ("w", "c1", "hh", "o", "y", "tr", "yn", "back", "ya", "x")}
    s_ch = c.sem("f_s_dve")
    with nc.Block() as block:
        @block.sync
        def _(sp):
            sp.dma_start(w1[:, :], c.ins["w_ff0a"]).then_inc(s["w"], 16)
            sp.dma_start(w2[:, :, :], c.ins["w_ff0b"]).then_inc(s["w"], 16)
            sp.dma_start(cols[:, :], c.ins["cols_ff0"]).then_inc(s["w"], 16)

        @block.tensor
        def _(pe):
            pe.wait_ge(s["w"], 48)
            for pair in range(NB // UN):
                it = pair * UN
                for u in range(UN):
                    for j in range(C):
                        if u == 0 and j < 2:
                            wait(pe, s["hh"], it * C)
                        else:
                            wait(pe, s["hh"], (it + u) * C + j - 1)
                        pe.matmul(psC[j % 2][:, :], w1[:, j * D:(j + 1) * D], c.H[:, ds((it + u) * N, N)], start=True,
                                  stop=True).then_inc(s["c1"], 1)
                for u in range(UN):
                    wait(pe, s["hh"], (it + u + 1) * C)
                    wait(pe, s["ya"], it)
                    for j in range(C):
                        last = pe.matmul(psY[u][:, :], w2[:, j, :], hh[u][:, j, :], start=(j == 0), stop=(j == C - 1))
                    last.then_inc(s["o"], 1)
                for u in range(UN):
                    pe.wait_ge(s["y"], it + u + 1)
                    for t in range(TILES):
                        tt = slice(128 * t, 128 * t + 128)
                        last = pe.transpose(psY[u][:, tt], y[u][:, tt], c.ident[:, :])
                    last.then_inc(s["tr"], 1)
                for u in range(UN):
                    pe.wait_ge(s["yn"], it + u + 1)
                    for t in range(TILES):
                        last = pe.transpose(psY[u][:, 128 * t:128 * t + 128], yn[u][:, t, :], c.ident[:, :])
                    last.then_inc(s["back"], 1)

        @block.scalar
        def _(act):
            act.wait_ge(s["w"], 48)
            for pair in range(NB // UN):
                it = pair * UN
                for u in range(UN):
                    wait(act, s["o"], it)
                    for j in range(C):
                        act.wait_ge(s["c1"], (it + u) * C + j + 1)
                        act.activation(hh[u][:, j, :], psC[j % 2][:, :], ACT.Gelu, bias=cols[:, j:j + 1]).then_inc(s["hh"], 1)
                for u in range(UN):
                    act.wait_ge(s["back"], it + u + 1)
                    wait(act, s["x"], it)
                    act.activation(ya[u][:, :], psY[u][:, :], ACT.Identity, bias=cols[:, C + 2:C + 3],
                                   scale=cols[:, C + 1:C + 2]).then_inc(s["ya"], 1)

        @block.vector
        def _(dve):
            for pair in range(NB // UN):
                it = pair * UN
                ch = Chain(dve, s_ch, 46, pair)
                for u in range(UN):
                    dve.wait_ge(s["o"], it + u + 1)
                    dve.scalar_tensor_tensor(out=y[u][:, :], in0=psY[u][:, :], scalar=cols[:, C:C + 1],
                                             in1=c.H[:, ds((it + u) * N, N)], op0=ALU.add, op1=ALU.add).then_inc(s["y"], 1)
                for u in range(UN):
                    dve.wait_ge(s["tr"], it + u + 1)
                    norm_tokens(c, dve, ch, yn[u], psY[u][:, :].rearrange("p (t c) -> p t c", t=TILES), stats[u], mv[u],
                                rs[u], 1e-12).then_inc(s["yn"], 1)
                for u in range(UN):
                    b = it + u
                    dve.wait_ge(s["ya"], b + 1)
                    dve.scalar_tensor_tensor(out=c.X[:, ds(b * N, N)], in0=ya[u][:, :], scalar=c.mods[:, 0, 2, ds(b, 1)],
                                             in1=c.X[:, ds(b * N, N)], op0=ALU.mult, op1=ALU.add).then_inc(s["x"], 1)
                ch.end()


def linear_attention(c):
    nc = c.nc
    LAYERS, NH, HD = 4, 16, 8
    UN = 2
    hs = [c.sb(f"la_hs{u}", [D, N]) for u in range(UN)]
    qg = [c.sb(f"la_qg{u}", [D, N]) for u in range(UN)]
    qp = [c.sb(f"la_qp{u}", [D, N]) for u in range(UN)]
    qc = [c.sb(f"la_qc{u}", [D, N]) for u in range(UN)]
    qs = [c.sb(f"la_qs{u}", [D, N]) for u in range(UN)]
    kg = [c.sb(f"la_kg{u}", [128, TILES, D]) for u in range(UN)]
    kc = [c.sb(f"la_kc{u}", [128, TILES, D]) for u in range(UN)]
    ks = [c.sb(f"la_ks{u}", [128, TILES, D]) for u in range(UN)]
    vv = [c.sb(f"la_v{u}", [128, TILES, D]) for u in range(UN)]
    a12 = [c.sb(f"la_a12_{u}", [D, 3, D]) for u in range(UN)]
    kvm = [c.sb(f"la_kvm{u}", [D, 2, D]) for u in range(UN)]
    kmm = [c.sb(f"la_kmm{u}", [D, D]) for u in range(UN)]
    z = [c.sb(f"la_z{u}", [128, TILES * NH]) for u in range(UN)]
    y = [c.sb(f"la_y{u}", [128, TILES, D]) for u in range(UN)]
    yn = [c.sb(f"la_yn{u}", [128, TILES, D]) for u in range(UN)]
    stats = [c.sb(f"la_stats{u}", [128, TILES, 6]) for u in range(UN)]
    mv = [c.sb(f"la_mv{u}", [128, TILES, 2]) for u in range(UN)]
    rs = [c.sb(f"la_rs{u}", [128, 3, TILES]) for u in range(UN)]
    wqkv = c.sb("la_wqkv", [D, 3 * D])
    bkv = c.sb("la_bkv", [1, 2 * D])
    lcols = c.sb("la_cols", [D, 3])
    psQ = [c.ps(f"la_psQ{u}") for u in range(UN)]
    psK = [c.ps(f"la_psK{u}", (128, 2, 512)) for u in range(UN)]
    psA = [c.ps(f"la_psA{u}") for u in range(UN)]

    names = ("w", "wfree", "hs", "q", "kv", "qg", "kg", "v", "qc", "kc", "a", "a12", "r", "kvm", "o", "xn", "yn",
             "t", "h", "x", "y")
    s = {k: c.sem("la_s_" + k) for k in names}
    s_chain = c.sem("la_s_dvechain")
    s_act = c.sem("la_s_actchain")

    def layers(eng, body):
        body(0)
        with eng.Fori(1, LAYERS) as layer:
            body(layer)

    with nc.Block() as block:
        @block.sync
        def _(sp):
            def body(layer):
                wait(sp, s["wfree"], layer * NB)
                sp.dma_start(wqkv[:, :], c.ins["w_qkv0"][layer]).then_inc(s["w"], 16)
                sp.dma_start(bkv[:, :], c.ins["b_kv0"][ds(layer, 1), :]).then_inc(s["w"], 16)
                sp.dma_start(lcols[:, :], c.ins["cols_la"][layer]).then_inc(s["w"], 16)
            layers(sp, body)

        @block.tensor
        def _(pe):
            def body(layer):
                for pair in range(NB // UN):
                    it = (layer * (NB // UN) + pair) * UN
                    pe.wait_ge(s["w"], (layer + 1) * 48)
                    for u in range(UN):
                        pe.wait_ge(s["hs"], it + u + 1)
                        wait(pe, s["y"], it)
                        pe.matmul(psQ[u][:, :], wqkv[:, 0:D], hs[u][:, :], start=True, stop=True).then_inc(s["q"], 1)
                        for t in range(TILES):
                            o = psK[u][:, t // 2, (t % 2) * 256:(t % 2 + 1) * 256]
                            pe.matmul(o, hs[u][:, t * 128:(t + 1) * 128], wqkv[:, D:3 * D], start=True, stop=False)
                            last = pe.matmul(o, c.ones[0:1, :], bkv[:, :], start=False, stop=True)
                        last.then_inc(s["kv"], 1)
                    for u in range(UN):
                        pe.wait_ge(s["kc"], it + u + 1)
                        pe.wait_ge(s["v"], it + u + 1)
                        wait(pe, s["h"], it)
                        for j, kk in enumerate((kc, ks)):
                            for t in range(TILES):
                                pe.matmul(psA[u][:, j * D:(j + 1) * D], kk[u][:, t, :], vv[u][:, t, :],
                                          start=(t == 0), stop=(t == TILES - 1))
                        for t in range(TILES):
                            last = pe.matmul(psA[u][:, 2 * D:3 * D], kg[u][:, t, :], c.ones_n[:, :],
                                             start=(t == 0), stop=(t == TILES - 1))
                        last.then_inc(s["a"], 1)
                        for t in range(TILES):
                            last = pe.transpose(psK[u][:, 0, t * 128:(t + 1) * 128], hs[u][:, t * 128:(t + 1) * 128],
                                                c.ident[:, :])
                        last.then_inc(s["x"], 1)
                    for u in range(UN):
                        pe.wait_ge(s["a12"], it + u + 1)
                        pe.matmul(psA[u][:, 0:D], c.ident[:, :], a12[u][:, 0, :], start=True, stop=False)
                        pe.matmul(psA[u][:, 0:D], c.rot_t[:, :], a12[u][:, 1, :], start=False, stop=True)
                        pe.matmul(psA[u][:, D:2 * D], c.rot[:, :], a12[u][:, 0, :], start=True, stop=False)
                        pe.matmul(psA[u][:, D:2 * D], c.ident[:, :], a12[u][:, 1, :], start=False,
                                  stop=True).then_inc(s["r"], 1)
                    for u in range(UN):
                        pe.wait_ge(s["qc"], it + u + 1)
                        pe.wait_ge(s["kvm"], it + u + 1)
                        for t in range(TILES):
                            tt = slice(t * 128, (t + 1) * 128)
                            pe.matmul(psQ[u][:, tt], qc[u][:, tt], kvm[u][:, 0, :], start=True, stop=False)
                            pe.matmul(psQ[u][:, tt], qs[u][:, tt], kvm[u][:, 1, :], start=False, stop=True)
                            last = pe.matmul(psK[u][:, 1, tt], qp[u][:, tt], kmm[u][:, :], start=True, stop=True)
                        last.then_inc(s["o"], 1)
                    for u in range(UN):
                        pe.wait_ge(s["yn"], it + u + 1)
                        for t in range(TILES):
                            last = pe.transpose(psA[u][:, t * 128:(t + 1) * 128], yn[u][:, t, :], c.ident[:, :])
                        last.then_inc(s["t"], 1)
            layers(pe, body)

        @block.scalar
        def _(act):
            def body(layer):
                act.wait_ge(s["w"], (layer + 1) * 48)
                for pair in range(NB // UN):
                    it = (layer * (NB // UN) + pair) * UN
                    for u in range(UN):
                        wait(act, s["x"], it)
                        c.wait_apart(act, s["h"], layer * NB)
                        act.activation(hs[u][:, :], c.H[:, ds((pair * UN + u) * N, N)], ACT.Copy).then_inc(s["hs"], 1)
                    for u in range(UN):
                        act.wait_ge(s["q"], it + u + 1)
                        wait(act, s["o"], it)
                        act.activation(qg[u][:, :], psQ[u][:, :], ACT.Gelu, bias=lcols[:, 0:1]).then_inc(s["qg"], 1)
                        act.wait_ge(s["kv"], it + u + 1)
                        for j in range(2):
                            pk = psK[u][:, j, :].rearrange("p (t k c) -> p t k c", t=2, k=2)
                            act.activation(kg[u][:, 2 * j:2 * j + 2, :], pk[:, :, 0, :], ACT.Gelu).then_inc(s["kg"], 1)
                        for j in range(2):
                            pk = psK[u][:, j, :].rearrange("p (t k c) -> p t k c", t=2, k=2)
                            last = act.activation(vv[u][:, 2 * j:2 * j + 2, :], pk[:, :, 1, :], ACT.Copy)
                            if j == 0:
                                last.then_inc(s_act, 1)
                        last.then_inc(s["v"], 1)
                    for u in range(UN):
                        act.wait_ge(s["a"], it + u + 1)
                        act.activation(a12[u][:, :, :], psA[u][:, 0:3 * D].rearrange("p (j c) -> p j c", j=3),
                                       ACT.Copy).then_inc(s["a12"], 1)
                    for u in range(UN):
                        c.wait_apart(act, s["t"], it + u + 1)
                        act.activation(c.H[:, ds((pair * UN + u) * N, N)], psA[u][:, :], ACT.Identity,
                                       bias=lcols[:, 2:3], scale=lcols[:, 1:2]).then_inc(s["h"], 1)
                act.wait_ge(s["h"], (layer + 1) * NB)
                act.sem_inc(s["wfree"], NB)
            layers(act, body)

        @block.vector
        def _(dve):
            CHAIN = 60
            def body(layer):
                for pair in range(NB // UN):
                    step = layer * (NB // UN) + pair
                    it = step * UN
                    ch = Chain(dve, s_chain, CHAIN, step)
                    for u in range(UN):
                        kk = kg[u][:, :, :]
                        dve.wait_ge(s["kg"], (it + u + 1) * 2)
                        wait(dve, s["a"], it)
                        ch.inc(dve.scalar_tensor_tensor(out=kc[u][:, :, :], in0=kk, scalar=0.21, in1=c.cos_tok[:, :, :],
                                                        op0=ALU.add, op1=ALU.mult))
                        dve.scalar_tensor_tensor(out=ks[u][:, :, :], in0=kk, scalar=0.21, in1=c.sin_tok[:, :, :],
                                                 op0=ALU.add, op1=ALU.mult).then_inc(s["kc"], 1)
                    for u in range(UN):
                        dve.wait_ge(s["qg"], it + u + 1)
                        wait(dve, s["o"], it)
                        ch.inc(dve.tensor_scalar(qp[u][:, :], qg[u][:, :], 0.21, None, ALU.add))
                        ch.inc(dve.scalar_tensor_tensor(out=qc[u][:, :], in0=qg[u][:, :], scalar=0.21, in1=c.cos_feat[:, :],
                                                        op0=ALU.add, op1=ALU.mult))
                        dve.scalar_tensor_tensor(out=qs[u][:, :], in0=qg[u][:, :], scalar=0.21, in1=c.sin_feat[:, :],
                                                 op0=ALU.add, op1=ALU.mult).then_inc(s["qc"], 1)
                    for u in range(UN):
                        dve.wait_ge(s["a12"], it + u + 1)
                        ch.inc(dve.scalar_tensor_tensor(out=kmm[u][:, :], in0=a12[u][:, 2, :], scalar=0.21,
                                                        in1=c.headmask[:, 0, :], op0=ALU.add, op1=ALU.mult))
                        dve.wait_ge(s["r"], it + u + 1)
                        dve.scalar_tensor_tensor(out=kvm[u][:, :, :], in0=psA[u][:, 0:2 * D].rearrange(
                            "p (j c) -> p j c", j=2), scalar=1.0 / N, in1=c.headmask[:, :, :],
                            op0=ALU.mult, op1=ALU.mult).then_inc(s["kvm"], 1)
                    for u in range(UN):
                        dve.wait_ge(s["o"], it + u + 1)
                        den = psK[u][:, 1, :].rearrange("p (h e) -> p h e", e=HD)[:, :, 0]
                        ch.link(dve.tensor_scalar(z[u][:, :], den, 1e-6, None, ALU.add))
                        ch.link(dve.reciprocal(z[u][:, :], z[u][:, :]))
                        o3 = psQ[u][:, :].rearrange("p (h e) -> p h e", e=HD)
                        y3 = y[u][:, :, :].rearrange("p t (h e) -> p (t h) e", e=HD)
                        ch.link(dve.tensor_tensor(y3, o3, z[u][:, :].unsqueeze(2).to_broadcast([128, TILES * NH, HD]),
                                                  ALU.mult))
                        dve.wait_ge(s["x"], it + u + 1)
                        dve.tensor_tensor(y[u][:, :, :], y[u][:, :, :],
                                          psK[u][:, 0, :].rearrange("p (t c) -> p t c", t=TILES),
                                          ALU.add).then_inc(s["y"], 1)
                        dve.wait_ge(s["y"], it + u + 1)
                        norm_tokens(c, dve, ch, yn[u], y[u], stats[u], mv[u], rs[u], 1e-12).then_inc(s["yn"], 1)
                    ch.end()
            layers(dve, body)


def experts(c):
    nc = c.nc
    E, TOPK, C, NT = 16, 4, 4, T // 128
    w1 = [c.sb(f"e_w1_{u}", [D, C * D]) for u in range(2)]
    w2 = [c.sb(f"e_w2_{u}", [D, C, D]) for u in range(2)]
    b1 = [c.sb(f"e_b1_{u}", [D, C]) for u in range(2)]
    b2 = c.sb("e_b2", [E, D])
    keys = c.sb("e_keys", [D, 2, E])
    rbias = c.sb("e_rb", [1, E])
    kr = c.sb("e_kr", [D, E])
    ksq = c.sb("e_ksq", [D, E])
    crow = c.sb("e_crow", [128, E])
    nones = c.sb("e_nones", [D, D])
    hst = [c.sb(f"e_hst{u}", [D, N]) for u in range(2)]
    hsq = [c.sb(f"e_hsq{u}", [D, N]) for u in range(2)]
    lg = c.sb("e_lg", [128, NT, E])
    m8 = c.sb("e_m8", [128, NT, 8])
    gt = c.sb("e_gt", [128, NT, E])
    eq = c.sb("e_eq", [128, NT, E])
    run = c.sb("e_run", [128, NT, E])
    zero = c.sb("e_zero", [128, E])
    left = c.sb("e_left", [128, NT])
    gate = c.sb("e_gate", [128, NT, E])
    gT = c.sb("e_gT", [E, 4, 128])
    acc = c.sb("e_acc", [128, NT, D])
    hh = [c.sb(f"e_hh{j}", [D, C, N]) for j in range(2)]
    psH = [c.ps(f"e_psH{j}") for j in range(4)]
    psY = [c.ps(f"e_psY{j}") for j in range(2)]
    psR = [c.ps(f"e_psR{j}") for j in range(2)]
    s = {k: c.sem("e_s_" + k) for k in ("w", "we0", "we1", "k", "crow", "hst", "hsq", "l", "lg", "gate", "gt", "gTe", "b2", "acc0",
                                        "h", "hh", "y", "acc", "tr", "x", "ksq", "tab")}
    s_ch, s_act = c.sem("e_s_dve"), c.sem("e_s_act")
    with nc.Block() as block:
        @block.sync
        def _(sp):
            sp.dma_start(keys[:, :, :], c.ins["keys_rw"]).then_inc(s["w"], 16)
            sp.dma_start(rbias[:, :], c.ins["rb"]).then_inc(s["w"], 16)
            sp.dma_start(b2[:, :], c.ins["b2_moe"]).then_inc(s["w"], 16)
            sp.dma_start(c.tables_1, c.ins["tables_1_in"]).then_inc(s["tab"], 16)

            def load_pair(ep):
                for u in range(2):
                    e = ep * 2 + u
                    wait(sp, s["y"], (ep * 2 + u - 1) * NB)
                    sp.dma_start(w1[u][:, :], c.ins["w1_moe"][e]).then_inc(s[f"we{u}"], 16)
                    sp.dma_start(w2[u][:, :, :], c.ins["w2_moe"][e]).then_inc(s[f"we{u}"], 16)
                    sp.dma_start(b1[u][:, :], c.ins["b1_moe"][e]).then_inc(s[f"we{u}"], 16)
            load_pair(0)
            with sp.Fori(1, E // 2) as ep:
                load_pair(ep)
            sp.wait_ge(s["tab"], 16)

        @block.tensor
        def _(pe):
            pe.wait_ge(s["k"], 1)
            pe.matmul(psR[0][:, 0:E], nones[:, :], ksq[:, :], start=True, stop=False)
            pe.matmul(psR[0][:, 0:E], c.ones[0:1, :], rbias[:, :], start=False, stop=True).then_inc(s["crow"], 1)
            for b in range(NB):
                u = b % 2
                pe.wait_ge(s["hsq"], b + 1)
                wait(pe, s["lg"], b - 1)
                if b == 0:
                    pe.wait_ge(s["ksq"], 1)
                for t in range(TILES):
                    tt = slice(128 * t, 128 * t + 128)
                    o = psR[u][:, E * t:E * t + E]
                    pe.matmul(o, hst[u][:, tt], kr[:, :], start=True, stop=False)
                    last = pe.matmul(o, hsq[u][:, tt], nones[:, 0:E], start=False, stop=True)
                last.then_inc(s["l"], 1)
            pe.wait_ge(s["gate"], 1)
            for b in range(NB):
                wait(pe, s["gTe"], b)
                wait(pe, s["acc0"], b - 1)
                for t in range(TILES):
                    last = pe.transpose(psR[0][0:E, 128 * t:128 * t + 128], gate[:, b * TILES + t, :], c.ident[:, :])
                last.then_inc(s["gt"], 1)
                pe.wait_ge(s["gTe"], b + 1)
                wait(pe, s["acc0"], b)
                for t in range(TILES):
                    last = pe.matmul(psR[1][:, 128 * t:128 * t + 128], gT[:, t, :], b2[:, :], start=True, stop=True)
                last.then_inc(s["b2"], 1)
            def hidden(ep, u, b, n):
                if b == 0:
                    wait(pe, s[f"we{u}"], (ep + 1) * 48)
                for j in range(C):
                    wait(pe, s["hh"], n * C + j - 3)
                    pe.matmul(psH[j][:, :], w1[u][:, j * D:(j + 1) * D], c.H[:, b * N:(b + 1) * N], start=True,
                              stop=True).then_inc(s["h"], 1)

            def outputs(u, b, n):
                wait(pe, s["hh"], n * C + C)
                wait(pe, s["acc"], n - 1)
                for t in range(TILES):
                    for j in range(C):
                        last = pe.matmul(psY[b % 2][:, 128 * t:128 * t + 128], hh[b % 2][:, j, 128 * t:128 * t + 128],
                                         w2[u][:, j, :], start=(j == 0), stop=(j == C - 1))
                last.then_inc(s["y"], 1)

            def expert_pair(ep):
                for u in range(2):
                    for b in range(NB):
                        n = (ep * 2 + u) * NB + b
                        hidden(ep, u, b, n)
                        if not (isinstance(n, int) and n == 0):
                            outputs((n2 := (u * NB + b - 1) % 8) // NB, (b - 1) % NB, n - 1)
            expert_pair(0)
            with pe.Fori(1, E // 2) as ep:
                expert_pair(ep)
            outputs(1, NB - 1, E * NB - 1)
            for b in range(NB):
                wait(pe, s["acc"], E * NB)
                wait(pe, s["x"], b - 1)
                for t in range(TILES):
                    last = pe.transpose(psR[b % 2][:, 128 * t:128 * t + 128], acc[:, b * TILES + t, :], c.ident[:, :])
                last.then_inc(s["tr"], 1)

        @block.scalar
        def _(act):
            for b in range(NB):
                wait(act, s["l"], b - 1)
                act.activation(hst[b % 2][:, :], c.H[:, b * N:(b + 1) * N], ACT.Copy).then_inc(s["hst"], 1)
                act.activation(hsq[b % 2][:, :], c.H[:, b * N:(b + 1) * N], ACT.Square).then_inc(s["hsq"], 1)
            act.wait_ge(s["lg"], NB + 1)
            act.activation(gate[:, :, :], lg[:, :, :], ACT.Exp).then_inc(s_act, 1)
            for b in range(NB):
                act.wait_ge(s["gt"], b + 1)
                wait(act, s["b2"], b)
                act.activation(gT[:, :, :], psR[0][0:E, :].rearrange("e (t p) -> e t p", t=TILES),
                               ACT.Copy).then_inc(s["gTe"], 1)

            def expert_pair(ep):
                for u in range(2):
                    for b in range(NB):
                        n = (ep * 2 + u) * NB + b
                        wait(act, s["y"], n - 1)
                        for j in range(C):
                            act.wait_ge(s["h"], n * C + j + 1)
                            act.activation(hh[b % 2][:, j, :], psH[j][:, :], ACT.Gelu, bias=b1[u][:, j:j + 1]).then_inc(s["hh"], 1)
            expert_pair(0)
            with act.Fori(1, E // 2) as ep:
                expert_pair(ep)

        @block.vector
        def _(dve):
            ch = Chain(dve, s_ch)
            dve.wait_ge(s["w"], 48)
            ch.inc(dve.memset(nones[:, :], -1.0))
            ch.inc(dve.memset(zero[:, :], 0.0))
            ch.inc(dve.scalar_tensor_tensor(out=kr[:, :], in0=keys[:, 0, :], scalar=2.0, in1=keys[:, 1, :], op0=ALU.mult,
                                            op1=ALU.add))
            dve.tensor_tensor(ksq[:, :], keys[:, 0, :], keys[:, 0, :], ALU.mult).then_inc(s["k"], 1)
            dve.wait_ge(s["crow"], 1)
            dve.tensor_copy(crow[:, :], psR[0][:, 0:E]).then_inc(s["ksq"], 1)
            dve.wait_ge(s["ksq"], 1)
            for b in range(NB):
                dve.wait_ge(s["l"], b + 1)
                dve.tensor_tensor(lg[:, b * TILES:(b + 1) * TILES, :],
                                  psR[b % 2][:, 0:TILES * E].rearrange("p (t e) -> p t e", e=E),
                                  crow[:, :].unsqueeze(1).to_broadcast([128, TILES, E]), ALU.add).then_inc(s["lg"], 1)
            wait(dve, s["lg"], NB)
            for t in range(NT):
                m = ch.inc(dve.max(m8[:, t, :], lg[:, t, :]))
            ch.wait(m)
            kth = m8[:, :, TOPK - 1].unsqueeze(2).to_broadcast([128, NT, E])
            ch.inc(dve.tensor_tensor(gt[:, :, :], lg[:, :, :], kth, ALU.is_gt))
            ch.link(dve.tensor_tensor(eq[:, :, :], lg[:, :, :], kth, ALU.is_equal))
            ch.link(dve.tensor_reduce(left[:, :], gt[:, :, :], AX_X, ALU.add))
            ch.link(dve.tensor_scalar(left[:, :], left[:, :], -1.0, float(TOPK), ALU.mult, ALU.add))
            for t in range(NT):
                m = ch.inc(dve.tensor_tensor_scan(run[:, t, :], eq[:, t, :], zero[:, :], 0.0, ALU.add, ALU.add))
            ch.wait(m)
            ch.link(dve.tensor_tensor(run[:, :, :], run[:, :, :], left[:, :].unsqueeze(2).to_broadcast([128, NT, E]),
                                      ALU.is_le))
            ch.link(dve.tensor_tensor(run[:, :, :], run[:, :, :], eq[:, :, :], ALU.mult))
            ch.link(dve.tensor_tensor(gt[:, :, :], gt[:, :, :], run[:, :, :], ALU.add))
            dve.tensor_tensor(lg[:, :, :], lg[:, :, :], m8[:, :, 0].unsqueeze(2).to_broadcast([128, NT, E]),
                              ALU.subtract).then_inc(s["lg"], 1)
            dve.wait_ge(s_act, 1)
            ch.link(dve.tensor_tensor(gate[:, :, :], gate[:, :, :], gt[:, :, :], ALU.mult))
            ch.link(dve.tensor_reduce(left[:, :], gate[:, :, :], AX_X, ALU.add))
            ch.link(dve.reciprocal(left[:, :], left[:, :]))
            dve.tensor_tensor(gate[:, :, :], gate[:, :, :], left[:, :].unsqueeze(2).to_broadcast([128, NT, E]),
                              ALU.mult).then_inc(s["gate"], 1)
            for b in range(NB):
                dve.wait_ge(s["b2"], b + 1)
                dve.tensor_copy(acc[:, b * TILES:(b + 1) * TILES, :],
                                psR[1][:, :].rearrange("p (t c) -> p t c", t=TILES)).then_inc(s["acc0"], 1)
            wait(dve, s["acc0"], NB)
            dve.wait_ge(s["gate"], 1)

            def expert_pair(ep):
                for u in range(2):
                    for b in range(NB):
                        e = ep * 2 + u
                        n = e * NB + b
                        dve.wait_ge(s["y"], n + 1)
                        wait(dve, s["acc"], n - 3)
                        for t in range(TILES):
                            a = acc[:, b * TILES + t, :]
                            last = dve.scalar_tensor_tensor(out=a, in0=psY[b % 2][:, 128 * t:128 * t + 128],
                                                            scalar=gate[:, b * TILES + t, ds(e, 1)], in1=a,
                                                            op0=ALU.mult, op1=ALU.add)
                        last.then_inc(s["acc"], 1)
            expert_pair(0)
            with dve.Fori(1, E // 2) as ep:
                expert_pair(ep)
            for b in range(NB):
                dve.wait_ge(s["tr"], b + 1)
                dve.scalar_tensor_tensor(out=c.X[:, b * N:(b + 1) * N], in0=psR[b % 2][:, :],
                                         scalar=c.mods[:, 0, 5, b:b + 1], in1=c.X[:, b * N:(b + 1) * N],
                                         op0=ALU.mult, op1=ALU.add).then_inc(s["x"], 1)


def causal_attention(c):
    nc = c.nc
    DQ, UN = 32, 2
    LOWEST = float(np.finfo(np.float32).min)
    wqk = c.sb("a_wqk", [D, 2, DQ])
    wvd = c.sb("a_wvd", [DQ, D])
    wvu = c.sb("a_wvu", [DQ, D])
    wv = c.sb("a_wv", [D, D])
    hst = [c.sb(f"a_hst{u}", [D, N]) for u in range(UN)]
    qk = [c.sb(f"a_qk{u}", [DQ, 2, N]) for u in range(UN)]
    v = [c.sb(f"a_v{u}", [128, TILES, D]) for u in range(UN)]
    sc = [c.sb(f"a_sc{u}", [128, N]) for u in range(UN)]
    zz = [c.sb(f"a_zz{u}", [128, N]) for u in range(UN)]
    pr = [c.sb(f"a_pr{u}", [128, N]) for u in range(UN)]
    pT = [c.sb(f"a_pT{u}", [128, TILES, 128]) for u in range(UN)]
    mx = [c.sb(f"a_mx{u}", [128, 1]) for u in range(UN)]
    sm = [c.sb(f"a_sm{u}", [128, 1]) for u in range(UN)]
    psA = [c.ps(f"a_psA{u}") for u in range(UN)]
    psS = [c.ps(f"a_psS{u}") for u in range(UN)]
    psT = [c.ps(f"a_psT{u}") for u in range(UN)]
    psO = [c.ps(f"a_psO{u}") for u in range(UN)]
    s = {k: c.sem("a_s_" + k) for k in ("w", "wv", "wve", "h", "qk", "qke", "v", "ve", "sc", "z", "mx", "e", "pr", "t", "te",
                                        "o", "x")}
    s_ch = c.sem("a_s_dve")
    with nc.Block() as block:
        @block.sync
        def _(sp):
            sp.dma_start(wqk[:, :, :], c.ins["w_qk1"]).then_inc(s["w"], 16)
            sp.dma_start(wvd[:, :], c.ins["w_vdT"]).then_inc(s["w"], 16)
            sp.dma_start(wvu[:, :], c.ins["w_vu"]).then_inc(s["w"], 16)

        @block.tensor
        def _(pe):
            pe.wait_ge(s["w"], 48)
            pe.matmul(psA[0][:, 0:D], wvd[:, :], wvu[:, :], start=True, stop=True).then_inc(s["wv"], 1)
            pe.wait_ge(s["wve"], 1)
            for pair in range(NB // UN):
                it = pair * UN
                for j in range(2):
                    for u in range(UN):
                        pe.wait_ge(s["h"], it + u + 1)
                        if j == 0:
                            wait(pe, s["ve"], it)
                        else:
                            wait(pe, s["qke"], 2 * (it + u) + 1 - u)
                            pe.wait_ge(s["qke"], 2 * it + 1 + u)
                        pe.matmul(psA[u][0:DQ, :], wqk[:, j, :], hst[u][:, :], start=True, stop=True).then_inc(s["qk"], 1)
                for u in range(UN):
                    pe.wait_ge(s["qke"], 2 * it + 3 + u)
                    for t in range(TILES):
                        last = pe.matmul(psA[u][:, 128 * t:128 * t + 128], hst[u][:, 128 * t:128 * t + 128], wv[:, :],
                                         start=True, stop=True)
                    last.then_inc(s["v"], 1)
                def attend(t, u):
                    if t == 0:
                        wait(pe, s["x"], it)
                        pe.wait_ge(s["ve"], it + u + 1)
                    pe.wait_ge(s["pr"], it * TILES + UN * t + u + 1)
                    wait(pe, s["te"], it * TILES + UN * t)
                    for k in range(TILES):
                        kk = slice(128 * k, 128 * k + 128)
                        last = pe.transpose(psT[u][:, kk], pr[u][:, kk], c.ident[:, :])
                    last.then_inc(s["t"], 1)
                    pe.wait_ge(s["te"], it * TILES + UN * t + u + 1)
                    for k in range(TILES):
                        last = pe.matmul(psO[u][:, 128 * t:128 * t + 128], v[u][:, k, :], pT[u][:, k, :],
                                         start=(k == 0), stop=(k == TILES - 1))
                    last.then_inc(s["o"], 1)
                for t in range(TILES + 1):
                    for u in range(UN):
                        if t < TILES:
                            wait(pe, s["z"], it * TILES + UN * t)
                            pe.matmul(psS[u][:, :], qk[u][:, 0, 128 * t:128 * t + 128], qk[u][:, 1, :], start=True,
                                      stop=True).then_inc(s["sc"], 1)
                    if t:
                        for u in range(UN):
                            attend(t - 1, u)

        @block.scalar
        def _(act):
            act.wait_ge(s["wv"], 1)
            act.activation(wv[:, :], psA[0][:, 0:D], ACT.Copy).then_inc(s["wve"], 1)
            for pair in range(NB // UN):
                it = pair * UN
                for u in range(UN):
                    wait(act, s["v"], it)
                    act.activation(hst[u][:, :], c.H[:, ds((it + u) * N, N)], ACT.Copy).then_inc(s["h"], 1)
                for j in range(2):
                    for u in range(UN):
                        act.wait_ge(s["qk"], 2 * it + 2 * j + u + 1)
                        wait(act, s["sc"], it * TILES)
                        act.activation(qk[u][:, j, :], psA[u][0:DQ, :], ACT.Copy).then_inc(s["qke"], 1)
                for u in range(UN):
                    act.wait_ge(s["v"], it + u + 1)
                    wait(act, s["o"], it * TILES)
                    act.activation(v[u][:, :, :], psA[u][:, :].rearrange("p (t c) -> p t c", t=TILES),
                                   ACT.Copy).then_inc(s["ve"], 1)
                def evac(t, u):
                    n = it * TILES + UN * t
                    act.wait_ge(s["t"], n + u + 1)
                    wait(act, s["o"], n)
                    act.activation(pT[u][:, :, :], psT[u][:, :].rearrange("p (t c) -> p t c", t=TILES),
                                   ACT.Copy).then_inc(s["te"], 1)
                for t in range(TILES + 1):
                    for u in range(UN):
                        if t:
                            evac(t - 1, u)
                        if t < TILES:
                            n = it * TILES + UN * t
                            act.wait_ge(s["mx"], n + u + 1)
                            wait(act, s["pr"], n)
                            act.activation(pr[u][:, :], sc[u][:, :], ACT.Exp, bias=mx[u][:, :],
                                           accum_out=sm[u][:, :]).then_inc(s["e"], 1)

        @block.vector
        def _(dve):
            for pair in range(NB // UN):
                it = pair * UN
                ch = Chain(dve, s_ch, 32, pair)
                for t in range(TILES):
                    n = it * TILES + UN * t
                    for u in range(UN):
                        dve.wait_ge(s["sc"], n + u + 1)
                        wait(dve, s["e"], n)
                        dve.scalar_tensor_tensor(out=sc[u][:, :], in0=psS[u][:, :], scalar=DQ ** -0.5,
                                                 in1=c.causal[:, t, :], op0=ALU.mult, op1=ALU.mult).then_inc(s["z"], 1)
                        dve.wait_ge(s["z"], n + u + 1)
                        ch.link(dve.tensor_scalar(zz[u][:, :], sc[u][:, :], 0.0, LOWEST, ALU.is_equal, ALU.mult))
                        ch.link(dve.tensor_tensor(sc[u][:, :], sc[u][:, :], zz[u][:, :], ALU.add))
                        ch.link(dve.tensor_reduce(mx[u][:, :], sc[u][:, :], AX_X, ALU.max))
                        dve.tensor_scalar(mx[u][:, :], mx[u][:, :], -1.0, None, ALU.mult).then_inc(s["mx"], 1)
                    for u in range(UN):
                        dve.wait_ge(s["e"], n + u + 1)
                        wait(dve, s["t"], n)
                        ch.link(dve.reciprocal(sm[u][:, :], sm[u][:, :]))
                        dve.tensor_scalar(pr[u][:, :], pr[u][:, :], sm[u][:, :], None, ALU.mult).then_inc(s["pr"], 1)
                for u in range(UN):
                    b = it + u
                    dve.wait_ge(s["o"], it * TILES + UN * (TILES - 1) + u + 1)
                    dve.scalar_tensor_tensor(out=c.X[:, ds(b * N, N)], in0=psO[u][:, :], scalar=c.mods[:, 1, 2, ds(b, 1)],
                                             in1=c.X[:, ds(b * N, N)], op0=ALU.mult, op1=ALU.add).then_inc(s["x"], 1)
                ch.end()


def finish(c, out):
    s_y, s_o = c.sem("o_s_y"), c.sem("o_s_out")
    with c.nc.Block() as block:
        @block.vector
        def _(dve):
            for b in range(NB):
                bb = slice(b * N, (b + 1) * N)
                dve.scalar_tensor_tensor(out=c.X[:, bb], in0=c.H[:, bb], scalar=c.mods[:, 1, 5, b:b + 1], in1=c.X[:, bb],
                                         op0=ALU.mult, op1=ALU.add).then_inc(s_y, 1)

        @block.sync
        def _(sp):
            for b in range(NB):
                sp.wait_ge(s_y, b + 1)
                sp.dma_start(out[:, b * N:(b + 1) * N], c.X[:, b * N:(b + 1) * N]).then_inc(s_o, 16)
            wait(sp, s_o, 16 * NB)


def windowed_layers(c):
    nc = c.nc
    DEPTH, HEADS, DH, WIN = 6, 16, 64, 32
    PAIRS, BLK = HEADS // 2, 64
    KEYS = WIN + BLK
    NBLK = N // BLK
    FF = 341
    CH = [(0, 128), (128, 128), (256, FF - 256)]
    ROUNDS = DEPTH * NB
    QKV = 3 * HEADS * DH
    UP, UT, UA = 24, 16, 2 * NBLK

    w_qkv = c.sb("w_qkv", [D, 2, QKV])
    w_o = c.sb("w_o", [D, PAIRS, D])
    w_1 = c.sb("w_1", [D, 2 * FF])
    w_2 = c.sb("w_2", [D, 3, D])
    cols = c.sb("w_cols", [D, 9])
    xs = c.sb("w_xs", [D, N])
    raw = [c.sb(f"w_raw{j}", [128, 4, 512]) for j in range(2)]
    sq = c.sb("w_sq", [128, 4, 512])
    qr = c.sb("w_qr", [128, 4, 512])
    t2 = c.sb("w_t2", [128, 512])
    nrm = [c.sb(f"w_nrm{j}", [128, 4, 32]) for j in range(2)]
    qb = [c.sb(f"w_qb{j}", [128, PAIRS, 2, 2, BLK]) for j in range(2)]
    kT = c.sb("w_kT", [128, PAIRS, WIN + N])
    v = [c.tables_1[:, 1024 * t:1024 * (t + 1)] for t in range(3)] + [c.sb("w_v3", [128, HEADS * DH])]
    v_even = c.sb("w_v_even", [KEYS, HEADS * DH])
    pb = [c.sb(f"w_pb{j}", [128, PAIRS, KEYS + WIN * j]) for j in range(2)]
    mx = c.sb("w_mx", [128, PAIRS])
    sm = [c.sb(f"w_sm{j}", [128, PAIRS]) for j in range(2)]
    pT = c.sb("w_pT", [128, PAIRS, 128])
    oT = c.sb("w_oT", [128, PAIRS, N])
    xsf = c.sb("w_xsf", [D, N])
    yn = c.sb("w_yn", [128, TILES, D])
    xn = c.sb("w_xn", [D, N])
    gg = yn[:, :, :].rearrange("p t c -> p (t c)")
    hh = c.sb("w_hh", [D, 3, N])
    stats = c.sb("w_stats", [128, TILES, 6])
    mv = c.sb("w_mv", [128, TILES, 2])
    rs = c.sb("w_rs", [128, 3, TILES])
    tabs = c.sb("w_tabs", [128, DEPTH, 4, TILES, DH])
    scl = sq[:, 0:3, :].rearrange("p a b -> p (a b)").rearrange("p (l k d) -> p l k d", l=DEPTH, k=4)

    psP = [c.ps(f"w_psP{j}") for j in range(2)]
    psT = c.ps("w_psT")
    psA = c.ps("w_psA")
    psS = [c.ps(f"w_psS{j}") for j in range(2)]
    psO = c.ps("w_psO")
    psF = c.ps("w_psF")

    names = ("wa", "wf", "tab", "z", "xs", "p", "pe", "sr", "rn", "t1", "qr", "t", "te", "s", "x1", "e", "r", "pn", "pt",
             "pte", "ve", "av", "ot", "f", "xf", "xsf", "yn", "xn", "gg", "hh", "out", "scl")
    s = {k: c.sem("w_s_" + k) for k in names}
    s_norm, s_x, s_f, s_pool = c.sem("w_s_norm"), c.sem("w_s_x"), c.sem("w_s_f_dve"), c.sem("w_s_pool")

    def proj_use(kind, t, j):
        return 6 * t + (j if kind == "P" else 4 + j)

    def slot(n):
        pt, dp = (n // 2 + 2) % TILES, (n // 2 + 2) // TILES
        tt, dt = (n // 2 + 1) % TILES, (n // 2 + 1) // TILES
        a, da = (n - 1) % NBLK, (n - 1) // NBLK
        if n % 2 == 0:
            pa, pb_, pc = (("P", pt, j, dp) for j in range(3))
        else:
            pa, pb_, pc = ("P", pt, 3, dp), ("V", pt, 0, dp), ("V", pt, 1, dp)
        T0, T1 = (("T", tt, 2 * (n % 2) + j, dt) for j in range(2))
        stage = [("stage", 0, 0, 1)] if n == 4 else []

        def F(table):
            return [("F", f, 0, -1) for f in table.get(n, [])]
        pe = [("S", n, 0, 0), ("S", n, 1, 0), pa, ("At", a, 0, da), pb_, *F({3: ["back"], 4: ["a0"], 5: ["a1"], 6: ["a2"],
                                                                            7: ["w2"]}),
              ("At", a, 1, da), T0, ("Av", a, 0, da), pc, ("Av", a, 1, da), T1,
              *F({0: ["wo"], 1: ["tr"], 3: ["g0"], 4: ["g1"], 5: ["g2"]})]
        act = [*stage, *F({4: ["g0"], 5: ["g1"], 6: ["g2"]}), pa, ("At", a, 0, da), pb_, ("X2", n, 0, 0),
               *F({1: ["tr"], 3: ["back"]}), ("At", a, 1, da), T0, pc, ("Av", a, 1, da), T1]
        if n % 2 == 0:
            dve = [("X1", n, 0, 0), *F({2: ["tr"]}), ("Rb", tt, 2, dt), ("Rb", tt, 3, dt), ("X2", n, 0, 0),
                   *F({4: ["a0"], 6: ["a2"]}),
                   *(("Rs", pt, j, dp) for j in range(3))]
            pool = [("Rb", tt, 2, dt), ("X2", n, 0, 0), ("Rb", tt, 3, dt)]
        else:
            dve = [("X1", n, 0, 0), *F({1: ["wo"]}), ("Rs", pt, 3, dp), ("Ra", pt, 0, dp), ("X2", n, 0, 0),
                   ("Rb", pt, 0, dp), ("Rb", pt, 1, dp), *F({5: ["a1"], 7: ["w2"]})]
            pool = [("X2", n, 0, 0), ("Rb", pt, 0, dp), ("Rb", pt, 1, dp)]
        return {"pe": pe, "act": act, "dve": dve, "pool": pool}

    slots = [slot(n) for n in range(NBLK)]

    def turns(eng, name, step):
        def turn(i):
            for n in range(NBLK):
                for kind, k, j, dr in slots[n][name]:
                    r = i + dr
                    if not isinstance(i, int) or 0 <= r < ROUNDS:
                        step(kind, k, j, r, r % NB, r // NB)
        for i in range(-1, 2):
            turn(i)
        with eng.Fori(2, ROUNDS - 1) as i:
            turn(i)
        turn(ROUNDS - 1)
        turn(ROUNDS)

    with nc.Block() as block:
        @block.sync
        def _(sp):
            sp.dma_start(sq[:, 0:3, :].rearrange("p a b -> p (a b)"),
                         c.ins["qk_scales"].to_broadcast([128, DEPTH * 4 * DH])).then_inc(s["scl"], 16)

            def load_qkv(layer):
                c.wait_apart(sp, s["p"], (layer - 1) * (NB * UP))
                sp.dma_start(w_qkv[:, ds(layer % 2, 1), :], c.ins["w_qkv1"][layer]).then_inc(s["wa"], 16)

            def load_tail(layer):
                c.wait_apart(sp, s["out"], layer * NB)
                sp.dma_start(w_o[:, :, :], c.ins["w_o1"][layer]).then_inc(s["wf"], 16)
                sp.dma_start(w_1[:, :], c.ins["w_ff1"][layer]).then_inc(s["wf"], 16)
                sp.dma_start(w_2[:, :, :], c.ins["w_ff2"][layer]).then_inc(s["wf"], 16)
                sp.dma_start(cols[:, :], c.ins["cols_w"][layer]).then_inc(s["wf"], 16)

            def rounds_of(layer, more):
                for b in range(NB):
                    r = layer * NB + b
                    for t in range(TILES):
                        c.wait_apart(sp, s["pe"], r * UP + proj_use("V", t, 1) + 1)
                        c.wait_apart(sp, s["av"], r * UA + 4 * t - 2)
                        sp.dma_start(v_even[WIN:KEYS, :], v[t][0:BLK, :]).then_inc(s["ve"], 16)
                        if t:
                            sp.dma_start(v_even[0:WIN, :], v[t - 1][128 - WIN:128, :]).then_inc(s["ve"], 16)
                    if b == 0:
                        if more:
                            load_qkv(layer + 1)
                        if not isinstance(layer, int) or layer > 0:
                            load_tail(layer)
            load_qkv(0)
            load_tail(0)
            sp.wait_ge(s["z"], 3)
            rounds_of(0, True)
            with sp.Fori(1, DEPTH - 1) as layer:
                rounds_of(layer, True)
            rounds_of(DEPTH - 1, False)

        VE = 16 * (2 * TILES - 1)

        def mm_tail(pe, f, r, layer):
            if f == "wo":
                pe.wait_ge(s["wf"], (layer + 1) * 64)
                pe.wait_ge(s["ot"], (r + 1) * NBLK)
                wait(pe, s["out"], r)
                for pair in range(PAIRS):
                    last = pe.matmul(psF[:, :], w_o[:, pair, :], oT[:, pair, :], start=(pair == 0), stop=(pair == PAIRS - 1))
            elif f == "tr":
                pe.wait_ge(s["xsf"], r + 1)
                for t in range(TILES):
                    last = pe.transpose(psF[:, 128 * t:128 * (t + 1)], xsf[:, 128 * t:128 * (t + 1)], c.ident[:, :])
            elif f == "back":
                pe.wait_ge(s["yn"], r + 1)
                for t in range(TILES):
                    last = pe.transpose(psF[:, 128 * t:128 * (t + 1)], yn[:, t, :], c.ident[:, :])
            elif f[0] in "ga":
                k = int(f[1])
                at, m = CH[k]
                if f[0] == "g":
                    pe.wait_ge(s["xn"], r + 1)
                    wait(pe, s["hh"], 3 * r + k)
                    at += FF
                else:
                    pe.wait_ge(s["gg"], 3 * r + k + 1)
                last = pe.matmul(psF[0:m, :], w_1[:, at:at + m], xn[:, :], start=True, stop=True)
            else:
                pe.wait_ge(s["hh"], 3 * r + 3)
                for k, (at, m) in enumerate(CH):
                    last = pe.matmul(psF[:, :], w_2[0:m, k, :], hh[0:m, k, :], start=(k == 0), stop=(k == 2))
            last.then_inc(s["f"], 1)

        @block.tensor
        def _(pe):
            def step(kind, k, j, r, b, layer):
                if kind in "PV":
                    u = proj_use(kind, k, j)
                    if u == 0:
                        pe.wait_ge(s["wa"], (layer + 1) * 16)
                        pe.wait_ge(s["xs"], r + 1)
                    wait(pe, s["pe"], r * UP + u - 1)
                    at = 512 * (j if kind == "P" else 4 + j)
                    pe.matmul(psP[u % 2][:, :], xs[:, 128 * k:128 * (k + 1)],
                              w_qkv[:, ds(layer % 2, 1), at:at + 512], start=True, stop=True).then_inc(s["p"], 1)
                elif kind == "T":
                    wait(pe, s["te"], r * UT + 4 * k + j)
                    pe.wait_ge(s["qr"], r * UT + 4 * k + j + 1)
                    for q in range(4):
                        last = pe.transpose(psT[:, 128 * q:128 * (q + 1)], qr[:, j, 128 * q:128 * (q + 1)], c.ident[:, :])
                    last.then_inc(s["t"], 1)
                elif kind == "S":
                    if k % 2 == 0 and j == 0:
                        pe.wait_ge(s["te"], r * UT + 4 * (k // 2) + 4)
                    wait(pe, s["x1"], r * UA + 2 * (k - 1) + j + 1)
                    pe.matmul(psS[j][:, 0:4 * KEYS], c.ident_bf[:, :], c.band_bf[:, min(k, 1), :], start=True, stop=False,
                              skip_group_check=True)
                    for q in range(4):
                        last = pe.matmul(psS[j][:, q * KEYS:(q + 1) * KEYS], qb[(k // 2) % 2][:, 4 * j + q, k % 2, :, :],
                                         kT[:, 4 * j + q, BLK * k:BLK * k + KEYS], start=False, stop=True,
                                         skip_group_check=True)
                    last.then_inc(s["s"], 1)
                elif kind == "At":
                    rows = KEYS + WIN * (k % 2)
                    pe.wait_ge(s["pn"], r * NBLK + k + 1)
                    wait(pe, s["pte"], r * UA + 2 * k + j)
                    for q in range(4):
                        last = pe.transpose(psA[0:rows, 128 * q:128 * (q + 1)], pb[k % 2][:, 4 * j + q, :], c.ident[:, :])
                    last.then_inc(s["pt"], 1)
                elif kind == "Av":
                    t, odd = k // 2, k % 2
                    rows = KEYS + WIN * odd
                    if odd:
                        pe.wait_ge(s["pe"], r * UP + proj_use("V", t, 1) + 1)
                        vals = v[t]
                    else:
                        pe.wait_ge(s["ve"], r * VE + 16 * (2 * t + 1))
                        vals = v_even
                    if j == 0:
                        wait(pe, s["ot"], r * NBLK + k)
                    pe.wait_ge(s["pte"], r * UA + 2 * k + j + 1)
                    for pair in range(4 * j, 4 * j + 4):
                        for h in range(2):
                            last = pe.matmul(psO[64 * h:64 * h + 64, BLK * pair:BLK * (pair + 1)],
                                             vals[0:rows, (2 * pair + h) * DH:(2 * pair + h + 1) * DH],
                                             pT[0:rows, pair, BLK * h:BLK * (h + 1)], start=True, stop=True)
                    last.then_inc(s["av"], 1)
                else:
                    mm_tail(pe, k, r, layer)
            pe.wait_ge(s["z"], 3)
            turns(pe, "pe", step)

        @block.scalar
        def _(act):
            def step(kind, k, j, r, b, layer):
                if kind == "stage":
                    wait(act, s["p"], r * UP)
                    c.wait_apart(act, s["out"], r - 2)
                    act.activation(xs[0:64, :], c.H[0:64, ds(b * N, N)], ACT.Copy)
                    act.activation(xs[64:128, 1:N], c.H[64:128, ds(b * N, N - 1)], ACT.Copy).then_inc(s["xs"], 1)
                elif kind == "P":
                    u = proj_use("P", k, j)
                    wait(act, s["qr"], r * UT + 4 * (k - 2) + j + 1)
                    wait(act, s["sr"], r * UT + 4 * (k - 1) + j + 1)
                    act.wait_ge(s["p"], r * UP + u + 1)
                    act.activation(raw[k % 2][:, j, :], psP[u % 2][:, :], ACT.Copy)
                    act.activation(sq[:, j, :], psP[u % 2][:, :], ACT.Square).then_inc(s["pe"], 1)
                elif kind == "V":
                    u = proj_use("V", k, j)
                    wait(act, s["av"], (r - 1) * UA + 4 * k + 4)
                    if k == TILES - 1:
                        wait(act, s["ve"], r * VE)
                    else:
                        wait(act, s["ve"], (r - 1) * VE + 16 * (2 * k + 3))
                    act.wait_ge(s["p"], r * UP + u + 1)
                    act.activation(v[k][:, 512 * j:512 * (j + 1)], psP[u % 2][:, :], ACT.Copy).then_inc(s["pe"], 1)
                elif kind == "T":
                    act.wait_ge(s["t"], r * UT + 4 * k + j + 1)
                    src = psT[:, :].rearrange("p (a b) -> p a b", a=4)
                    if j < 2:
                        for h in range(2):
                            rows = slice(64 * h, 64 * h + 64)
                            last = act.activation(qb[k % 2][rows, 4 * j:4 * j + 4, :, h, :],
                                                  src[rows].rearrange("p a (b q) -> p a b q", b=2), ACT.Copy)
                    else:
                        last = act.activation(kT[:, 4 * (j - 2):4 * (j - 2) + 4, WIN + 128 * k:WIN + 128 * (k + 1)],
                                              src, ACT.Copy)
                    last.then_inc(s["te"], 1)
                elif kind == "X2":
                    act.wait_ge(s["x1"], r * UA + 2 * k + 2)
                    p = pb[k % 2][:, :, WIN * (k % 2):]
                    act.activation(p, p, ACT.Exp, scale=8.0).then_inc(s["e"], 1)
                elif kind == "At":
                    rows = KEYS + WIN * (k % 2)
                    wait(act, s["av"], r * UA + 2 * (k - 1) + j + 1)
                    act.wait_ge(s["pt"], r * UA + 2 * k + j + 1)
                    act.activation(pT[0:rows, 4 * j:4 * j + 4, :], psA[0:rows, :].rearrange("p (a b) -> p a b", a=4),
                                   ACT.Copy).then_inc(s["pte"], 1)
                elif kind == "Av":
                    if k == 0:
                        wait(act, s["f"], (r - 1) * 10 + 1)
                    act.wait_ge(s["av"], r * UA + 2 * k + 2)
                    act.activation(oT[:, :, BLK * k:BLK * (k + 1)], psO[:, :].rearrange("p (a b) -> p a b", b=BLK),
                                   ACT.Copy).then_inc(s["ot"], 1)
                elif k == "tr":
                    wait(act, s["yn"], r)
                    c.wait_apart(act, s["xf"], r + 1)
                    act.activation(xsf[0:64, :], c.H[0:64, ds(b * N, N)], ACT.Copy)
                    act.activation(xsf[64:128, 1:N], c.H[64:128, ds(b * N, N - 1)], ACT.Copy).then_inc(s["xsf"], 1)
                elif k == "back":
                    act.wait_ge(s["f"], r * 10 + 3)
                    act.activation(xn[:, :], psF[:, :], ACT.Identity, bias=cols[:, 1:2],
                                   scale=cols[:, 0:1]).then_inc(s["xn"], 1)
                else:
                    n, (at, m) = int(k[1]), CH[int(k[1])]
                    act.wait_ge(s["f"], r * 10 + 4 + 2 * n)
                    wait(act, s["hh"], 3 * r + n)
                    act.activation(gg[0:m, :], psF[0:m, :], ACT.Gelu, bias=cols[0:m, 5 + n:6 + n]).then_inc(s["gg"], 1)
            act.wait_ge(s["tab"], 4 * DEPTH)
            act.wait_ge(s["z"], 1)
            turns(act, "act", step)

        @block.vector
        def _(dve):
            def step(kind, k, j, r, b, layer):
                if kind == "Rs":
                    dve.wait_ge(s["pe"], r * UP + proj_use("P", k, j) + 1)
                    wait(dve, s["rn"], r * UT + 4 * (k - 2) + 4)
                    dve.tensor_reduce(nrm[k % 2][:, 0, 8 * j:8 * j + 8], sq[:, j, :].rearrange(
                        "p (h d) -> p h d", d=DH), AX_X, ALU.add).then_inc(s["sr"], 1)
                elif kind == "Ra":
                    nn = nrm[k % 2]
                    ch = Chain(dve, s_norm, 13, r * TILES + k)
                    dve.wait_ge(s["sr"], r * UT + 4 * k + 4)
                    ch.link(dve.tensor_scalar(nn[:, 0, :], nn[:, 0, :], 1e-24, None, ALU.max))
                    rsqrt(dve, ch, nn[:, 1, :], nn[:, 0, :], nn[:, 2, :], nn[:, 3, :], 0.0)
                    ch.end()
                elif kind == "Rb":
                    u = r * UT + 4 * k + j
                    xv = raw[k % 2][:, j, :].rearrange("p (h d) -> p h d", d=DH)
                    dve.tensor_tensor(xv, xv, nrm[k % 2][:, 1, 8 * j:8 * j + 8].unsqueeze(2).to_broadcast(
                        [128, 8, DH]), ALU.mult).then_inc(s["rn"], 1)
                    dve.wait_ge(s["rn"], u + 1)
                    wait(dve, s["t"], u - 3)
                    tab = tabs[:, ds(layer, 1), 2 * (j // 2), k, :].to_broadcast([128, 8, DH])
                    dve.tensor_tensor(qr[:, j, :].rearrange("p (h d) -> p h d", d=DH), xv, tab,
                                      ALU.mult).then_inc(s["t1"], 1)
                elif kind == "X1":
                    wait(dve, s["pt"], r * UA + 2 * (k - 2) + 2)
                    ch = Chain(dve, s_x, 3, r * NBLK + k)
                    p = pb[k % 2][:, :, WIN * (k % 2):]
                    for h in range(2):
                        sc = psS[h][:, 0:4 * KEYS].rearrange("p (a b) -> p a b", a=4)
                        dve.wait_ge(s["s"], r * UA + 2 * k + h + 1)
                        ch.link(dve.tensor_reduce(mx[:, 4 * h:4 * h + 4], sc, AX_X, ALU.max))
                        dve.tensor_tensor(p[:, 4 * h:4 * h + 4, :], sc,
                                          mx[:, 4 * h:4 * h + 4].unsqueeze(2).to_broadcast([128, 4, KEYS]),
                                          ALU.subtract).then_inc(s["x1"], 1)
                elif kind == "X2":
                    ch = Chain(dve, s_x, 3, r * NBLK + k)
                    ch.n = 2
                    dve.wait_ge(s["e"], r * NBLK + k + 1)
                    wait(dve, s["pn"], r * NBLK + k - 1)
                    ch.link(dve.tensor_reduce(sm[k % 2][:, :], pb[k % 2][:, :, WIN * (k % 2):], AX_X, ALU.add))
                    ch.end()
                    dve.reciprocal(sm[k % 2][:, :], sm[k % 2][:, :]).then_inc(s["r"], 1)
                elif k == "wo":
                    dve.wait_ge(s["f"], r * 10 + 1)
                    wait(dve, s["out"], r)
                    dve.tensor_tensor(c.H[:, ds(b * N, N)], psF[:, :], c.H[:, ds(b * N, N)], ALU.add).then_inc(s["xf"], 1)
                elif k == "tr":
                    cf = Chain(dve, s_f, 23, r)
                    dve.wait_ge(s["f"], r * 10 + 2)
                    norm_tokens(c, dve, cf, yn, psF[:, :].rearrange("p (t c) -> p t c", t=TILES), stats, mv, rs,
                                1e-5).then_inc(s["yn"], 1)
                    cf.end()
                elif k[0] == "a":
                    n, (at, m) = int(k[1]), CH[int(k[1])]
                    dve.wait_ge(s["f"], r * 10 + 5 + 2 * n)
                    dve.scalar_tensor_tensor(out=hh[0:m, n, :], in0=psF[0:m, :], scalar=cols[0:m, 2 + n:3 + n],
                                             in1=gg[0:m, :], op0=ALU.add, op1=ALU.mult).then_inc(s["hh"], 1)
                else:
                    dve.wait_ge(s["f"], r * 10 + 10)
                    dve.scalar_tensor_tensor(out=c.H[:, ds(b * N, N)], in0=psF[:, :], scalar=cols[:, 8:9],
                                             in1=c.H[:, ds(b * N, N)], op0=ALU.add, op1=ALU.add).then_inc(s["out"], 1)
            dve.wait_ge(s["tab"], 4 * DEPTH)
            turns(dve, "dve", step)

        @block.gpsimd
        def _(pool):
            pool.memset(xs[:, 0:1], 0.0)
            pool.memset(xsf[:, 0:1], 0.0).then_inc(s["z"], 1)
            for j in range(2):
                pool.memset(qb[j][:, :, :, :, :], 0.0)
            pool.memset(kT[:, :, 0:WIN], 0.0)
            pool.memset(pb[1][:, :, 0:WIN], 0.0).then_inc(s["z"], 1)
            pool.memset(v_even[:, :], 0.0).then_inc(s["z"], 1)
            pool.wait_ge(s["scl"], 16)
            for layer in range(DEPTH):
                for k, base in enumerate((c.rope_cos_q, c.rope_sin_q, c.rope_cos_k, c.rope_sin_k)):
                    pool.tensor_tensor(tabs[:, layer, k, :, :], base[:, :, :],
                                       scl[:, layer, ds(k, 1), :].to_broadcast([128, TILES, DH]), ALU.mult).then_inc(s["tab"], 1)

            def step(kind, k, j, r, b, layer):
                if kind == "Rb":
                    u = r * UT + 4 * k + j
                    xv = raw[k % 2][:, j, :].rearrange("p (h x d) -> p h x d", x=2, d=32)
                    tv = t2[:, :].rearrange("p (h x d) -> p h x d", x=2, d=32)
                    wait(pool, s["qr"], u)
                    c.wait_apart(pool, s["rn"], u + 1)
                    for x in range(2):
                        tab = tabs[:, ds(layer, 1), 2 * (j // 2) + 1, k, 32 * x:32 * x + 32].to_broadcast([128, 8, 32])
                        last = pool.tensor_tensor(tv[:, :, x, :], xv[:, :, 1 - x, :], tab, ALU.mult)
                    last.then_inc(s_pool, 1)
                    pool.wait_ge(s_pool, u + 1)
                    pool.wait_ge(s["t1"], u + 1)
                    pool.tensor_tensor(qr[:, j, :], qr[:, j, :], t2[:, :], ALU.add).then_inc(s["qr"], 1)
                else:
                    pool.wait_ge(s["r"], r * NBLK + k + 1)
                    p = pb[k % 2][:, :, WIN * (k % 2):]
                    pool.tensor_tensor(p, p, sm[k % 2][:, :].unsqueeze(2).to_broadcast([128, PAIRS, KEYS]),
                                       ALU.mult).then_inc(s["pn"], 1)
            pool.wait_ge(s["tab"], 4 * DEPTH)
            turns(pool, "pool", step)


def program(nc, ins, out):
    with ExitStack() as stack:
        c = Core(nc, ins, stack)
        place_tables(c)
        stages = [lambda: setup(c), lambda: adaln(c, 0, 0), lambda: convolutions(c), lambda: linear_attention(c),
                  lambda: feed_forward(c), lambda: adaln(c, 0, 1), lambda: experts(c), lambda: adaln(c, 1, 0),
                  lambda: causal_attention(c), lambda: adaln(c, 1, 1), lambda: windowed_layers(c),
                  lambda: finish(c, out)]
        for stage in stages:
            with ExitStack() as c.stage:
                stage()


def layouts(i):
    A = lambda n: np.asarray(i["L0_attn_" + n])
    E = lambda n: np.asarray(i["L0_ffn_" + n])
    B = lambda n: np.asarray(i["L1_attn_" + n])
    W = lambda n: np.asarray(i["L1_ffn_" + n])
    col = lambda a: a.reshape(-1, D).T
    swap = lambda a: np.concatenate([a[:, 32:], a[:, :32]], 1)
    FF, DEPTH = 341, 6

    def ff_cols(a):
        return np.pad(a, ((0, 0), (0, 3 * D - FF))).reshape(DEPTH, 3, D).transpose(0, 2, 1)

    return {
        "x": np.asarray(i["L0_attn_x"]).reshape(T, D).T,
        "c_cols": np.stack([np.asarray(i["L0_c"]).T, np.asarray(i["L1_c"]).T], 1),
        "w_mod": np.stack([np.asarray(i["L0_wmod"]), np.asarray(i["L1_wmod"])]),
        "tables_all_in": group_array("all"),
        "tables_0_in": group_array("L0"),
        "tables_1_in": group_array("L1"),
        "cols_conv": np.concatenate([A("conv1_w").reshape(D, 20), A("conv2_w").reshape(D, 20), A("conv1_b").reshape(D, 4),
                                     col(A("conv2_b")), col(A("ln0_g")), col(A("ln0_b"))], 1),
        "w_qkv0": np.concatenate([A("Wq"), A("Wk"), A("Wv")], 2),
        "b_kv0": np.concatenate([A("bk"), A("bv")], 1),
        "cols_la": np.stack([A("bq"), A("lnA_g"), A("lnA_b")], 2),
        "w_ff0a": A("W1"),
        "w_ff0b": A("W2").reshape(4, D, D).transpose(1, 0, 2),
        "cols_ff0": np.concatenate([col(A("b1")), col(A("b2")), col(A("ln2_g")), col(A("ln2_b"))], 1),
        "keys_rw": np.stack([E("keys").T, E("rw").T], 1),
        "rb": E("rb").reshape(1, 16),
        "b2_moe": E("b2"),
        "w1_moe": E("w1").transpose(0, 2, 1),
        "w2_moe": E("w2").reshape(16, D, 4, D).transpose(0, 3, 2, 1),
        "b1_moe": E("b1").reshape(16, 4, D).transpose(0, 2, 1),
        "w_qk1": np.stack([B("Wq"), B("Wk")], 1),
        "w_vdT": B("Wvdown").T,
        "w_vu": B("Wvup"),
        "qk_scales": np.stack([W("q_scale"), swap(W("q_scale")), W("k_scale"), swap(W("k_scale"))], 1).reshape(1, -1),
        "w_qkv1": W("Wqkv"),
        "w_o1": W("Wo").reshape(DEPTH, 8, D, D).transpose(0, 2, 1, 3),
        "w_ff1": W("W1"),
        "w_ff2": np.pad(W("W2"), ((0, 0), (0, 3 * D - FF), (0, 0))).reshape(DEPTH, 3, D, D).transpose(0, 2, 1, 3),
        "cols_w": np.concatenate([W("ln_g")[:, :, None], W("ln_b")[:, :, None], ff_cols(W("b1")[:, :FF]),
                                  ff_cols(W("b1")[:, FF:]), W("b2")[:, :, None]], 2),
    }


def kernel(**inputs):
    import concourse.bacc as _bacc
    from concourse.bass_utils import run_bass_kernel_spmd as _run

    nc = _bacc.Bacc("TRN2", target_bir_lowering=False, num_devices=1)
    arrays, ins = {}, {}
    for name, a in layouts(inputs).items():
        a = np.ascontiguousarray(a)
        arrays[f"in_{name}"] = a
        ins[name] = nc.dram_tensor(f"in_{name}", a.shape, mybir.dt.from_np(a.dtype), kind="ExternalInput").ap()
    out = nc.dram_tensor("out_x", (D, T), F32, kind="ExternalOutput").ap()
    program(nc, ins, out)
    r = _run(nc, [arrays], core_ids=[0])
    return np.ascontiguousarray(r.results[0]["out_x"].T.reshape(NB, N, D))
```

```python
from contextlib import ExitStack

import numpy as np

import concourse.bass as bass
from concourse import mybir

F32 = mybir.dt.float32
BF16 = mybir.dt.bfloat16
I32 = mybir.dt.int32
ALU = mybir.AluOpType
ACT = mybir.ActivationFunctionType
AX_X = mybir.AxisListType.X
ds = bass.ds

D = 128
NB, N = 4, 512
T = NB * N
TILES = N // 128
MAGIC = float(0x5F3759DF)


class Chain:

    def __init__(self, eng, sem, per_iteration=0, iteration=0):
        self.eng, self.sem, self.n = eng, sem, 0
        self.per, self.base = per_iteration, per_iteration * iteration

    def inc(self, instruction):
        self.n += 1
        instruction.then_inc(self.sem, 1)
        return self.n

    def wait(self, mark):
        self.eng.wait_ge(self.sem, self.base + mark)

    def link(self, instruction):
        self.wait(self.inc(instruction))

    def end(self):
        assert self.n == self.per, (self.n, self.per)


def rsqrt(dve, ch, y, x, half, tmp, eps):
    ch.link(dve.tensor_scalar(half, x, float(eps), None, ALU.add))
    ch.link(dve.tensor_scalar(y.bitcast(I32), half.bitcast(I32), -0.5, MAGIC, ALU.mult, ALU.add))
    ch.link(dve.tensor_scalar(half, half, -0.5, None, ALU.mult))
    for _ in range(3):
        ch.link(dve.tensor_tensor(tmp, y, y, ALU.mult))
        ch.link(dve.tensor_tensor(tmp, tmp, half, ALU.mult))
        ch.link(dve.scalar_tensor_tensor(out=y, in0=tmp, scalar=1.5, in1=y, op0=ALU.add, op1=ALU.mult))


def norm_tokens(c, dve, ch, out, src, stats, mv, rs, eps):
    marks = [ch.inc(dve.bn_stats(stats[:, t, :], src[:, t, :])) for t in range(TILES)]
    c.wait_apart(dve, ch.sem, ch.base + marks[-1])
    marks = [ch.inc(dve.bn_aggr(mv[:, t, :], stats[:, t, :])) for t in range(TILES)]
    ch.wait(marks[-1])
    rsqrt(dve, ch, rs[:, 0, :], mv[:, :, 1], rs[:, 1, :], rs[:, 2, :], eps)
    for t in range(TILES):
        last = dve.tensor_scalar(out[:, t, :], src[:, t, :], mv[:, t, 0:1], rs[:, 0, t:t + 1],
                                 ALU.subtract, ALU.mult)
        if t < TILES - 1:
            ch.inc(last)
    return last


class Core:

    def __init__(self, nc, ins, stack):
        self.nc, self.ins, self.stack = nc, ins, stack
        self.stage = stack

    def sb(self, name, shape, dt=F32, keep=False):
        return (self.stack if keep else self.stage).enter_context(self.nc.sbuf_tensor(name, shape, dt))

    def ps(self, name, shape=(128, 512), dt=F32):
        return self.stage.enter_context(self.nc.psum_tensor(name, list(shape), dt))

    def wait_apart(self, eng, sem, value):
        wait(eng, sem, value)
        if not isinstance(value, int):
            eng.sem_inc(self.passed)

    def sem(self, name, keep=False):
        return (self.stack if keep else self.stage).enter_context(self.nc.semaphore(name))


def wait(eng, sem, value):
    if not isinstance(value, int) or value > 0:
        eng.wait_ge(sem, value)


def shape_constants():
    out = {}
    inv = (1.0 / 10000.0 ** (np.arange(0, D, 2, dtype=np.float32) / np.float32(D))).astype(np.float32)
    freqs = np.repeat(np.arange(N, dtype=np.float32)[:, None] * inv[None, :], 2, axis=-1)
    cos, sin = np.cos(freqs).astype(np.float32), np.sin(freqs).astype(np.float32)
    by_tile = lambda a: a.reshape(TILES, 128, -1).transpose(1, 0, 2)
    out["cos_tok"], out["sin_tok"] = by_tile(cos), by_tile(sin)
    out["cos_feat"], out["sin_feat"] = cos.T, sin.T
    rot = np.zeros((D, D), np.float32)
    rot[np.arange(0, D, 2), np.arange(1, D, 2)] = -1
    rot[np.arange(1, D, 2), np.arange(0, D, 2)] = 1
    out["rot"], out["rot_t"] = rot, rot.T
    out["ident"] = np.eye(D, dtype=np.float32)
    head = np.kron(np.eye(16), np.ones((8, 8))).astype(np.float32)
    out["headmask"] = np.stack([head, head], axis=1)
    out["ones_n"] = np.full((D, D), 1.0 / N, np.float32)
    out["ones"] = np.ones((D, D), np.float32)
    half = np.arange(0, 64, 2, dtype=np.float32)
    fr = np.arange(N, dtype=np.float32)[:, None] * (1.0 / 10000.0 ** (half / 64)).astype(np.float32)[None, :]
    base = ((half + np.float32(0.4 * 64)) / np.float32(1.4 * 64)).astype(np.float32)
    power = ((np.arange(N, dtype=np.float32) - N // 2) / 16).astype(np.float32)
    scale = (base[None, :] ** power[:, None]).astype(np.float32)
    c1, s1 = np.cos(fr).astype(np.float32), np.sin(fr).astype(np.float32)
    for kind, f in (("q", scale), ("k", (1.0 / scale).astype(np.float32))):
        out["rope_cos_" + kind] = by_tile(np.concatenate([c1 * f, c1 * f], -1))
        out["rope_sin_" + kind] = by_tile(np.concatenate([-s1 * f, s1 * f], -1))
    out["causal"] = by_tile(np.tril(np.ones((N, N), np.float32)))
    qpos, kpos = np.tile(np.arange(64), 2)[:, None], np.arange(-32, 64)[None, :]
    band = (qpos - kpos >= 0) & (qpos - kpos <= 32)
    out["band"] = np.stack([np.tile(np.where(m, 0.0, -1e30), (1, 4)) for m in (band & (kpos >= 0), band)],
                           axis=1).astype(np.float32)
    return {k: np.ascontiguousarray(v, np.float32) for k, v in out.items()}


GROUPS = {
    "all": ("ident", "ones", "band"),
    "L0": ("cos_tok", "sin_tok", "cos_feat", "sin_feat", "rot", "rot_t", "headmask", "ones_n"),
    "L1": ("causal", "rope_cos_q", "rope_sin_q", "rope_cos_k", "rope_sin_k"),
}


def group_array(group):
    tables = shape_constants()
    return np.concatenate([tables[name].reshape(128, -1) for name in GROUPS[group]], 1)


def place_tables(c):
    tables = shape_constants()
    width = {g: sum(tables[name].size // 128 for name in names) for g, names in GROUPS.items()}
    c.tables_all = c.sb("tables_all", [128, width["all"]], keep=True)
    both = c.sb("tables_layer", [128, max(width["L0"], width["L1"])], keep=True)
    c.tables_0, c.tables_1 = both[:, 0:width["L0"]], both[:, 0:width["L1"]]
    views = {}
    for group, buf in (("all", c.tables_all), ("L0", c.tables_0), ("L1", c.tables_1)):
        at = 0
        for name in GROUPS[group]:
            shape = tables[name].shape
            v = buf[:, at:at + tables[name].size // 128]
            at += tables[name].size // 128
            views[name] = v.rearrange("p (a b) -> p a b", a=shape[1]) if len(shape) == 3 else v
    c.ident, c.ones, c.band = (views[name] for name in GROUPS["all"])
    c.cos_tok, c.sin_tok, c.cos_feat, c.sin_feat, c.rot, c.rot_t, c.headmask, c.ones_n = (
        views[name] for name in GROUPS["L0"])
    c.causal, c.rope_cos_q, c.rope_sin_q, c.rope_cos_k, c.rope_sin_k = (views[name] for name in GROUPS["L1"])


def setup(c):
    nc = c.nc
    c.passed = c.sem("passed", keep=True)
    c.adaln_sems = [c.sem("n_s_" + k, keep=True) for k in ("xs", "tr", "yn", "back", "h", "dve")]
    c.X = c.sb("X", [D, T], keep=True)
    c.H = c.sb("H", [D, T], keep=True)
    c.mods = c.sb("mods", [D, 2, 6, NB], keep=True)
    c.ident_bf = c.sb("ident_bf", [D, D], BF16, keep=True)
    c.band_bf = c.sb("band_bf", [D, 2, 384], BF16, keep=True)
    cT = c.sb("m_cT", [D, 2, NB])
    sT = c.sb("m_sT", [D, 2, NB])
    wm = [c.sb(f"m_w{j}", [D, 6 * D]) for j in range(2)]
    ga = c.sb("m_abs", [D, 2, 2, NB])
    gs = c.sb("m_sign", [D, 2, 2, NB])
    ps = c.ps("m_ps")
    s_x, s_c, s_k = c.sem("m_s_x"), c.sem("m_s_c"), c.sem("m_s_tables")
    s_silu, s_mm, s_ch = c.sem("m_s_silu"), c.sem("m_s_mm"), c.sem("m_s_dve")

    with nc.Block() as block:
        @block.sync
        def _(sp):
            sp.dma_start(cT[:, :, :], c.ins["c_cols"]).then_inc(s_c, 16)
            for j in range(2):
                sp.dma_start(wm[j][:, :], c.ins["w_mod"][j]).then_inc(s_c, 16)
            sp.dma_start(c.X[:, :], c.ins["x"]).then_inc(s_x, 16)
            sp.dma_start(c.tables_all[:, :], c.ins["tables_all_in"]).then_inc(s_k, 16)
            sp.dma_start(c.tables_0, c.ins["tables_0_in"]).then_inc(s_k, 16)
            sp.wait_ge(s_x, 16)
            sp.wait_ge(s_k, 32)

        @block.scalar
        def _(act):
            act.wait_ge(s_c, 48)
            act.activation(sT[:, :, :], cT[:, :, :], ACT.Silu).then_inc(s_silu, 1)

        @block.tensor
        def _(pe):
            pe.wait_ge(s_silu, 1)
            for l in range(2):
                for j in range(6):
                    at = (l * 6 + j) * NB
                    last = pe.matmul(ps[:, at:at + NB], wm[l][:, j * D:(j + 1) * D], sT[:, l, :], start=True, stop=True)
            last.then_inc(s_mm, 1)

        @block.vector
        def _(dve):
            ch = Chain(dve, s_ch)
            dve.wait_ge(s_mm, 1)
            ch.link(dve.tensor_copy(c.mods[:, :, :, :], ps[:, 0:48].rearrange("p (l j b) -> p l j b", l=2, j=6)))
            for j in (1, 4):
                ch.inc(dve.tensor_scalar(c.mods[:, :, j, :], c.mods[:, :, j, :], 1.0, None, ALU.add))
            for n, j in enumerate((2, 5)):
                g = c.mods[:, :, j, :]
                ch.link(dve.scalar_tensor_tensor(out=ga[:, n, :, :], in0=g, scalar=-1.0, in1=g, op0=ALU.mult, op1=ALU.max))
                ch.link(dve.tensor_scalar(ga[:, n, :, :], ga[:, n, :, :], 0.25, None, ALU.max))
                ch.link(dve.tensor_scalar(gs[:, n, :, :], g, 0.0, 2.0, ALU.is_ge, ALU.mult))
                ch.link(dve.tensor_scalar(gs[:, n, :, :], gs[:, n, :, :], -1.0, None, ALU.add))
                ch.inc(dve.tensor_tensor(g, ga[:, n, :, :], gs[:, n, :, :], ALU.mult))
            dve.wait_ge(s_k, 32)
            ch.inc(dve.tensor_copy(c.ident_bf[:, :], c.ident[:, :]))
            ch.link(dve.tensor_copy(c.band_bf[:, :, :], c.band[:, :, :]))


def adaln(c, layer, part):
    nc, n = c.nc, f"n{layer}{part}_"
    UN = 2
    xs = [c.sb(n + f"xs{u}", [D, N]) for u in range(UN)]
    yn = [c.sb(n + f"yn{u}", [128, TILES, D]) for u in range(UN)]
    stats = [c.sb(n + f"stats{u}", [128, TILES, 6]) for u in range(UN)]
    mv = [c.sb(n + f"mv{u}", [128, TILES, 2]) for u in range(UN)]
    rs = [c.sb(n + f"rs{u}", [128, 3, TILES]) for u in range(UN)]
    ps = [c.ps(n + f"ps{u}") for u in range(UN)]
    s_xs, s_tr, s_yn, s_bk, s_h, s_ch = c.adaln_sems
    done = (2 * layer + part) * NB
    with nc.Block() as block:
        @block.scalar
        def _(act):
            for pair in range(NB // UN):
                for u in range(UN):
                    wait(act, s_tr, done + pair * UN)
                    act.activation(xs[u][:, :], c.X[:, ds((pair * UN + u) * N, N)], ACT.Copy).then_inc(s_xs, 1)
                for u in range(UN):
                    b = pair * UN + u
                    act.wait_ge(s_bk, done + b + 1)
                    act.activation(c.H[:, ds(b * N, N)], ps[u][:, :], ACT.Identity,
                                   bias=c.mods[:, layer, 3 * part, ds(b, 1)],
                                   scale=c.mods[:, layer, 3 * part + 1, ds(b, 1)]).then_inc(s_h, 1)

        @block.tensor
        def _(pe):
            for pair in range(NB // UN):
                for u in range(UN):
                    pe.wait_ge(s_xs, done + pair * UN + u + 1)
                    wait(pe, s_h, done + pair * UN)
                    for t in range(TILES):
                        tt = slice(128 * t, 128 * t + 128)
                        last = pe.transpose(ps[u][:, tt], xs[u][:, tt], c.ident[:, :])
                    last.then_inc(s_tr, 1)
                for u in range(UN):
                    pe.wait_ge(s_yn, done + pair * UN + u + 1)
                    for t in range(TILES):
                        last = pe.transpose(ps[u][:, 128 * t:128 * t + 128], yn[u][:, t, :], c.ident[:, :])
                    last.then_inc(s_bk, 1)

        @block.vector
        def _(dve):
            for pair in range(NB // UN):
                ch = Chain(dve, s_ch, 46, done // UN + pair)
                for u in range(UN):
                    dve.wait_ge(s_tr, done + pair * UN + u + 1)
                    norm_tokens(c, dve, ch, yn[u], ps[u][:, :].rearrange("p (t c) -> p t c", t=TILES), stats[u], mv[u],
                                rs[u], 1e-5).then_inc(s_yn, 1)
                ch.end()


def convolutions(c):
    nc = c.nc
    UN, O, K = 2, 4, 5
    cols = c.sb("c_cols_sb", [D, 2 * O * K + O + 3])
    w1, w2 = cols[:, 0:O * K], cols[:, O * K:2 * O * K]
    b1 = cols[:, 2 * O * K:2 * O * K + O]
    b2, gain, shift = (cols[:, 2 * O * K + O + j:2 * O * K + O + j + 1] for j in range(3))
    diag = c.sb("c_diag", [D, O * K, D])
    hp = [c.sb(f"c_hp{u}", [D, N + K - 1]) for u in range(UN)]
    hid = [c.sb(f"c_hid{u}", [D, O, N + K - 1]) for u in range(UN)]
    acc = [c.sb(f"c_acc{u}", [D, N]) for u in range(UN)]
    yn = [c.sb(f"c_yn{u}", [128, TILES, D]) for u in range(UN)]
    stats = [c.sb(f"c_stats{u}", [128, TILES, 6]) for u in range(UN)]
    mv = [c.sb(f"c_mv{u}", [128, TILES, 2]) for u in range(UN)]
    rs = [c.sb(f"c_rs{u}", [128, 3, TILES]) for u in range(UN)]
    psC = [c.ps(f"c_psC{j}") for j in range(4)]
    psN = [c.ps(f"c_psN{u}") for u in range(UN)]
    s = {k: c.sem("c_s_" + k) for k in ("w", "z", "dg", "hp", "c1", "hid", "acc", "tr", "yn", "back", "h")}
    s_ch, s_ch0 = c.sem("c_s_dve"), c.sem("c_s_dve0")
    with nc.Block() as block:
        @block.sync
        def _(sp):
            sp.dma_start(cols[:, :], c.ins["cols_conv"]).then_inc(s["w"], 16)

        @block.gpsimd
        def _(pool):
            for u in range(UN):
                pool.memset(hp[u][:, :], 0.0)
                last = pool.memset(hid[u][:, :, :], 0.0)
            last.then_inc(s["z"], 1)

        @block.scalar
        def _(act):
            act.wait_ge(s["w"], 16)
            act.wait_ge(s["z"], 1)
            for pair in range(NB // UN):
                it = pair * UN
                for u in range(UN):
                    wait(act, s["acc"], it)
                    act.activation(hp[u][:, 2:2 + N], c.H[:, ds((it + u) * N, N)], ACT.Copy).then_inc(s["hp"], 1)
                for u in range(UN):
                    for o in range(O):
                        act.wait_ge(s["c1"], (it + u) * O + o + 1)
                        act.activation(hid[u][:, o, 2:2 + N], psC[o][:, :], ACT.Gelu,
                                       bias=b1[:, o:o + 1]).then_inc(s["hid"], 1)
                for u in range(UN):
                    act.wait_ge(s["back"], it + u + 1)
                    act.activation(c.H[:, ds((it + u) * N, N)], psN[u][:, :], ACT.Identity, bias=shift,
                                   scale=gain).then_inc(s["h"], 1)

        @block.tensor
        def _(pe):
            pe.wait_ge(s["dg"], O * K)
            for pair in range(NB // UN):
                it = pair * UN
                for u in range(UN):
                    pe.wait_ge(s["hp"], it + u + 1)
                    for o in range(O):
                        if u:
                            pe.wait_ge(s["hid"], it * O + o + 1)
                        else:
                            wait(pe, s["hid"], it * O)
                        for k in range(K):
                            last = pe.matmul(psC[o][:, :], diag[:, o * K + k, :], hp[u][:, k:k + N],
                                             start=(k == 0), stop=(k == K - 1))
                        last.then_inc(s["c1"], 1)
                for u in range(UN):
                    pe.wait_ge(s["acc"], it + u + 1)
                    wait(pe, s["h"], it)
                    for t in range(TILES):
                        tt = slice(128 * t, 128 * t + 128)
                        last = pe.transpose(psN[u][:, tt], acc[u][:, tt], c.ident[:, :])
                    last.then_inc(s["tr"], 1)
                for u in range(UN):
                    pe.wait_ge(s["yn"], it + u + 1)
                    for t in range(TILES):
                        last = pe.transpose(psN[u][:, 128 * t:128 * t + 128], yn[u][:, t, :], c.ident[:, :])
                    last.then_inc(s["back"], 1)

        @block.vector
        def _(dve):
            dve.wait_ge(s["w"], 16)
            for j in range(O * K):
                dve.tensor_scalar(diag[:, j, :], c.ident[:, :], w1[:, j:j + 1], None, ALU.mult).then_inc(s["dg"], 1)
            for pair in range(NB // UN):
                it = pair * UN
                ch = Chain(dve, s_ch, 46 + 2 * O * K, pair)
                for u in range(UN):
                    a = acc[u][:, :]
                    for o in range(O):
                        dve.wait_ge(s["hid"], (it + u) * O + o + 1)
                        for k in range(K):
                            x, w = hid[u][:, o, k:k + N], w2[:, o * K + k:o * K + k + 1]
                            if o == 0 and k == 0:
                                wait(dve, s["tr"], it)
                                ch.link(dve.tensor_scalar(a, x, w, b2, ALU.mult, ALU.add))
                            else:
                                ch.link(dve.scalar_tensor_tensor(out=a, in0=x, scalar=w, in1=a, op0=ALU.mult, op1=ALU.add))
                    dve.tensor_tensor(a, a, hp[u][:, 2:2 + N], ALU.add).then_inc(s["acc"], 1)
                for u in range(UN):
                    dve.wait_ge(s["tr"], it + u + 1)
                    norm_tokens(c, dve, ch, yn[u], psN[u][:, :].rearrange("p (t c) -> p t c", t=TILES), stats[u], mv[u],
                                rs[u], 1e-12).then_inc(s["yn"], 1)
                ch.end()


def feed_forward(c):
    nc = c.nc
    UN, C = 2, 4
    w1 = c.sb("f_w1", [D, C * D])
    w2 = c.sb("f_w2", [D, C, D])
    cols = c.sb("f_cols", [D, C + 3])
    hh = [c.sb(f"f_hh{u}", [D, C, N]) for u in range(UN)]
    y = [c.sb(f"f_y{u}", [D, N]) for u in range(UN)]
    yn = [c.sb(f"f_yn{u}", [128, TILES, D]) for u in range(UN)]
    ya = [c.sb(f"f_ya{u}", [D, N]) for u in range(UN)]
    stats = [c.sb(f"f_stats{u}", [128, TILES, 6]) for u in range(UN)]
    mv = [c.sb(f"f_mv{u}", [128, TILES, 2]) for u in range(UN)]
    rs = [c.sb(f"f_rs{u}", [128, 3, TILES]) for u in range(UN)]
    psC = [c.ps(f"f_psC{j}") for j in range(2)]
    psY = [c.ps(f"f_psY{u}") for u in range(UN)]
    s = {k: c.sem("f_s_" + k) for k in ("w", "c1", "hh", "o", "y", "tr", "yn", "back", "ya", "x")}
    s_ch = c.sem("f_s_dve")
    with nc.Block() as block:
        @block.sync
        def _(sp):
            sp.dma_start(w1[:, :], c.ins["w_ff0a"]).then_inc(s["w"], 16)
            sp.dma_start(w2[:, :, :], c.ins["w_ff0b"]).then_inc(s["w"], 16)
            sp.dma_start(cols[:, :], c.ins["cols_ff0"]).then_inc(s["w"], 16)

        @block.tensor
        def _(pe):
            pe.wait_ge(s["w"], 48)
            for pair in range(NB // UN):
                it = pair * UN
                for u in range(UN):
                    for j in range(C):
                        if u == 0 and j < 2:
                            wait(pe, s["hh"], it * C)
                        else:
                            wait(pe, s["hh"], (it + u) * C + j - 1)
                        pe.matmul(psC[j % 2][:, :], w1[:, j * D:(j + 1) * D], c.H[:, ds((it + u) * N, N)], start=True,
                                  stop=True).then_inc(s["c1"], 1)
                for u in range(UN):
                    wait(pe, s["hh"], (it + u + 1) * C)
                    wait(pe, s["ya"], it)
                    for j in range(C):
                        last = pe.matmul(psY[u][:, :], w2[:, j, :], hh[u][:, j, :], start=(j == 0), stop=(j == C - 1))
                    last.then_inc(s["o"], 1)
                for u in range(UN):
                    pe.wait_ge(s["y"], it + u + 1)
                    for t in range(TILES):
                        tt = slice(128 * t, 128 * t + 128)
                        last = pe.transpose(psY[u][:, tt], y[u][:, tt], c.ident[:, :])
                    last.then_inc(s["tr"], 1)
                for u in range(UN):
                    pe.wait_ge(s["yn"], it + u + 1)
                    for t in range(TILES):
                        last = pe.transpose(psY[u][:, 128 * t:128 * t + 128], yn[u][:, t, :], c.ident[:, :])
                    last.then_inc(s["back"], 1)

        @block.scalar
        def _(act):
            act.wait_ge(s["w"], 48)
            for pair in range(NB // UN):
                it = pair * UN
                for u in range(UN):
                    wait(act, s["o"], it)
                    for j in range(C):
                        act.wait_ge(s["c1"], (it + u) * C + j + 1)
                        act.activation(hh[u][:, j, :], psC[j % 2][:, :], ACT.Gelu, bias=cols[:, j:j + 1]).then_inc(s["hh"], 1)
                for u in range(UN):
                    act.wait_ge(s["back"], it + u + 1)
                    wait(act, s["x"], it)
                    act.activation(ya[u][:, :], psY[u][:, :], ACT.Identity, bias=cols[:, C + 2:C + 3],
                                   scale=cols[:, C + 1:C + 2]).then_inc(s["ya"], 1)

        @block.vector
        def _(dve):
            for pair in range(NB // UN):
                it = pair * UN
                ch = Chain(dve, s_ch, 46, pair)
                for u in range(UN):
                    dve.wait_ge(s["o"], it + u + 1)
                    dve.scalar_tensor_tensor(out=y[u][:, :], in0=psY[u][:, :], scalar=cols[:, C:C + 1],
                                             in1=c.H[:, ds((it + u) * N, N)], op0=ALU.add, op1=ALU.add).then_inc(s["y"], 1)
                for u in range(UN):
                    dve.wait_ge(s["tr"], it + u + 1)
                    norm_tokens(c, dve, ch, yn[u], psY[u][:, :].rearrange("p (t c) -> p t c", t=TILES), stats[u], mv[u],
                                rs[u], 1e-12).then_inc(s["yn"], 1)
                for u in range(UN):
                    b = it + u
                    dve.wait_ge(s["ya"], b + 1)
                    dve.scalar_tensor_tensor(out=c.X[:, ds(b * N, N)], in0=ya[u][:, :], scalar=c.mods[:, 0, 2, ds(b, 1)],
                                             in1=c.X[:, ds(b * N, N)], op0=ALU.mult, op1=ALU.add).then_inc(s["x"], 1)
                ch.end()


def linear_attention(c):
    nc = c.nc
    LAYERS, NH, HD = 4, 16, 8
    UN = 2
    hs = [c.sb(f"la_hs{u}", [D, N]) for u in range(UN)]
    qg = [c.sb(f"la_qg{u}", [D, N]) for u in range(UN)]
    qp = [c.sb(f"la_qp{u}", [D, N]) for u in range(UN)]
    qc = [c.sb(f"la_qc{u}", [D, N]) for u in range(UN)]
    qs = [c.sb(f"la_qs{u}", [D, N]) for u in range(UN)]
    kg = [c.sb(f"la_kg{u}", [128, TILES, D]) for u in range(UN)]
    kc = [c.sb(f"la_kc{u}", [128, TILES, D]) for u in range(UN)]
    ks = [c.sb(f"la_ks{u}", [128, TILES, D]) for u in range(UN)]
    vv = [c.sb(f"la_v{u}", [128, TILES, D]) for u in range(UN)]
    a12 = [c.sb(f"la_a12_{u}", [D, 3, D]) for u in range(UN)]
    kvm = [c.sb(f"la_kvm{u}", [D, 2, D]) for u in range(UN)]
    kmm = [c.sb(f"la_kmm{u}", [D, D]) for u in range(UN)]
    z = [c.sb(f"la_z{u}", [128, TILES * NH]) for u in range(UN)]
    y = [c.sb(f"la_y{u}", [128, TILES, D]) for u in range(UN)]
    yn = [c.sb(f"la_yn{u}", [128, TILES, D]) for u in range(UN)]
    stats = [c.sb(f"la_stats{u}", [128, TILES, 6]) for u in range(UN)]
    mv = [c.sb(f"la_mv{u}", [128, TILES, 2]) for u in range(UN)]
    rs = [c.sb(f"la_rs{u}", [128, 3, TILES]) for u in range(UN)]
    wqkv = c.sb("la_wqkv", [D, 3 * D])
    lcols = c.sb("la_cols", [D, 3, LAYERS])
    bias = c.sb("la_bias", [3, LAYERS * 2 * D])
    rest = c.sb("la_rest", [3, LAYERS * 2 * D])
    part = c.sb("la_part", [3, 3, LAYERS * 2 * D], BF16)
    bias3 = c.sb("la_bias3", [3, LAYERS * 2 * D], BF16)
    ones3 = c.sb("la_ones3", [3, D], BF16)
    psQ = [c.ps(f"la_psQ{u}") for u in range(UN)]
    psK = [c.ps(f"la_psK{u}", (128, 2, 512)) for u in range(UN)]
    psA = [c.ps(f"la_psA{u}") for u in range(UN)]

    names = ("w", "c", "b3", "hs", "q", "kv", "qg", "kg", "v", "qc", "kc", "a", "a12", "kmm", "r", "kvm", "o", "yn", "t",
             "h", "x", "y")
    s = {k: c.sem("la_s_" + k) for k in names}
    s_bias, s_k, s_q, s_y, s_n = (c.sem("la_s_chain_" + k) for k in ("bias", "k", "q", "y", "norm"))

    ORDER = {
        "pe": "kv0 r3- t2- q0 o3- a0 kv1 x0 r0 q1 t3- o0 a1 kv2 r1 x1 t0 o1 a2 q2 q3 r2 x2 kv3 t1 o2 x3 a3",
        "act": "hs0 a123- kg0 H2- hs1 qg0 v0 a120 hs2 kg1 qg1 H3- v1 a121 kg2 v2 hs3 H0 a122 qg2 qg3 kg3 H1 v3",
        "dve": "n2- kmm3- kvm3- kc0 qc0 y3- n3- kmm0 kvm0 kc1 qc1 y0 n0 kmm1 kvm1 kc2 y1 n1 qc2 kmm2 kvm2 qc3 kc3 y2",
    }

    def layers(eng, name, step):
        def turn(i):
            for word in ORDER[name].split():
                before = word[-1] == "-"
                word = word.rstrip("-")
                layer = i - 1 if before else i
                if not isinstance(i, int) or 0 <= layer < LAYERS:
                    b = int(word[-1])
                    step(word[:-1], b, layer * NB + b, layer)
        turn(0)
        turn(1)
        with eng.Fori(2, LAYERS) as i:
            turn(i)
        turn(LAYERS)

    with nc.Block() as block:
        @block.sync
        def _(sp):
            sp.dma_start(lcols[:, :, :], c.ins["cols_la"]).then_inc(s["c"], 16)
            sp.dma_start(bias[:, :], c.ins["b_kv0"].to_broadcast([3, LAYERS * 2 * D])).then_inc(s["c"], 16)
            for layer in range(LAYERS):
                wait(sp, s["kv"], layer * NB)
                wait(sp, s["q"], layer * NB)
                sp.dma_start(wqkv[:, :], c.ins["w_qkv0"][layer]).then_inc(s["w"], 16)

        @block.tensor
        def _(pe):
            def step(kind, b, g, layer):
                u = b % UN
                if kind in ("q", "kv"):
                    pe.wait_ge(s["w"], (layer + 1) * 16)
                    pe.wait_ge(s["hs"], g + 1)
                    wait(pe, s["y"], g - 1)
                if kind == "q":
                    pe.matmul(psQ[u][:, :], wqkv[:, 0:D], hs[u][:, :], start=True, stop=True).then_inc(s["q"], 1)
                elif kind == "kv":
                    for t in range(TILES):
                        o = psK[u][:, t // 2, (t % 2) * 256:(t % 2 + 1) * 256]
                        pe.matmul(o, hs[u][:, t * 128:(t + 1) * 128], wqkv[:, D:3 * D], start=True, stop=False)
                        last = pe.matmul(o, ones3[:, :], bias3[:, ds(layer * 2 * D, 2 * D)], start=False, stop=True)
                    last.then_inc(s["kv"], 1)
                elif kind == "a":
                    pe.wait_ge(s["kc"], g + 1)
                    pe.wait_ge(s["v"], g + 1)
                    wait(pe, s["h"], g - 1)
                    for j, kk in enumerate((kc, ks)):
                        for t in range(TILES):
                            pe.matmul(psA[u][:, j * D:(j + 1) * D], kk[u][:, t, :], vv[u][:, t, :],
                                      start=(t == 0), stop=(t == TILES - 1))
                    for t in range(TILES):
                        last = pe.matmul(psA[u][:, 2 * D:3 * D], kg[u][:, t, :], c.ones_n[:, :],
                                         start=(t == 0), stop=(t == TILES - 1))
                    last.then_inc(s["a"], 1)
                elif kind == "x":
                    pe.wait_ge(s["v"], g + 1)
                    for t in range(TILES):
                        last = pe.transpose(psK[u][:, 0, t * 128:(t + 1) * 128], hs[u][:, t * 128:(t + 1) * 128],
                                            c.ident[:, :])
                    last.then_inc(s["x"], 1)
                elif kind == "r":
                    pe.wait_ge(s["a12"], g + 1)
                    pe.matmul(psA[u][:, 0:D], c.ident[:, :], a12[u][:, 0, :], start=True, stop=False)
                    pe.matmul(psA[u][:, 0:D], c.rot_t[:, :], a12[u][:, 1, :], start=False, stop=True)
                    pe.matmul(psA[u][:, D:2 * D], c.rot[:, :], a12[u][:, 0, :], start=True, stop=False)
                    pe.matmul(psA[u][:, D:2 * D], c.ident[:, :], a12[u][:, 1, :], start=False,
                              stop=True).then_inc(s["r"], 1)
                elif kind == "o":
                    pe.wait_ge(s["qc"], g + 1)
                    pe.wait_ge(s["kvm"], g + 1)
                    for t in range(TILES):
                        tt = slice(t * 128, (t + 1) * 128)
                        pe.matmul(psQ[u][:, tt], qc[u][:, tt], kvm[u][:, 0, :], start=True, stop=False)
                        pe.matmul(psQ[u][:, tt], qs[u][:, tt], kvm[u][:, 1, :], start=False, stop=True)
                        last = pe.matmul(psK[u][:, 1, tt], qp[u][:, tt], kmm[u][:, :], start=True, stop=True)
                    last.then_inc(s["o"], 1)
                else:
                    pe.wait_ge(s["yn"], g + 1)
                    for t in range(TILES):
                        last = pe.transpose(psA[u][:, t * 128:(t + 1) * 128], yn[u][:, t, :], c.ident[:, :])
                    last.then_inc(s["t"], 1)
            pe.wait_ge(s["b3"], 1)
            layers(pe, "pe", step)

        @block.scalar
        def _(act):
            def step(kind, b, g, layer):
                u = b % UN
                if kind == "hs":
                    wait(act, s["x"], g - 1)
                    wait(act, s["kv"], g - 1)
                    wait(act, s["q"], g - 1)
                    wait(act, s["h"], g - 3)
                    act.activation(hs[u][:, :], c.H[:, b * N:(b + 1) * N], ACT.Copy).then_inc(s["hs"], 1)
                elif kind == "qg":
                    wait(act, s["o"], g - 1)
                    c.wait_apart(act, s["q"], g + 1)
                    act.activation(qg[u][:, :], psQ[u][:, :], ACT.Gelu,
                                   bias=lcols[:, 0, ds(layer, 1)]).then_inc(s["qg"], 1)
                elif kind == "kg":
                    wait(act, s["a"], g - 1)
                    act.wait_ge(s["kv"], g + 1)
                    for j in range(2):
                        pk = psK[u][:, j, :].rearrange("p (t k c) -> p t k c", t=2, k=2)
                        last = act.activation(kg[u][:, 2 * j:2 * j + 2, :], pk[:, :, 0, :], ACT.Gelu)
                    last.then_inc(s["kg"], 1)
                elif kind == "v":
                    wait(act, s["a"], g - 1)
                    act.wait_ge(s["kv"], g + 1)
                    for j in range(2):
                        pk = psK[u][:, j, :].rearrange("p (t k c) -> p t k c", t=2, k=2)
                        last = act.activation(vv[u][:, 2 * j:2 * j + 2, :], pk[:, :, 1, :], ACT.Copy)
                    last.then_inc(s["v"], 1)
                elif kind == "a12":
                    wait(act, s["kvm"], g - 1)
                    act.wait_ge(s["a"], g + 1)
                    act.activation(a12[u][:, :, :], psA[u][:, 0:3 * D].rearrange("p (j c) -> p j c", j=3),
                                   ACT.Copy).then_inc(s["a12"], 1)
                else:
                    c.wait_apart(act, s["t"], g + 1)
                    act.activation(c.H[:, b * N:(b + 1) * N], psA[u][:, :], ACT.Identity,
                                   bias=lcols[:, 2, ds(layer, 1)], scale=lcols[:, 1, ds(layer, 1)]).then_inc(s["h"], 1)
            act.wait_ge(s["c"], 32)
            layers(act, "act", step)

        @block.vector
        def _(dve):
            def step(kind, b, g, layer):
                u = b % UN
                if kind == "kc":
                    kk = kg[u][:, :, :]
                    ch = Chain(dve, s_k, 1, g)
                    dve.wait_ge(s["kg"], g + 1)
                    wait(dve, s["a"], g - 1)
                    ch.inc(dve.scalar_tensor_tensor(out=kc[u][:, :, :], in0=kk, scalar=0.21, in1=c.cos_tok[:, :, :],
                                                    op0=ALU.add, op1=ALU.mult))
                    dve.scalar_tensor_tensor(out=ks[u][:, :, :], in0=kk, scalar=0.21, in1=c.sin_tok[:, :, :],
                                             op0=ALU.add, op1=ALU.mult).then_inc(s["kc"], 1)
                elif kind == "qc":
                    ch = Chain(dve, s_q, 2, g)
                    dve.wait_ge(s["qg"], g + 1)
                    wait(dve, s["o"], g - 1)
                    ch.inc(dve.tensor_scalar(qp[u][:, :], qg[u][:, :], 0.21, None, ALU.add))
                    ch.inc(dve.scalar_tensor_tensor(out=qc[u][:, :], in0=qg[u][:, :], scalar=0.21, in1=c.cos_feat[:, :],
                                                    op0=ALU.add, op1=ALU.mult))
                    dve.scalar_tensor_tensor(out=qs[u][:, :], in0=qg[u][:, :], scalar=0.21, in1=c.sin_feat[:, :],
                                             op0=ALU.add, op1=ALU.mult).then_inc(s["qc"], 1)
                elif kind == "kmm":
                    dve.wait_ge(s["a12"], g + 1)
                    wait(dve, s["o"], g - 1)
                    dve.scalar_tensor_tensor(out=kmm[u][:, :], in0=a12[u][:, 2, :], scalar=0.21,
                                             in1=c.headmask[:, 0, :], op0=ALU.add, op1=ALU.mult).then_inc(s["kmm"], 1)
                elif kind == "kvm":
                    dve.wait_ge(s["r"], g + 1)
                    dve.scalar_tensor_tensor(out=kvm[u][:, :, :], in0=psA[u][:, 0:2 * D].rearrange(
                        "p (j c) -> p j c", j=2), scalar=1.0 / N, in1=c.headmask[:, :, :],
                        op0=ALU.mult, op1=ALU.mult).then_inc(s["kvm"], 1)
                elif kind == "y":
                    ch = Chain(dve, s_y, 3, g)
                    dve.wait_ge(s["o"], g + 1)
                    wait(dve, s["yn"], g - 1)
                    den = psK[u][:, 1, :].rearrange("p (h e) -> p h e", e=HD)[:, :, 0]
                    ch.link(dve.tensor_scalar(z[u][:, :], den, 1e-6, None, ALU.add))
                    ch.link(dve.reciprocal(z[u][:, :], z[u][:, :]))
                    o3 = psQ[u][:, :].rearrange("p (h e) -> p h e", e=HD)
                    y3 = y[u][:, :, :].rearrange("p t (h e) -> p (t h) e", e=HD)
                    ch.link(dve.tensor_tensor(y3, o3, z[u][:, :].unsqueeze(2).to_broadcast([128, TILES * NH, HD]),
                                              ALU.mult))
                    dve.wait_ge(s["x"], g + 1)
                    dve.tensor_tensor(y[u][:, :, :], y[u][:, :, :],
                                      psK[u][:, 0, :].rearrange("p (t c) -> p t c", t=TILES), ALU.add).then_inc(s["y"], 1)
                else:
                    ch = Chain(dve, s_n, 23, g)
                    dve.wait_ge(s["y"], g + 1)
                    wait(dve, s["t"], g - 1)
                    norm_tokens(c, dve, ch, yn[u], y[u], stats[u], mv[u], rs[u], 1e-12).then_inc(s["yn"], 1)
                    ch.end()
            ch = Chain(dve, s_bias)
            dve.wait_ge(s["c"], 32)
            ch.inc(dve.tensor_copy(ones3[:, :], c.ones[0:3, :]))
            src = bias
            for n in range(3):
                ch.link(dve.tensor_copy(part[:, n, :], src[:, :]))
                if n < 2:
                    ch.link(dve.tensor_tensor(rest[:, :], src[:, :], part[:, n, :], ALU.subtract))
                    src = rest
            ch.link(dve.tensor_scalar(bias3[:, :], part[:, 0, :], c.ident[0:3, 0:1], None, ALU.mult))
            for n in (1, 2):
                last = dve.scalar_tensor_tensor(out=bias3[:, :], in0=part[:, n, :], scalar=c.ident[0:3, n:n + 1],
                                                in1=bias3[:, :], op0=ALU.mult, op1=ALU.add)
                if n == 1:
                    ch.link(last)
            last.then_inc(s["b3"], 1)
            layers(dve, "dve", step)


def experts(c):
    nc = c.nc
    E, TOPK, C, NT = 16, 4, 4, T // 128
    w1 = [c.sb(f"e_w1_{u}", [D, C * D]) for u in range(2)]
    w2 = [c.sb(f"e_w2_{u}", [D, C, D]) for u in range(2)]
    b1 = [c.sb(f"e_b1_{u}", [D, C]) for u in range(2)]
    b2 = c.sb("e_b2", [E, D])
    keys = c.sb("e_keys", [D, 2, E])
    rbias = c.sb("e_rb", [1, E])
    kr = c.sb("e_kr", [D, E])
    ksq = c.sb("e_ksq", [D, E])
    crow = c.sb("e_crow", [128, E])
    nones = c.sb("e_nones", [D, D])
    hst = [c.sb(f"e_hst{u}", [D, N]) for u in range(2)]
    hsq = [c.sb(f"e_hsq{u}", [D, N]) for u in range(2)]
    lg = c.sb("e_lg", [128, NT, E])
    m8 = c.sb("e_m8", [128, NT, 8])
    gt = c.sb("e_gt", [128, NT, E])
    eq = c.sb("e_eq", [128, NT, E])
    run = c.sb("e_run", [128, NT, E])
    zero = c.sb("e_zero", [128, E])
    left = c.sb("e_left", [128, NT])
    gate = c.sb("e_gate", [128, NT, E])
    gT = c.sb("e_gT", [E, 4, 128])
    acc = c.sb("e_acc", [128, NT, D])
    hh = [c.sb(f"e_hh{j}", [D, C, N]) for j in range(2)]
    psH = [c.ps(f"e_psH{j}") for j in range(4)]
    psY = [c.ps(f"e_psY{j}") for j in range(2)]
    psR = [c.ps(f"e_psR{j}") for j in range(2)]
    s = {k: c.sem("e_s_" + k) for k in ("w", "we0", "we1", "k", "crow", "hst", "hsq", "l", "lg", "gate", "gt", "gTe", "b2", "acc0",
                                        "h", "hh", "y", "acc", "tr", "x", "ksq", "tab")}
    s_ch, s_act = c.sem("e_s_dve"), c.sem("e_s_act")
    with nc.Block() as block:
        @block.sync
        def _(sp):
            sp.dma_start(keys[:, :, :], c.ins["keys_rw"]).then_inc(s["w"], 16)
            sp.dma_start(rbias[:, :], c.ins["rb"]).then_inc(s["w"], 16)
            sp.dma_start(b2[:, :], c.ins["b2_moe"]).then_inc(s["w"], 16)
            sp.dma_start(c.tables_1, c.ins["tables_1_in"]).then_inc(s["tab"], 16)

            def load_pair(ep):
                for u in range(2):
                    e = ep * 2 + u
                    wait(sp, s["y"], (ep * 2 + u - 1) * NB)
                    sp.dma_start(w1[u][:, :], c.ins["w1_moe"][e]).then_inc(s[f"we{u}"], 16)
                    sp.dma_start(w2[u][:, :, :], c.ins["w2_moe"][e]).then_inc(s[f"we{u}"], 16)
                    sp.dma_start(b1[u][:, :], c.ins["b1_moe"][e]).then_inc(s[f"we{u}"], 16)
            load_pair(0)
            with sp.Fori(1, E // 2) as ep:
                load_pair(ep)
            sp.wait_ge(s["tab"], 16)

        @block.tensor
        def _(pe):
            pe.wait_ge(s["k"], 1)
            pe.matmul(psR[0][:, 0:E], nones[:, :], ksq[:, :], start=True, stop=False)
            pe.matmul(psR[0][:, 0:E], c.ones[0:1, :], rbias[:, :], start=False, stop=True).then_inc(s["crow"], 1)
            for b in range(NB):
                u = b % 2
                pe.wait_ge(s["hsq"], b + 1)
                wait(pe, s["lg"], b - 1)
                if b == 0:
                    pe.wait_ge(s["ksq"], 1)
                for t in range(TILES):
                    tt = slice(128 * t, 128 * t + 128)
                    o = psR[u][:, E * t:E * t + E]
                    pe.matmul(o, hst[u][:, tt], kr[:, :], start=True, stop=False)
                    last = pe.matmul(o, hsq[u][:, tt], nones[:, 0:E], start=False, stop=True)
                last.then_inc(s["l"], 1)
            pe.wait_ge(s["gate"], 1)
            for b in range(NB):
                wait(pe, s["gTe"], b)
                wait(pe, s["acc0"], b - 1)
                for t in range(TILES):
                    last = pe.transpose(psR[0][0:E, 128 * t:128 * t + 128], gate[:, b * TILES + t, :], c.ident[:, :])
                last.then_inc(s["gt"], 1)
                pe.wait_ge(s["gTe"], b + 1)
                wait(pe, s["acc0"], b)
                for t in range(TILES):
                    last = pe.matmul(psR[1][:, 128 * t:128 * t + 128], gT[:, t, :], b2[:, :], start=True, stop=True)
                last.then_inc(s["b2"], 1)
            def hidden(ep, u, b, n):
                if b == 0:
                    wait(pe, s[f"we{u}"], (ep + 1) * 48)
                for j in range(C):
                    wait(pe, s["hh"], n * C + j - 3)
                    pe.matmul(psH[j][:, :], w1[u][:, j * D:(j + 1) * D], c.H[:, b * N:(b + 1) * N], start=True,
                              stop=True).then_inc(s["h"], 1)

            def outputs(u, b, n):
                wait(pe, s["hh"], n * C + C)
                wait(pe, s["acc"], n - 1)
                for t in range(TILES):
                    for j in range(C):
                        last = pe.matmul(psY[b % 2][:, 128 * t:128 * t + 128], hh[b % 2][:, j, 128 * t:128 * t + 128],
                                         w2[u][:, j, :], start=(j == 0), stop=(j == C - 1))
                last.then_inc(s["y"], 1)

            def expert_pair(ep):
                for u in range(2):
                    for b in range(NB):
                        n = (ep * 2 + u) * NB + b
                        hidden(ep, u, b, n)
                        if not (isinstance(n, int) and n == 0):
                            outputs((n2 := (u * NB + b - 1) % 8) // NB, (b - 1) % NB, n - 1)
            expert_pair(0)
            with pe.Fori(1, E // 2) as ep:
                expert_pair(ep)
            outputs(1, NB - 1, E * NB - 1)
            for b in range(NB):
                wait(pe, s["acc"], E * NB)
                wait(pe, s["x"], b - 1)
                for t in range(TILES):
                    last = pe.transpose(psR[b % 2][:, 128 * t:128 * t + 128], acc[:, b * TILES + t, :], c.ident[:, :])
                last.then_inc(s["tr"], 1)

        @block.scalar
        def _(act):
            for b in range(NB):
                wait(act, s["l"], b - 1)
                act.activation(hst[b % 2][:, :], c.H[:, b * N:(b + 1) * N], ACT.Copy).then_inc(s["hst"], 1)
                act.activation(hsq[b % 2][:, :], c.H[:, b * N:(b + 1) * N], ACT.Square).then_inc(s["hsq"], 1)
            act.wait_ge(s["lg"], NB + 1)
            act.activation(gate[:, :, :], lg[:, :, :], ACT.Exp).then_inc(s_act, 1)
            for b in range(NB):
                act.wait_ge(s["gt"], b + 1)
                wait(act, s["b2"], b)
                act.activation(gT[:, :, :], psR[0][0:E, :].rearrange("e (t p) -> e t p", t=TILES),
                               ACT.Copy).then_inc(s["gTe"], 1)

            def expert_pair(ep):
                for u in range(2):
                    for b in range(NB):
                        n = (ep * 2 + u) * NB + b
                        wait(act, s["y"], n - 1)
                        for j in range(C):
                            act.wait_ge(s["h"], n * C + j + 1)
                            act.activation(hh[b % 2][:, j, :], psH[j][:, :], ACT.Gelu, bias=b1[u][:, j:j + 1]).then_inc(s["hh"], 1)
            expert_pair(0)
            with act.Fori(1, E // 2) as ep:
                expert_pair(ep)

        @block.vector
        def _(dve):
            ch = Chain(dve, s_ch)
            dve.wait_ge(s["w"], 48)
            ch.inc(dve.memset(nones[:, :], -1.0))
            ch.inc(dve.memset(zero[:, :], 0.0))
            ch.inc(dve.scalar_tensor_tensor(out=kr[:, :], in0=keys[:, 0, :], scalar=2.0, in1=keys[:, 1, :], op0=ALU.mult,
                                            op1=ALU.add))
            dve.tensor_tensor(ksq[:, :], keys[:, 0, :], keys[:, 0, :], ALU.mult).then_inc(s["k"], 1)
            dve.wait_ge(s["crow"], 1)
            dve.tensor_copy(crow[:, :], psR[0][:, 0:E]).then_inc(s["ksq"], 1)
            dve.wait_ge(s["ksq"], 1)
            for b in range(NB):
                dve.wait_ge(s["l"], b + 1)
                dve.tensor_tensor(lg[:, b * TILES:(b + 1) * TILES, :],
                                  psR[b % 2][:, 0:TILES * E].rearrange("p (t e) -> p t e", e=E),
                                  crow[:, :].unsqueeze(1).to_broadcast([128, TILES, E]), ALU.add).then_inc(s["lg"], 1)
            wait(dve, s["lg"], NB)
            for t in range(NT):
                m = ch.inc(dve.max(m8[:, t, :], lg[:, t, :]))
            ch.wait(m)
            kth = m8[:, :, TOPK - 1].unsqueeze(2).to_broadcast([128, NT, E])
            ch.inc(dve.tensor_tensor(gt[:, :, :], lg[:, :, :], kth, ALU.is_gt))
            ch.link(dve.tensor_tensor(eq[:, :, :], lg[:, :, :], kth, ALU.is_equal))
            ch.link(dve.tensor_reduce(left[:, :], gt[:, :, :], AX_X, ALU.add))
            ch.link(dve.tensor_scalar(left[:, :], left[:, :], -1.0, float(TOPK), ALU.mult, ALU.add))
            for t in range(NT):
                m = ch.inc(dve.tensor_tensor_scan(run[:, t, :], eq[:, t, :], zero[:, :], 0.0, ALU.add, ALU.add))
            ch.wait(m)
            ch.link(dve.tensor_tensor(run[:, :, :], run[:, :, :], left[:, :].unsqueeze(2).to_broadcast([128, NT, E]),
                                      ALU.is_le))
            ch.link(dve.tensor_tensor(run[:, :, :], run[:, :, :], eq[:, :, :], ALU.mult))
            ch.link(dve.tensor_tensor(gt[:, :, :], gt[:, :, :], run[:, :, :], ALU.add))
            dve.tensor_tensor(lg[:, :, :], lg[:, :, :], m8[:, :, 0].unsqueeze(2).to_broadcast([128, NT, E]),
                              ALU.subtract).then_inc(s["lg"], 1)
            dve.wait_ge(s_act, 1)
            ch.link(dve.tensor_tensor(gate[:, :, :], gate[:, :, :], gt[:, :, :], ALU.mult))
            ch.link(dve.tensor_reduce(left[:, :], gate[:, :, :], AX_X, ALU.add))
            ch.link(dve.reciprocal(left[:, :], left[:, :]))
            dve.tensor_tensor(gate[:, :, :], gate[:, :, :], left[:, :].unsqueeze(2).to_broadcast([128, NT, E]),
                              ALU.mult).then_inc(s["gate"], 1)
            for b in range(NB):
                dve.wait_ge(s["b2"], b + 1)
                dve.tensor_copy(acc[:, b * TILES:(b + 1) * TILES, :],
                                psR[1][:, :].rearrange("p (t c) -> p t c", t=TILES)).then_inc(s["acc0"], 1)
            wait(dve, s["acc0"], NB)
            dve.wait_ge(s["gate"], 1)

            def expert_pair(ep):
                for u in range(2):
                    for b in range(NB):
                        e = ep * 2 + u
                        n = e * NB + b
                        dve.wait_ge(s["y"], n + 1)
                        wait(dve, s["acc"], n - 3)
                        for t in range(TILES):
                            a = acc[:, b * TILES + t, :]
                            last = dve.scalar_tensor_tensor(out=a, in0=psY[b % 2][:, 128 * t:128 * t + 128],
                                                            scalar=gate[:, b * TILES + t, ds(e, 1)], in1=a,
                                                            op0=ALU.mult, op1=ALU.add)
                        last.then_inc(s["acc"], 1)
            expert_pair(0)
            with dve.Fori(1, E // 2) as ep:
                expert_pair(ep)
            for b in range(NB):
                dve.wait_ge(s["tr"], b + 1)
                dve.scalar_tensor_tensor(out=c.X[:, b * N:(b + 1) * N], in0=psR[b % 2][:, :],
                                         scalar=c.mods[:, 0, 5, b:b + 1], in1=c.X[:, b * N:(b + 1) * N],
                                         op0=ALU.mult, op1=ALU.add).then_inc(s["x"], 1)


def causal_attention(c):
    nc = c.nc
    DQ, UN = 32, 2
    LOWEST = float(np.finfo(np.float32).min)
    wqk = c.sb("a_wqk", [D, 2, DQ])
    wvd = c.sb("a_wvd", [DQ, D])
    wvu = c.sb("a_wvu", [DQ, D])
    wv = c.sb("a_wv", [D, D])
    hst = [c.sb(f"a_hst{u}", [D, N]) for u in range(UN)]
    qk = [c.sb(f"a_qk{u}", [DQ, 2, N]) for u in range(UN)]
    v = [c.sb(f"a_v{u}", [128, TILES, D]) for u in range(UN)]
    sc = [c.sb(f"a_sc{u}", [128, N]) for u in range(UN)]
    zz = [c.sb(f"a_zz{u}", [128, N]) for u in range(UN)]
    pr = [c.sb(f"a_pr{u}", [128, N]) for u in range(UN)]
    pT = [c.sb(f"a_pT{u}", [128, TILES, 128]) for u in range(UN)]
    mx = [c.sb(f"a_mx{u}", [128, 1]) for u in range(UN)]
    sm = [c.sb(f"a_sm{u}", [128, 1]) for u in range(UN)]
    psA = [c.ps(f"a_psA{u}") for u in range(UN)]
    psS = [c.ps(f"a_psS{u}") for u in range(UN)]
    psT = [c.ps(f"a_psT{u}") for u in range(UN)]
    psO = [c.ps(f"a_psO{u}") for u in range(UN)]
    s = {k: c.sem("a_s_" + k) for k in ("w", "wv", "wve", "h", "qk", "qke", "v", "ve", "sc", "z", "mx", "e", "pr", "t", "te",
                                        "o", "x")}
    s_ch = c.sem("a_s_dve")
    with nc.Block() as block:
        @block.sync
        def _(sp):
            sp.dma_start(wqk[:, :, :], c.ins["w_qk1"]).then_inc(s["w"], 16)
            sp.dma_start(wvd[:, :], c.ins["w_vdT"]).then_inc(s["w"], 16)
            sp.dma_start(wvu[:, :], c.ins["w_vu"]).then_inc(s["w"], 16)

        @block.tensor
        def _(pe):
            pe.wait_ge(s["w"], 48)
            pe.matmul(psA[0][:, 0:D], wvd[:, :], wvu[:, :], start=True, stop=True).then_inc(s["wv"], 1)
            pe.wait_ge(s["wve"], 1)
            for pair in range(NB // UN):
                it = pair * UN
                for j in range(2):
                    for u in range(UN):
                        pe.wait_ge(s["h"], it + u + 1)
                        if j == 0:
                            wait(pe, s["ve"], it)
                        else:
                            wait(pe, s["qke"], 2 * (it + u) + 1 - u)
                            pe.wait_ge(s["qke"], 2 * it + 1 + u)
                        pe.matmul(psA[u][0:DQ, :], wqk[:, j, :], hst[u][:, :], start=True, stop=True).then_inc(s["qk"], 1)
                for u in range(UN):
                    pe.wait_ge(s["qke"], 2 * it + 3 + u)
                    for t in range(TILES):
                        last = pe.matmul(psA[u][:, 128 * t:128 * t + 128], hst[u][:, 128 * t:128 * t + 128], wv[:, :],
                                         start=True, stop=True)
                    last.then_inc(s["v"], 1)
                def attend(t, u):
                    if t == 0:
                        wait(pe, s["x"], it)
                        pe.wait_ge(s["ve"], it + u + 1)
                    pe.wait_ge(s["pr"], it * TILES + UN * t + u + 1)
                    wait(pe, s["te"], it * TILES + UN * t)
                    for k in range(TILES):
                        kk = slice(128 * k, 128 * k + 128)
                        last = pe.transpose(psT[u][:, kk], pr[u][:, kk], c.ident[:, :])
                    last.then_inc(s["t"], 1)
                    pe.wait_ge(s["te"], it * TILES + UN * t + u + 1)
                    for k in range(TILES):
                        last = pe.matmul(psO[u][:, 128 * t:128 * t + 128], v[u][:, k, :], pT[u][:, k, :],
                                         start=(k == 0), stop=(k == TILES - 1))
                    last.then_inc(s["o"], 1)
                for t in range(TILES + 1):
                    for u in range(UN):
                        if t < TILES:
                            wait(pe, s["z"], it * TILES + UN * t)
                            pe.matmul(psS[u][:, :], qk[u][:, 0, 128 * t:128 * t + 128], qk[u][:, 1, :], start=True,
                                      stop=True).then_inc(s["sc"], 1)
                    if t:
                        for u in range(UN):
                            attend(t - 1, u)

        @block.scalar
        def _(act):
            act.wait_ge(s["wv"], 1)
            act.activation(wv[:, :], psA[0][:, 0:D], ACT.Copy).then_inc(s["wve"], 1)
            for pair in range(NB // UN):
                it = pair * UN
                for u in range(UN):
                    wait(act, s["v"], it)
                    act.activation(hst[u][:, :], c.H[:, ds((it + u) * N, N)], ACT.Copy).then_inc(s["h"], 1)
                for j in range(2):
                    for u in range(UN):
                        act.wait_ge(s["qk"], 2 * it + 2 * j + u + 1)
                        wait(act, s["sc"], it * TILES)
                        act.activation(qk[u][:, j, :], psA[u][0:DQ, :], ACT.Copy).then_inc(s["qke"], 1)
                for u in range(UN):
                    act.wait_ge(s["v"], it + u + 1)
                    wait(act, s["o"], it * TILES)
                    act.activation(v[u][:, :, :], psA[u][:, :].rearrange("p (t c) -> p t c", t=TILES),
                                   ACT.Copy).then_inc(s["ve"], 1)
                def evac(t, u):
                    n = it * TILES + UN * t
                    act.wait_ge(s["t"], n + u + 1)
                    wait(act, s["o"], n)
                    act.activation(pT[u][:, :, :], psT[u][:, :].rearrange("p (t c) -> p t c", t=TILES),
                                   ACT.Copy).then_inc(s["te"], 1)
                for t in range(TILES + 1):
                    for u in range(UN):
                        if t:
                            evac(t - 1, u)
                        if t < TILES:
                            n = it * TILES + UN * t
                            act.wait_ge(s["mx"], n + u + 1)
                            wait(act, s["pr"], n)
                            act.activation(pr[u][:, :], sc[u][:, :], ACT.Exp, bias=mx[u][:, :],
                                           accum_out=sm[u][:, :]).then_inc(s["e"], 1)

        @block.vector
        def _(dve):
            for pair in range(NB // UN):
                it = pair * UN
                ch = Chain(dve, s_ch, 32, pair)
                for t in range(TILES):
                    n = it * TILES + UN * t
                    for u in range(UN):
                        dve.wait_ge(s["sc"], n + u + 1)
                        wait(dve, s["e"], n)
                        dve.scalar_tensor_tensor(out=sc[u][:, :], in0=psS[u][:, :], scalar=DQ ** -0.5,
                                                 in1=c.causal[:, t, :], op0=ALU.mult, op1=ALU.mult).then_inc(s["z"], 1)
                        dve.wait_ge(s["z"], n + u + 1)
                        ch.link(dve.tensor_scalar(zz[u][:, :], sc[u][:, :], 0.0, LOWEST, ALU.is_equal, ALU.mult))
                        ch.link(dve.tensor_tensor(sc[u][:, :], sc[u][:, :], zz[u][:, :], ALU.add))
                        ch.link(dve.tensor_reduce(mx[u][:, :], sc[u][:, :], AX_X, ALU.max))
                        dve.tensor_scalar(mx[u][:, :], mx[u][:, :], -1.0, None, ALU.mult).then_inc(s["mx"], 1)
                    for u in range(UN):
                        dve.wait_ge(s["e"], n + u + 1)
                        wait(dve, s["t"], n)
                        ch.link(dve.reciprocal(sm[u][:, :], sm[u][:, :]))
                        dve.tensor_scalar(pr[u][:, :], pr[u][:, :], sm[u][:, :], None, ALU.mult).then_inc(s["pr"], 1)
                for u in range(UN):
                    b = it + u
                    dve.wait_ge(s["o"], it * TILES + UN * (TILES - 1) + u + 1)
                    dve.scalar_tensor_tensor(out=c.X[:, ds(b * N, N)], in0=psO[u][:, :], scalar=c.mods[:, 1, 2, ds(b, 1)],
                                             in1=c.X[:, ds(b * N, N)], op0=ALU.mult, op1=ALU.add).then_inc(s["x"], 1)
                ch.end()


def finish(c, out):
    s_y, s_o = c.sem("o_s_y"), c.sem("o_s_out")
    with c.nc.Block() as block:
        @block.vector
        def _(dve):
            for b in range(NB):
                bb = slice(b * N, (b + 1) * N)
                dve.scalar_tensor_tensor(out=c.X[:, bb], in0=c.H[:, bb], scalar=c.mods[:, 1, 5, b:b + 1], in1=c.X[:, bb],
                                         op0=ALU.mult, op1=ALU.add).then_inc(s_y, 1)

        @block.sync
        def _(sp):
            for b in range(NB):
                sp.wait_ge(s_y, b + 1)
                sp.dma_start(out[:, b * N:(b + 1) * N], c.X[:, b * N:(b + 1) * N]).then_inc(s_o, 16)
            wait(sp, s_o, 16 * NB)


def windowed_layers(c):
    nc = c.nc
    DEPTH, HEADS, DH, WIN = 6, 16, 64, 32
    PAIRS, BLK = HEADS // 2, 64
    KEYS = WIN + BLK
    NBLK = N // BLK
    FF = 341
    CH = [(0, 128), (128, 128), (256, FF - 256)]
    ROUNDS = DEPTH * NB
    QKV = 3 * HEADS * DH
    UP, UT, UA = 24, 16, 2 * NBLK

    w_qkv = c.sb("w_qkv", [D, 2, QKV])
    w_o = c.sb("w_o", [D, PAIRS, D])
    w_1 = c.sb("w_1", [D, 2 * FF])
    w_2 = c.sb("w_2", [D, 3, D])
    cols = c.sb("w_cols", [D, 9])
    xs = c.sb("w_xs", [D, N])
    raw = [c.sb(f"w_raw{j}", [128, 4, 512]) for j in range(2)]
    sq = c.sb("w_sq", [128, 4, 512])
    qr = c.sb("w_qr", [128, 4, 512])
    t2 = c.sb("w_t2", [128, 512])
    nrm = [c.sb(f"w_nrm{j}", [128, 4, 32]) for j in range(2)]
    qb = [c.sb(f"w_qb{j}", [128, PAIRS, 2, 2, BLK]) for j in range(2)]
    kT = c.sb("w_kT", [128, PAIRS, WIN + N])
    v = [c.tables_1[:, 1024 * t:1024 * (t + 1)] for t in range(3)] + [c.sb("w_v3", [128, HEADS * DH])]
    v_even = c.sb("w_v_even", [KEYS, HEADS * DH])
    pb = [c.sb(f"w_pb{j}", [128, PAIRS, KEYS + WIN * j]) for j in range(2)]
    mx = c.sb("w_mx", [128, PAIRS])
    sm = [c.sb(f"w_sm{j}", [128, PAIRS]) for j in range(2)]
    pT = c.sb("w_pT", [128, PAIRS, 128])
    oT = c.sb("w_oT", [128, PAIRS, N])
    xsf = c.sb("w_xsf", [D, N])
    yn = c.sb("w_yn", [128, TILES, D])
    xn = c.sb("w_xn", [D, N])
    gg = yn[:, :, :].rearrange("p t c -> p (t c)")
    hh = c.sb("w_hh", [D, 3, N])
    stats = c.sb("w_stats", [128, TILES, 6])
    mv = c.sb("w_mv", [128, TILES, 2])
    rs = c.sb("w_rs", [128, 3, TILES])
    tabs = c.sb("w_tabs", [128, DEPTH, 4, TILES, DH])
    scl = sq[:, 0:3, :].rearrange("p a b -> p (a b)").rearrange("p (l k d) -> p l k d", l=DEPTH, k=4)

    psP = [c.ps(f"w_psP{j}") for j in range(2)]
    psT = c.ps("w_psT")
    psA = c.ps("w_psA")
    psS = [c.ps(f"w_psS{j}") for j in range(2)]
    psO = c.ps("w_psO")
    psF = c.ps("w_psF")

    names = ("wa", "wf", "tab", "z", "xs", "p", "pe", "sr", "rn", "t1", "qr", "t", "te", "s", "x1", "e", "r", "pn", "pt",
             "pte", "ve", "av", "ot", "f", "xf", "xsf", "yn", "xn", "gg", "hh", "out", "scl")
    s = {k: c.sem("w_s_" + k) for k in names}
    s_norm, s_max, s_sum, s_f, s_pool = (c.sem("w_s_chain_" + k) for k in ("norm", "max", "sum", "tail", "pool"))

    def proj_use(kind, t, j):
        return 6 * t + (j if kind == "P" else 4 + j)

    ORDER = {
        "pe": """P2.0 At7.0- P2.1 S0.0 At7.1- P2.2 Av7.0- T1.0 S0.1 P2.3 S1.0 Av7.1- S1.1 V2.0 V2.1 P3.0
            At0.0 T1.1 wo0- T1.2 P3.1 T1.3 At0.1 wo1- S2.0 P3.2 S2.1 T2.0 Av0.0 P3.3 tr- At1.0 Av0.1
            T2.1 S3.0 S3.1 T2.2 At1.1 V3.0 Av1.0 Av1.1 At2.0 back- T2.3 At2.1 V3.1 Av2.0 S4.0 P0.0+
            P0.1+ S4.1 Av2.1 g0- At3.0 S5.0 P0.2+ At3.1 P0.3+ T3.0 Av3.0 a0- S5.1 T3.1 V0.0+ g1- At4.0
            a1- V0.1+ T3.2 Av3.1 g2- Av4.0 At4.1 T3.3 P1.0+ a2- S6.0 P1.1+ S6.1 Av4.1 At5.0 S7.0 At5.1
            P1.2+ P1.3+ T0.0+ V1.0+ S7.1 Av5.0 T0.1+ At6.0 Av5.1 w2- V1.1+ T0.2+ At6.1 Av6.0 T0.3+ Av6.1""",
        "act": """At7.0- P2.0 P2.1 At7.1- T1.0 Xb0.0 P2.2 P2.3 V2.0 Av7.1- T1.1 V2.1 At0.0 T1.2 Xb1.0 P3.0
            At0.1 T1.3 P3.1 tr- P3.2 Xb2.0 T2.0 P3.3 T2.1 At1.0 At1.1 Av0.1 T2.2 V3.0 Av1.1 At2.0 At2.1
            V3.1 T2.3 stage+ Xb3.0 P0.0+ back- Av2.1 At3.0 P0.1+ Xb4.0 g0- P0.2+ T3.0 At3.1 P0.3+ T3.1
            g1- V0.0+ V0.1+ At4.0 T3.2 Av3.1 g2- Xb5.0 T3.3 P1.0+ At4.1 P1.1+ At5.0 Xb6.0 At5.1 Av4.1
            P1.2+ P1.3+ T0.0+ Av5.1 Xb7.0 T0.1+ At6.0 T0.2+ V1.0+ At6.1 T0.3+ Av6.1 V1.1+""",
        "dve": """Rs2.0 Xa0.0 Rb1.2 Xa0.1 Rs2.1 Xa1.0 Xb0.0 Xa1.1 Rs2.2 Rs2.3 Rb1.3 Ra2.0 Rb2.0 Rb2.1 Rb2.2
            Rs3.0 Xb1.0 wo- Rs3.1 Xa2.0 Xa2.1 Rb2.3 Xb2.0 tr- Rs3.2 Xa3.0 Rs3.3 Xa3.1 Ra3.0 Xb3.0 Rb3.0
            Xa4.0 Xa4.1 Rs0.0+ Rb3.1 Xb4.0 Rb3.2 Xa5.0 a0- Rs0.1+ Rs0.2+ Rb3.3 Rs0.3+ a1- Xa5.1 Ra0.0+
            Rb0.0+ Xb5.0 Xa6.0 Rs1.0+ Xa6.1 Rb0.1+ a2- Rs1.1+ Xb6.0 Xa7.0 Rs1.2+ Rs1.3+ Rb0.2+ Xa7.1
            Rb0.3+ Xb7.0 Ra1.0+ w2- Rb1.0+ Rb1.1+""",
        "pool": """Rb1.2 Xb0.0 Rb1.3 Rb2.0 Xb1.0 Rb2.1 Rb2.2 Rb2.3 Xb2.0 Xb3.0 Rb3.0 Rb3.1 Xb4.0 Rb3.2 Rb3.3
            Xb5.0 Rb0.0+ Rb0.1+ Xb6.0 Rb0.2+ Rb0.3+ Xb7.0 Rb1.0+ Rb1.1+""",
    }

    def unit(word):
        dr = {"+": 1, "-": -1}.get(word[-1], 0)
        word = word.rstrip("+-")
        if "." in word:
            at = next(n for n, ch in enumerate(word) if ch.isdigit() and word[n + 1] == ".")
            return word[:at], int(word[at]), int(word[at + 2]), dr
        return ("stage", 0, 0, dr) if word == "stage" else ("F", word, 0, dr)

    order = {name: [unit(word) for word in text.split()] for name, text in ORDER.items()}

    def turns(eng, name, step):
        def turn(i):
            for kind, k, j, dr in order[name]:
                r = i + dr
                if not isinstance(i, int) or 0 <= r < ROUNDS:
                    step(kind, k, j, r, r % NB, r // NB)
        for i in range(-1, 2):
            turn(i)
        with eng.Fori(2, ROUNDS - 1) as i:
            turn(i)
        turn(ROUNDS - 1)
        turn(ROUNDS)

    with nc.Block() as block:
        @block.sync
        def _(sp):
            sp.dma_start(sq[:, 0:3, :].rearrange("p a b -> p (a b)"),
                         c.ins["qk_scales"].to_broadcast([128, DEPTH * 4 * DH])).then_inc(s["scl"], 16)

            def load_qkv(layer):
                c.wait_apart(sp, s["p"], (layer - 1) * (NB * UP))
                sp.dma_start(w_qkv[:, ds(layer % 2, 1), :], c.ins["w_qkv1"][layer]).then_inc(s["wa"], 16)

            def load_tail(layer):
                c.wait_apart(sp, s["out"], layer * NB)
                sp.dma_start(w_o[:, :, :], c.ins["w_o1"][layer]).then_inc(s["wf"], 16)
                sp.dma_start(w_1[:, :], c.ins["w_ff1"][layer]).then_inc(s["wf"], 16)
                sp.dma_start(w_2[:, :, :], c.ins["w_ff2"][layer]).then_inc(s["wf"], 16)
                sp.dma_start(cols[:, :], c.ins["cols_w"][layer]).then_inc(s["wf"], 16)

            def rounds_of(layer, more):
                for b in range(NB):
                    r = layer * NB + b
                    for t in range(TILES):
                        c.wait_apart(sp, s["pe"], r * UP + proj_use("V", t, 1) + 1)
                        c.wait_apart(sp, s["av"], r * UA + 4 * t - 2)
                        sp.dma_start(v_even[WIN:KEYS, :], v[t][0:BLK, :]).then_inc(s["ve"], 16)
                        if t:
                            sp.dma_start(v_even[0:WIN, :], v[t - 1][128 - WIN:128, :]).then_inc(s["ve"], 16)
                    if b == 0:
                        if more:
                            load_qkv(layer + 1)
                        if not isinstance(layer, int) or layer > 0:
                            load_tail(layer)
            load_qkv(0)
            load_tail(0)
            sp.wait_ge(s["z"], 3)
            rounds_of(0, True)
            with sp.Fori(1, DEPTH - 1) as layer:
                rounds_of(layer, True)
            rounds_of(DEPTH - 1, False)

        VE = 16 * (2 * TILES - 1)

        def mm_tail(pe, f, r, layer):
            if f[:2] == "wo":
                half = int(f[2])
                if half == 0:
                    pe.wait_ge(s["wf"], (layer + 1) * 64)
                    pe.wait_ge(s["ot"], (r + 1) * NBLK)
                    wait(pe, s["out"], r)
                for pair in range(4 * half, 4 * half + 4):
                    last = pe.matmul(psF[:, :], w_o[:, pair, :], oT[:, pair, :], start=(pair == 0),
                                     stop=(pair == PAIRS - 1), skip_group_check=True)
                if half == 0:
                    return
            elif f == "tr":
                pe.wait_ge(s["xsf"], r + 1)
                for t in range(TILES):
                    last = pe.transpose(psF[:, 128 * t:128 * (t + 1)], xsf[:, 128 * t:128 * (t + 1)], c.ident[:, :])
            elif f == "back":
                pe.wait_ge(s["yn"], r + 1)
                for t in range(TILES):
                    last = pe.transpose(psF[:, 128 * t:128 * (t + 1)], yn[:, t, :], c.ident[:, :])
            elif f[0] in "ga":
                k = int(f[1])
                at, m = CH[k]
                if f[0] == "g":
                    pe.wait_ge(s["xn"], r + 1)
                    wait(pe, s["hh"], 3 * r + k)
                    at += FF
                else:
                    pe.wait_ge(s["gg"], 3 * r + k + 1)
                last = pe.matmul(psF[0:m, :], w_1[:, at:at + m], xn[:, :], start=True, stop=True)
            else:
                pe.wait_ge(s["hh"], 3 * r + 3)
                for k, (at, m) in enumerate(CH):
                    last = pe.matmul(psF[:, :], w_2[0:m, k, :], hh[0:m, k, :], start=(k == 0), stop=(k == 2))
            last.then_inc(s["f"], 1)

        @block.tensor
        def _(pe):
            def step(kind, k, j, r, b, layer):
                if kind in "PV":
                    u = proj_use(kind, k, j)
                    if u == 0:
                        pe.wait_ge(s["wa"], (layer + 1) * 16)
                        pe.wait_ge(s["xs"], r + 1)
                    wait(pe, s["pe"], r * UP + u - 1)
                    at = 512 * (j if kind == "P" else 4 + j)
                    pe.matmul(psP[u % 2][:, :], xs[:, 128 * k:128 * (k + 1)],
                              w_qkv[:, ds(layer % 2, 1), at:at + 512], start=True, stop=True).then_inc(s["p"], 1)
                elif kind == "T":
                    wait(pe, s["te"], r * UT + 4 * k + j)
                    pe.wait_ge(s["qr"], r * UT + 4 * k + j + 1)
                    for q in range(4):
                        last = pe.transpose(psT[:, 128 * q:128 * (q + 1)], qr[:, j, 128 * q:128 * (q + 1)], c.ident[:, :])
                    last.then_inc(s["t"], 1)
                elif kind == "S":
                    if k % 2 == 0 and j == 0:
                        pe.wait_ge(s["te"], r * UT + 4 * (k // 2) + 4)
                    wait(pe, s["x1"], r * UA + 2 * (k - 1) + j + 1)
                    pe.matmul(psS[j][:, 0:4 * KEYS], c.ident_bf[:, :], c.band_bf[:, min(k, 1), :], start=True, stop=False,
                              skip_group_check=True)
                    for q in range(4):
                        last = pe.matmul(psS[j][:, q * KEYS:(q + 1) * KEYS], qb[(k // 2) % 2][:, 4 * j + q, k % 2, :, :],
                                         kT[:, 4 * j + q, BLK * k:BLK * k + KEYS], start=False, stop=True,
                                         skip_group_check=True)
                    last.then_inc(s["s"], 1)
                elif kind == "At":
                    rows = KEYS + WIN * (k % 2)
                    pe.wait_ge(s["pn"], r * NBLK + k + 1)
                    wait(pe, s["pte"], r * UA + 2 * k + j)
                    for q in range(4):
                        last = pe.transpose(psA[0:rows, 128 * q:128 * (q + 1)], pb[k % 2][:, 4 * j + q, :], c.ident[:, :])
                    last.then_inc(s["pt"], 1)
                elif kind == "Av":
                    t, odd = k // 2, k % 2
                    rows = KEYS + WIN * odd
                    if odd:
                        pe.wait_ge(s["pe"], r * UP + proj_use("V", t, 1) + 1)
                        vals = v[t]
                    else:
                        pe.wait_ge(s["ve"], r * VE + 16 * (2 * t + 1))
                        vals = v_even
                    if j == 0:
                        wait(pe, s["ot"], r * NBLK + k)
                    pe.wait_ge(s["pte"], r * UA + 2 * k + j + 1)
                    for pair in range(4 * j, 4 * j + 4):
                        for h in range(2):
                            last = pe.matmul(psO[64 * h:64 * h + 64, BLK * pair:BLK * (pair + 1)],
                                             vals[0:rows, (2 * pair + h) * DH:(2 * pair + h + 1) * DH],
                                             pT[0:rows, pair, BLK * h:BLK * (h + 1)], start=True, stop=True)
                    last.then_inc(s["av"], 1)
                else:
                    mm_tail(pe, k, r, layer)
            pe.wait_ge(s["z"], 3)
            turns(pe, "pe", step)

        @block.scalar
        def _(act):
            def step(kind, k, j, r, b, layer):
                if kind == "stage":
                    wait(act, s["p"], r * UP)
                    c.wait_apart(act, s["out"], r - 2)
                    act.activation(xs[0:64, :], c.H[0:64, ds(b * N, N)], ACT.Copy)
                    act.activation(xs[64:128, 1:N], c.H[64:128, ds(b * N, N - 1)], ACT.Copy).then_inc(s["xs"], 1)
                elif kind == "P":
                    u = proj_use("P", k, j)
                    wait(act, s["qr"], r * UT + 4 * (k - 2) + j + 1)
                    wait(act, s["sr"], r * UT + 4 * (k - 1) + j + 1)
                    act.wait_ge(s["p"], r * UP + u + 1)
                    act.activation(raw[k % 2][:, j, :], psP[u % 2][:, :], ACT.Copy)
                    act.activation(sq[:, j, :], psP[u % 2][:, :], ACT.Square).then_inc(s["pe"], 1)
                elif kind == "V":
                    u = proj_use("V", k, j)
                    wait(act, s["av"], (r - 1) * UA + 4 * k + 4)
                    if k == TILES - 1:
                        wait(act, s["ve"], r * VE)
                    else:
                        wait(act, s["ve"], (r - 1) * VE + 16 * (2 * k + 3))
                    act.wait_ge(s["p"], r * UP + u + 1)
                    act.activation(v[k][:, 512 * j:512 * (j + 1)], psP[u % 2][:, :], ACT.Copy).then_inc(s["pe"], 1)
                elif kind == "T":
                    act.wait_ge(s["t"], r * UT + 4 * k + j + 1)
                    src = psT[:, :].rearrange("p (a b) -> p a b", a=4)
                    if j < 2:
                        for h in range(2):
                            rows = slice(64 * h, 64 * h + 64)
                            last = act.activation(qb[k % 2][rows, 4 * j:4 * j + 4, :, h, :],
                                                  src[rows].rearrange("p a (b q) -> p a b q", b=2), ACT.Copy)
                    else:
                        last = act.activation(kT[:, 4 * (j - 2):4 * (j - 2) + 4, WIN + 128 * k:WIN + 128 * (k + 1)],
                                              src, ACT.Copy)
                    last.then_inc(s["te"], 1)
                elif kind == "Xb":
                    act.wait_ge(s["x1"], r * UA + 2 * k + 2)
                    p = pb[k % 2][:, :, WIN * (k % 2):]
                    act.activation(p, p, ACT.Exp, scale=8.0).then_inc(s["e"], 1)
                elif kind == "At":
                    rows = KEYS + WIN * (k % 2)
                    wait(act, s["av"], r * UA + 2 * (k - 1) + j + 1)
                    act.wait_ge(s["pt"], r * UA + 2 * k + j + 1)
                    act.activation(pT[0:rows, 4 * j:4 * j + 4, :], psA[0:rows, :].rearrange("p (a b) -> p a b", a=4),
                                   ACT.Copy).then_inc(s["pte"], 1)
                elif kind == "Av":
                    if k == 0:
                        wait(act, s["f"], (r - 1) * 10 + 1)
                    act.wait_ge(s["av"], r * UA + 2 * k + 2)
                    act.activation(oT[:, :, BLK * k:BLK * (k + 1)], psO[:, :].rearrange("p (a b) -> p a b", b=BLK),
                                   ACT.Copy).then_inc(s["ot"], 1)
                elif k == "tr":
                    wait(act, s["yn"], r)
                    c.wait_apart(act, s["xf"], r + 1)
                    act.activation(xsf[0:64, :], c.H[0:64, ds(b * N, N)], ACT.Copy)
                    act.activation(xsf[64:128, 1:N], c.H[64:128, ds(b * N, N - 1)], ACT.Copy).then_inc(s["xsf"], 1)
                elif k == "back":
                    act.wait_ge(s["f"], r * 10 + 3)
                    act.activation(xn[:, :], psF[:, :], ACT.Identity, bias=cols[:, 1:2],
                                   scale=cols[:, 0:1]).then_inc(s["xn"], 1)
                else:
                    n, (at, m) = int(k[1]), CH[int(k[1])]
                    act.wait_ge(s["f"], r * 10 + 4 + 2 * n)
                    wait(act, s["hh"], 3 * r + n)
                    act.activation(gg[0:m, :], psF[0:m, :], ACT.Gelu, bias=cols[0:m, 5 + n:6 + n]).then_inc(s["gg"], 1)
            act.wait_ge(s["tab"], 4 * DEPTH)
            act.wait_ge(s["z"], 1)
            turns(act, "act", step)

        @block.vector
        def _(dve):
            def step(kind, k, j, r, b, layer):
                if kind == "Rs":
                    dve.wait_ge(s["pe"], r * UP + proj_use("P", k, j) + 1)
                    wait(dve, s["rn"], r * UT + 4 * (k - 2) + 4)
                    dve.tensor_reduce(nrm[k % 2][:, 0, 8 * j:8 * j + 8], sq[:, j, :].rearrange(
                        "p (h d) -> p h d", d=DH), AX_X, ALU.add).then_inc(s["sr"], 1)
                elif kind == "Ra":
                    nn = nrm[k % 2]
                    ch = Chain(dve, s_norm, 13, r * TILES + k)
                    dve.wait_ge(s["sr"], r * UT + 4 * k + 4)
                    ch.link(dve.tensor_scalar(nn[:, 0, :], nn[:, 0, :], 1e-24, None, ALU.max))
                    rsqrt(dve, ch, nn[:, 1, :], nn[:, 0, :], nn[:, 2, :], nn[:, 3, :], 0.0)
                    ch.end()
                elif kind == "Rb":
                    u = r * UT + 4 * k + j
                    xv = raw[k % 2][:, j, :].rearrange("p (h d) -> p h d", d=DH)
                    dve.tensor_tensor(xv, xv, nrm[k % 2][:, 1, 8 * j:8 * j + 8].unsqueeze(2).to_broadcast(
                        [128, 8, DH]), ALU.mult).then_inc(s["rn"], 1)
                    dve.wait_ge(s["rn"], u + 1)
                    wait(dve, s["t"], u - 3)
                    tab = tabs[:, ds(layer, 1), 2 * (j // 2), k, :].to_broadcast([128, 8, DH])
                    dve.tensor_tensor(qr[:, j, :].rearrange("p (h d) -> p h d", d=DH), xv, tab,
                                      ALU.mult).then_inc(s["t1"], 1)
                elif kind == "Xa":
                    wait(dve, s["pt"], r * UA + 2 * (k - 2) + 2)
                    ch = Chain(dve, s_max, 1, r * UA + 2 * k + j)
                    half = slice(4 * j, 4 * j + 4)
                    sc = psS[j][:, 0:4 * KEYS].rearrange("p (a b) -> p a b", a=4)
                    dve.wait_ge(s["s"], r * UA + 2 * k + j + 1)
                    ch.link(dve.tensor_reduce(mx[:, half], sc, AX_X, ALU.max))
                    dve.tensor_tensor(pb[k % 2][:, half, WIN * (k % 2):], sc, mx[:, half].unsqueeze(2).to_broadcast(
                        [128, 4, KEYS]), ALU.subtract).then_inc(s["x1"], 1)
                elif kind == "Xb":
                    ch = Chain(dve, s_sum, 1, r * NBLK + k)
                    dve.wait_ge(s["e"], r * NBLK + k + 1)
                    wait(dve, s["pn"], r * NBLK + k - 1)
                    ch.link(dve.tensor_reduce(sm[k % 2][:, :], pb[k % 2][:, :, WIN * (k % 2):], AX_X, ALU.add))
                    dve.reciprocal(sm[k % 2][:, :], sm[k % 2][:, :]).then_inc(s["r"], 1)
                elif k == "wo":
                    dve.wait_ge(s["f"], r * 10 + 1)
                    wait(dve, s["out"], r)
                    dve.tensor_tensor(c.H[:, ds(b * N, N)], psF[:, :], c.H[:, ds(b * N, N)], ALU.add).then_inc(s["xf"], 1)
                elif k == "tr":
                    cf = Chain(dve, s_f, 23, r)
                    dve.wait_ge(s["f"], r * 10 + 2)
                    norm_tokens(c, dve, cf, yn, psF[:, :].rearrange("p (t c) -> p t c", t=TILES), stats, mv, rs,
                                1e-5).then_inc(s["yn"], 1)
                    cf.end()
                elif k[0] == "a":
                    n, (at, m) = int(k[1]), CH[int(k[1])]
                    dve.wait_ge(s["f"], r * 10 + 5 + 2 * n)
                    dve.scalar_tensor_tensor(out=hh[0:m, n, :], in0=psF[0:m, :], scalar=cols[0:m, 2 + n:3 + n],
                                             in1=gg[0:m, :], op0=ALU.add, op1=ALU.mult).then_inc(s["hh"], 1)
                else:
                    dve.wait_ge(s["f"], r * 10 + 10)
                    dve.scalar_tensor_tensor(out=c.H[:, ds(b * N, N)], in0=psF[:, :], scalar=cols[:, 8:9],
                                             in1=c.H[:, ds(b * N, N)], op0=ALU.add, op1=ALU.add).then_inc(s["out"], 1)
            dve.wait_ge(s["tab"], 4 * DEPTH)
            turns(dve, "dve", step)

        @block.gpsimd
        def _(pool):
            pool.memset(xs[:, 0:1], 0.0)
            pool.memset(xsf[:, 0:1], 0.0).then_inc(s["z"], 1)
            for j in range(2):
                pool.memset(qb[j][:, :, :, :, :], 0.0)
            pool.memset(kT[:, :, 0:WIN], 0.0)
            pool.memset(pb[1][:, :, 0:WIN], 0.0).then_inc(s["z"], 1)
            pool.memset(v_even[:, :], 0.0).then_inc(s["z"], 1)
            pool.wait_ge(s["scl"], 16)
            for layer in range(DEPTH):
                for k, base in enumerate((c.rope_cos_q, c.rope_sin_q, c.rope_cos_k, c.rope_sin_k)):
                    pool.tensor_tensor(tabs[:, layer, k, :, :], base[:, :, :],
                                       scl[:, layer, ds(k, 1), :].to_broadcast([128, TILES, DH]), ALU.mult).then_inc(s["tab"], 1)

            def step(kind, k, j, r, b, layer):
                if kind == "Rb":
                    u = r * UT + 4 * k + j
                    xv = raw[k % 2][:, j, :].rearrange("p (h x d) -> p h x d", x=2, d=32)
                    tv = t2[:, :].rearrange("p (h x d) -> p h x d", x=2, d=32)
                    wait(pool, s["qr"], u)
                    c.wait_apart(pool, s["rn"], u + 1)
                    for x in range(2):
                        tab = tabs[:, ds(layer, 1), 2 * (j // 2) + 1, k, 32 * x:32 * x + 32].to_broadcast([128, 8, 32])
                        last = pool.tensor_tensor(tv[:, :, x, :], xv[:, :, 1 - x, :], tab, ALU.mult)
                    last.then_inc(s_pool, 1)
                    pool.wait_ge(s_pool, u + 1)
                    pool.wait_ge(s["t1"], u + 1)
                    pool.tensor_tensor(qr[:, j, :], qr[:, j, :], t2[:, :], ALU.add).then_inc(s["qr"], 1)
                else:
                    pool.wait_ge(s["r"], r * NBLK + k + 1)
                    p = pb[k % 2][:, :, WIN * (k % 2):]
                    pool.tensor_tensor(p, p, sm[k % 2][:, :].unsqueeze(2).to_broadcast([128, PAIRS, KEYS]),
                                       ALU.mult).then_inc(s["pn"], 1)
            pool.wait_ge(s["tab"], 4 * DEPTH)
            turns(pool, "pool", step)


def program(nc, ins, out):
    with ExitStack() as stack:
        c = Core(nc, ins, stack)
        place_tables(c)
        stages = [lambda: setup(c), lambda: adaln(c, 0, 0), lambda: convolutions(c), lambda: linear_attention(c),
                  lambda: feed_forward(c), lambda: adaln(c, 0, 1), lambda: experts(c), lambda: adaln(c, 1, 0),
                  lambda: causal_attention(c), lambda: adaln(c, 1, 1), lambda: windowed_layers(c),
                  lambda: finish(c, out)]
        for stage in stages:
            with ExitStack() as c.stage:
                stage()


def layouts(i):
    A = lambda n: np.asarray(i["L0_attn_" + n])
    E = lambda n: np.asarray(i["L0_ffn_" + n])
    B = lambda n: np.asarray(i["L1_attn_" + n])
    W = lambda n: np.asarray(i["L1_ffn_" + n])
    col = lambda a: a.reshape(-1, D).T
    swap = lambda a: np.concatenate([a[:, 32:], a[:, :32]], 1)
    FF, DEPTH = 341, 6

    def ff_cols(a):
        return np.pad(a, ((0, 0), (0, 3 * D - FF))).reshape(DEPTH, 3, D).transpose(0, 2, 1)

    return {
        "x": np.asarray(i["L0_attn_x"]).reshape(T, D).T,
        "c_cols": np.stack([np.asarray(i["L0_c"]).T, np.asarray(i["L1_c"]).T], 1),
        "w_mod": np.stack([np.asarray(i["L0_wmod"]), np.asarray(i["L1_wmod"])]),
        "tables_all_in": group_array("all"),
        "tables_0_in": group_array("L0"),
        "tables_1_in": group_array("L1"),
        "cols_conv": np.concatenate([A("conv1_w").reshape(D, 20), A("conv2_w").reshape(D, 20), A("conv1_b").reshape(D, 4),
                                     col(A("conv2_b")), col(A("ln0_g")), col(A("ln0_b"))], 1),
        "w_qkv0": np.concatenate([A("Wq"), A("Wk"), A("Wv")], 2),
        "b_kv0": np.concatenate([A("bk"), A("bv")], 1).reshape(1, -1),
        "cols_la": np.stack([A("bq"), A("lnA_g"), A("lnA_b")]).transpose(2, 0, 1),
        "w_ff0a": A("W1"),
        "w_ff0b": A("W2").reshape(4, D, D).transpose(1, 0, 2),
        "cols_ff0": np.concatenate([col(A("b1")), col(A("b2")), col(A("ln2_g")), col(A("ln2_b"))], 1),
        "keys_rw": np.stack([E("keys").T, E("rw").T], 1),
        "rb": E("rb").reshape(1, 16),
        "b2_moe": E("b2"),
        "w1_moe": E("w1").transpose(0, 2, 1),
        "w2_moe": E("w2").reshape(16, D, 4, D).transpose(0, 3, 2, 1),
        "b1_moe": E("b1").reshape(16, 4, D).transpose(0, 2, 1),
        "w_qk1": np.stack([B("Wq"), B("Wk")], 1),
        "w_vdT": B("Wvdown").T,
        "w_vu": B("Wvup"),
        "qk_scales": np.stack([W("q_scale"), swap(W("q_scale")), W("k_scale"), swap(W("k_scale"))], 1).reshape(1, -1),
        "w_qkv1": W("Wqkv"),
        "w_o1": W("Wo").reshape(DEPTH, 8, D, D).transpose(0, 2, 1, 3),
        "w_ff1": W("W1"),
        "w_ff2": np.pad(W("W2"), ((0, 0), (0, 3 * D - FF), (0, 0))).reshape(DEPTH, 3, D, D).transpose(0, 2, 1, 3),
        "cols_w": np.concatenate([W("ln_g")[:, :, None], W("ln_b")[:, :, None], ff_cols(W("b1")[:, :FF]),
                                  ff_cols(W("b1")[:, FF:]), W("b2")[:, :, None]], 2),
    }


def kernel(**inputs):
    import concourse.bacc as _bacc
    from concourse.bass_utils import run_bass_kernel_spmd as _run

    nc = _bacc.Bacc("TRN2", target_bir_lowering=False, num_devices=1)
    arrays, ins = {}, {}
    for name, a in layouts(inputs).items():
        a = np.ascontiguousarray(a)
        arrays[f"in_{name}"] = a
        ins[name] = nc.dram_tensor(f"in_{name}", a.shape, mybir.dt.from_np(a.dtype), kind="ExternalInput").ap()
    out = nc.dram_tensor("out_x", (D, T), F32, kind="ExternalOutput").ap()
    program(nc, ins, out)
    r = _run(nc, [arrays], core_ids=[0])
    return np.ascontiguousarray(r.results[0]["out_x"].T.reshape(NB, N, D))
```

```python
from contextlib import ExitStack

import numpy as np

import concourse.bass as bass
from concourse import mybir

F32 = mybir.dt.float32
BF16 = mybir.dt.bfloat16
I32 = mybir.dt.int32
ALU = mybir.AluOpType
ACT = mybir.ActivationFunctionType
AX_X = mybir.AxisListType.X
ds = bass.ds

D = 128
NB, N = 4, 512
T = NB * N
TILES = N // 128


class Chain:

    def __init__(self, eng, sem, per_iteration=0, iteration=0):
        self.eng, self.sem, self.n = eng, sem, 0
        self.per, self.base = per_iteration, per_iteration * iteration

    def inc(self, instruction):
        self.n += 1
        instruction.then_inc(self.sem, 1)
        return self.n

    def wait(self, mark):
        self.eng.wait_ge(self.sem, self.base + mark)

    def link(self, instruction):
        self.wait(self.inc(instruction))

    def end(self):
        assert self.n == self.per, (self.n, self.per)


GUESS = float(0x5F1FFFF9 - 0x400000)
STEP_A, STEP_C = 2.38924456, 0.703952253
BETA = float(np.sqrt(3 / 8 * STEP_C))


def rsqrt(dve, ch, y, x, half, tmp, first, op):
    ch.link(dve.tensor_scalar(half, x, float(first), 0.5, op, ALU.mult))
    ch.link(dve.tensor_scalar(y.bitcast(I32), half.bitcast(I32), -0.5, GUESS, ALU.mult, ALU.add))

    def fused(out, in0, scalar, in1, op0):
        ch.link(dve.scalar_tensor_tensor(out=out, in0=in0, scalar=float(scalar), in1=in1, op0=op0, op1=ALU.mult))
    ch.link(dve.tensor_tensor(tmp, y, y, ALU.mult))
    fused(tmp, tmp, -2.0, half, ALU.mult)
    fused(y, tmp, STEP_A, y, ALU.add)
    ch.link(dve.tensor_tensor(tmp, y, y, ALU.mult))
    fused(tmp, tmp, 2 * BETA * STEP_C ** 2, half, ALU.mult)
    fused(half, tmp, -10 / 3 * BETA, tmp, ALU.add)
    fused(y, half, 5 * BETA ** 2, y, ALU.add)


def norm_tokens(c, dve, ch, out, src, stats, mv, rs, eps):
    marks = [ch.inc(dve.bn_stats(stats[:, t, :], src[:, t, :])) for t in range(TILES)]
    c.wait_apart(dve, ch.sem, ch.base + marks[-1])
    marks = [ch.inc(dve.bn_aggr(mv[:, t, :], stats[:, t, :])) for t in range(TILES)]
    ch.wait(marks[-1])
    rsqrt(dve, ch, rs[:, 0, :], mv[:, :, 1], rs[:, 1, :], rs[:, 2, :], eps, ALU.add)
    for t in range(TILES):
        last = dve.tensor_scalar(out[:, t, :], src[:, t, :], mv[:, t, 0:1], rs[:, 0, t:t + 1],
                                 ALU.subtract, ALU.mult)
        if t < TILES - 1:
            ch.inc(last)
    return last


class Core:

    def __init__(self, nc, ins, stack):
        self.nc, self.ins, self.stack = nc, ins, stack
        self.stage = stack

    def sb(self, name, shape, dt=F32, keep=False):
        return (self.stack if keep else self.stage).enter_context(self.nc.sbuf_tensor(name, shape, dt))

    def ps(self, name, shape=(128, 512), dt=F32):
        return self.stage.enter_context(self.nc.psum_tensor(name, list(shape), dt))

    def wait_apart(self, eng, sem, value):
        wait(eng, sem, value)
        if not isinstance(value, int):
            eng.sem_inc(self.passed)

    def sem(self, name, keep=False):
        return (self.stack if keep else self.stage).enter_context(self.nc.semaphore(name))


def wait(eng, sem, value):
    if not isinstance(value, int) or value > 0:
        eng.wait_ge(sem, value)


def shape_constants():
    out = {}
    inv = (1.0 / 10000.0 ** (np.arange(0, D, 2, dtype=np.float32) / np.float32(D))).astype(np.float32)
    freqs = np.repeat(np.arange(N, dtype=np.float32)[:, None] * inv[None, :], 2, axis=-1)
    cos, sin = np.cos(freqs).astype(np.float32), np.sin(freqs).astype(np.float32)
    by_tile = lambda a: a.reshape(TILES, 128, -1).transpose(1, 0, 2)
    out["cos_tok"], out["sin_tok"] = by_tile(cos), by_tile(sin)
    out["cos_feat"], out["sin_feat"] = cos.T, sin.T
    rot = np.zeros((D, D), np.float32)
    rot[np.arange(0, D, 2), np.arange(1, D, 2)] = -1
    rot[np.arange(1, D, 2), np.arange(0, D, 2)] = 1
    out["rot"], out["rot_t"] = rot, rot.T
    out["ident"] = np.eye(D, dtype=np.float32)
    head = np.kron(np.eye(16), np.ones((8, 8))).astype(np.float32)
    out["headmask"] = np.stack([head, head], axis=1)
    out["ones_n"] = np.full((D, D), 1.0 / N, np.float32)
    out["ones"] = np.ones((D, D), np.float32)
    half = np.arange(0, 64, 2, dtype=np.float32)
    fr = np.arange(N, dtype=np.float32)[:, None] * (1.0 / 10000.0 ** (half / 64)).astype(np.float32)[None, :]
    base = ((half + np.float32(0.4 * 64)) / np.float32(1.4 * 64)).astype(np.float32)
    power = ((np.arange(N, dtype=np.float32) - N // 2) / 16).astype(np.float32)
    scale = (base[None, :] ** power[:, None]).astype(np.float32)
    c1, s1 = np.cos(fr).astype(np.float32), np.sin(fr).astype(np.float32)
    for kind, f in (("q", scale), ("k", (1.0 / scale).astype(np.float32))):
        out["rope_cos_" + kind] = by_tile(np.concatenate([c1 * f, c1 * f], -1))
        out["rope_sin_" + kind] = by_tile(np.concatenate([-s1 * f, s1 * f], -1))
    out["causal"] = by_tile(np.tril(np.ones((N, N), np.float32)))
    qpos, kpos = np.tile(np.arange(64), 2)[:, None], np.arange(-32, 64)[None, :]
    band = (qpos - kpos >= 0) & (qpos - kpos <= 32)
    out["band"] = np.stack([np.tile(np.where(m, 0.0, -1e30), (1, 4)) for m in (band & (kpos >= 0), band)],
                           axis=1).astype(np.float32)
    return {k: np.ascontiguousarray(v, np.float32) for k, v in out.items()}


GROUPS = {
    "all": ("ident", "ones", "band"),
    "L0": ("cos_tok", "sin_tok", "cos_feat", "sin_feat", "rot", "rot_t", "headmask", "ones_n"),
    "L1": ("causal", "rope_cos_q", "rope_sin_q", "rope_cos_k", "rope_sin_k"),
}


def group_array(group):
    tables = shape_constants()
    return np.concatenate([tables[name].reshape(128, -1) for name in GROUPS[group]], 1)


def place_tables(c):
    tables = shape_constants()
    width = {g: sum(tables[name].size // 128 for name in names) for g, names in GROUPS.items()}
    c.tables_all = c.sb("tables_all", [128, width["all"]], keep=True)
    both = c.sb("tables_layer", [128, max(width["L0"], width["L1"])], keep=True)
    c.tables_0, c.tables_1 = both[:, 0:width["L0"]], both[:, 0:width["L1"]]
    views = {}
    for group, buf in (("all", c.tables_all), ("L0", c.tables_0), ("L1", c.tables_1)):
        at = 0
        for name in GROUPS[group]:
            shape = tables[name].shape
            v = buf[:, at:at + tables[name].size // 128]
            at += tables[name].size // 128
            views[name] = v.rearrange("p (a b) -> p a b", a=shape[1]) if len(shape) == 3 else v
    c.ident, c.ones, c.band = (views[name] for name in GROUPS["all"])
    c.cos_tok, c.sin_tok, c.cos_feat, c.sin_feat, c.rot, c.rot_t, c.headmask, c.ones_n = (
        views[name] for name in GROUPS["L0"])
    c.causal, c.rope_cos_q, c.rope_sin_q, c.rope_cos_k, c.rope_sin_k = (views[name] for name in GROUPS["L1"])


def setup(c):
    nc = c.nc
    c.passed = c.sem("passed", keep=True)
    c.adaln_sems = [c.sem("n_s_" + k, keep=True) for k in ("tr", "yn_act", "yn_dve", "back", "rs", "dve")]
    c.X = c.sb("X", [D, T], keep=True)
    c.H = c.sb("H", [D, T], keep=True)
    c.mods = c.sb("mods", [D, 2, 6, NB], keep=True)
    c.ident_bf = c.sb("ident_bf", [D, D], BF16, keep=True)
    c.band_bf = c.sb("band_bf", [D, 2, 384], BF16, keep=True)
    cT = c.sb("m_cT", [D, 2, NB])
    sT = c.sb("m_sT", [D, 2, NB])
    wm = [c.sb(f"m_w{j}", [D, 6 * D]) for j in range(2)]
    ga = c.sb("m_abs", [D, 2, 2, NB])
    gs = c.sb("m_sign", [D, 2, 2, NB])
    ps = c.ps("m_ps")
    s_x, s_c, s_k = c.sem("m_s_x"), c.sem("m_s_c"), c.sem("m_s_tables")
    s_silu, s_mm, s_ch = c.sem("m_s_silu"), c.sem("m_s_mm"), c.sem("m_s_dve")

    with nc.Block() as block:
        @block.sync
        def _(sp):
            sp.dma_start(cT[:, :, :], c.ins["c_cols"]).then_inc(s_c, 16)
            for j in range(2):
                sp.dma_start(wm[j][:, :], c.ins["w_mod"][j]).then_inc(s_c, 16)
            sp.dma_start(c.X[:, :], c.ins["x"]).then_inc(s_x, 16)
            sp.dma_start(c.tables_all[:, :], c.ins["tables_all_in"]).then_inc(s_k, 16)
            sp.dma_start(c.tables_0, c.ins["tables_0_in"]).then_inc(s_k, 16)
            sp.wait_ge(s_x, 16)
            sp.wait_ge(s_k, 32)

        @block.scalar
        def _(act):
            act.wait_ge(s_c, 48)
            act.activation(sT[:, :, :], cT[:, :, :], ACT.Silu).then_inc(s_silu, 1)

        @block.tensor
        def _(pe):
            pe.wait_ge(s_silu, 1)
            for l in range(2):
                for j in range(6):
                    at = (l * 6 + j) * NB
                    last = pe.matmul(ps[:, at:at + NB], wm[l][:, j * D:(j + 1) * D], sT[:, l, :], start=True, stop=True)
            last.then_inc(s_mm, 1)

        @block.vector
        def _(dve):
            ch = Chain(dve, s_ch)
            dve.wait_ge(s_mm, 1)
            ch.link(dve.tensor_copy(c.mods[:, :, :, :], ps[:, 0:48].rearrange("p (l j b) -> p l j b", l=2, j=6)))
            for j in (1, 4):
                ch.inc(dve.tensor_scalar(c.mods[:, :, j, :], c.mods[:, :, j, :], 1.0, None, ALU.add))
            for n, j in enumerate((2, 5)):
                g = c.mods[:, :, j, :]
                ch.link(dve.scalar_tensor_tensor(out=ga[:, n, :, :], in0=g, scalar=-1.0, in1=g, op0=ALU.mult, op1=ALU.max))
                ch.link(dve.tensor_scalar(ga[:, n, :, :], ga[:, n, :, :], 0.25, None, ALU.max))
                ch.link(dve.tensor_scalar(gs[:, n, :, :], g, 0.0, 2.0, ALU.is_ge, ALU.mult))
                ch.link(dve.tensor_scalar(gs[:, n, :, :], gs[:, n, :, :], -1.0, None, ALU.add))
                ch.inc(dve.tensor_tensor(g, ga[:, n, :, :], gs[:, n, :, :], ALU.mult))
            dve.wait_ge(s_k, 32)
            ch.inc(dve.tensor_copy(c.ident_bf[:, :], c.ident[:, :]))
            ch.link(dve.tensor_copy(c.band_bf[:, :, :], c.band[:, :, :]))


def adaln(c, layer, part):
    nc, n = c.nc, f"n{layer}{part}_"
    NT = NB * TILES
    yn = c.sb(n + "yn", [128, NT, D])
    stats = c.sb(n + "stats", [128, NT, 6])
    mv = c.sb(n + "mv", [128, NT, 2])
    rs = c.sb(n + "rs", [128, 3, NT])
    shift = c.sb(n + "shift", [128, NT])
    psX = [c.ps(n + f"psX{b}") for b in range(NB)]
    psB = [c.ps(n + f"psB{b}") for b in range(NB)]
    s_tr, s_yn_act, s_yn_dve, s_bk, s_rs, s_ch = c.adaln_sems
    call = 2 * layer + part
    gain = lambda b: c.mods[:, layer, 3 * part + 1, b:b + 1]
    add = lambda b: c.mods[:, layer, 3 * part, b:b + 1]
    with nc.Block() as block:
        @block.tensor
        def _(pe):
            for b in range(NB):
                for t in range(TILES):
                    at = b * N + 128 * t
                    last = pe.transpose(psX[b][:, 128 * t:128 * t + 128], c.X[:, at:at + 128], c.ident[:, :])
                last.then_inc(s_tr, 1)
            for b in (0, 2, 1, 3):
                if b < 2:
                    pe.wait_ge(s_yn_act, call * 2 + b + 1)
                else:
                    pe.wait_ge(s_yn_dve, call * 2 + b - 1)
                for t in range(TILES):
                    last = pe.transpose(psB[b][:, 128 * t:128 * t + 128], yn[:, b * TILES + t, :], c.ident[:, :])
                last.then_inc(s_bk, 1)

        @block.scalar
        def _(act):
            act.wait_ge(s_rs, call + 1)
            for b in range(2):
                for t in range(TILES):
                    k = b * TILES + t
                    last = act.activation(yn[:, k, :], psX[b][:, 128 * t:128 * t + 128], ACT.Identity,
                                          bias=shift[:, k:k + 1], scale=rs[:, 0, k:k + 1])
                last.then_inc(s_yn_act, 1)
            for b in range(2):
                act.wait_ge(s_bk, call * NB + 2 * b + 1)
                act.activation(c.H[:, b * N:(b + 1) * N], psB[b][:, :], ACT.Identity, bias=add(b), scale=gain(b))

        @block.vector
        def _(dve):
            ch = Chain(dve, s_ch, 2 * NT + 9, call)
            for b in range(NB):
                dve.wait_ge(s_tr, call * NB + b + 1)
                for t in range(TILES):
                    mark = ch.inc(dve.bn_stats(stats[:, b * TILES + t, :], psX[b][:, 128 * t:128 * t + 128]))
            ch.wait(mark)
            for k in range(NT):
                mark = ch.inc(dve.bn_aggr(mv[:, k, :], stats[:, k, :]))
            ch.wait(mark)
            rsqrt(dve, ch, rs[:, 0, :], mv[:, :, 1], rs[:, 1, :], rs[:, 2, :], 1e-5, ALU.add)
            dve.scalar_tensor_tensor(out=shift[:, :], in0=mv[:, :, 0], scalar=-1.0, in1=rs[:, 0, :], op0=ALU.mult,
                                     op1=ALU.mult).then_inc(s_rs, 1)
            for b in range(2, NB):
                for t in range(TILES):
                    k = b * TILES + t
                    last = dve.tensor_scalar(yn[:, k, :], psX[b][:, 128 * t:128 * t + 128], mv[:, k, 0:1],
                                             rs[:, 0, k:k + 1], ALU.subtract, ALU.mult)
                last.then_inc(s_yn_dve, 1)
            for b in range(2, NB):
                dve.wait_ge(s_bk, call * NB + 2 * (b - 2) + 2)
                dve.tensor_scalar(c.H[:, b * N:(b + 1) * N], psB[b][:, :], gain(b), add(b), ALU.mult, ALU.add)
            ch.end()


def convolutions(c):
    nc = c.nc
    O, K = 4, 5
    POOL_O = 2
    cols = c.sb("c_cols_sb", [D, 2 * O * K + O + 3])
    w1, w2 = cols[:, 0:O * K], cols[:, O * K:2 * O * K]
    b1 = cols[:, 2 * O * K:2 * O * K + O]
    b2, gain, shift = (cols[:, 2 * O * K + O + j:2 * O * K + O + j + 1] for j in range(3))
    diag = c.sb("c_diag", [D, O * K, D])
    hp = [c.sb(f"c_hp{b}", [D, N + K - 1]) for b in range(NB)]
    hid = [c.sb(f"c_hid{b}", [D, O, N + K - 1]) for b in range(NB)]
    acc = [c.sb(f"c_acc{b}", [D, N]) for b in range(NB)]
    accp = [c.sb(f"c_accp{b}", [D, N]) for b in range(NB)]
    tap = c.sb("c_tap", [D, N])
    yn = [c.sb(f"c_yn{b}", [128, TILES, D]) for b in range(NB)]
    stats = c.sb("c_stats", [128, TILES, 6])
    mv = c.sb("c_mv", [128, TILES, 2])
    rs = c.sb("c_rs", [128, 3, TILES])
    psC = [c.ps(f"c_psC{j}") for j in range(4)]
    psN = [c.ps(f"c_psN{b}") for b in range(NB)]
    s = {k: c.sem("c_s_" + k) for k in ("w", "z", "dg", "hp", "c1", "hid", "acc", "accp", "tr", "yn", "back", "h")}
    s_ch, s_pool = c.sem("c_s_dve"), c.sem("c_s_pool")
    with nc.Block() as block:
        @block.sync
        def _(sp):
            sp.dma_start(cols[:, :], c.ins["cols_conv"]).then_inc(s["w"], 16)

        @block.gpsimd
        def _(pool):
            for b in range(NB):
                for buf in (hp[b][:, :].unsqueeze(1), hid[b][:, :, :]):
                    pool.memset(buf[:, :, 0:K // 2], 0.0)
                    last = pool.memset(buf[:, :, K // 2 + N:], 0.0)
            last.then_inc(s["z"], 1)
            pool.wait_ge(s["w"], 16)
            ch = Chain(pool, s_pool)
            for b in range(NB):
                a = accp[b][:, :]
                pool.wait_ge(s["hid"], b * O + POOL_O + 1)
                for k in range(K):
                    x, w = hid[b][:, POOL_O, k:k + N], w2[:, POOL_O * K + k:POOL_O * K + k + 1]
                    if k == 0:
                        ch.link(pool.tensor_scalar(a, x, w, b2, ALU.mult, ALU.add))
                    else:
                        ch.link(pool.tensor_scalar(tap[:, :], x, w, None, ALU.mult))
                        last = pool.tensor_tensor(a, a, tap[:, :], ALU.add)
                        if k < K - 1:
                            ch.link(last)
                last.then_inc(s["accp"], 1)

        @block.scalar
        def _(act):
            act.wait_ge(s["w"], 16)
            act.wait_ge(s["z"], 1)
            for b in range(NB):
                act.activation(hp[b][:, 2:2 + N], c.H[:, b * N:(b + 1) * N], ACT.Copy).then_inc(s["hp"], 1)

            def result(b):
                act.wait_ge(s["back"], b + 1)
                act.activation(c.H[:, b * N:(b + 1) * N], psN[b][:, :], ACT.Identity, bias=shift, scale=gain)
            for b in range(NB):
                for o in range(O):
                    act.wait_ge(s["c1"], b * O + o + 1)
                    act.activation(hid[b][:, o, 2:2 + N], psC[o][:, :], ACT.Gelu, bias=b1[:, o:o + 1]).then_inc(s["hid"], 1)
                if b >= 2:
                    result(b - 2)
            result(NB - 2)
            result(NB - 1)

        @block.tensor
        def _(pe):
            def conv1(b):
                pe.wait_ge(s["hp"], b + 1)
                for o in range(O):
                    wait(pe, s["hid"], (b - 1) * O + o + 1)
                    if b == 0:
                        pe.wait_ge(s["dg"], (o + 1) * K)
                    for k in range(K):
                        last = pe.matmul(psC[o][:, :], diag[:, o * K + k, :], hp[b][:, k:k + N],
                                         start=(k == 0), stop=(k == K - 1))
                    last.then_inc(s["c1"], 1)

            def by_tokens(b):
                pe.wait_ge(s["acc"], b + 1)
                for t in range(TILES):
                    tt = slice(128 * t, 128 * t + 128)
                    last = pe.transpose(psN[b][:, tt], acc[b][:, tt], c.ident[:, :])
                last.then_inc(s["tr"], 1)

            def by_features(b):
                pe.wait_ge(s["yn"], b + 1)
                for t in range(TILES):
                    last = pe.transpose(psN[b][:, 128 * t:128 * t + 128], yn[b][:, t, :], c.ident[:, :])
                last.then_inc(s["back"], 1)
            conv1(0)
            conv1(1)
            for b in range(2, NB + 2):
                by_tokens(b - 2)
                if b < NB:
                    conv1(b)
                by_features(b - 2)

        @block.vector
        def _(dve):
            dve.wait_ge(s["w"], 16)
            for j in range(O * K):
                dve.tensor_scalar(diag[:, j, :], c.ident[:, :], w1[:, j:j + 1], None, ALU.mult).then_inc(s["dg"], 1)
            mine = [o for o in range(O) if o != POOL_O]
            ch = Chain(dve, s_ch)

            def norm(b):
                dve.wait_ge(s["tr"], b + 1)
                norm_tokens(c, dve, ch, yn[b], psN[b][:, :].rearrange("p (t c) -> p t c", t=TILES), stats, mv, rs,
                            1e-12).then_inc(s["yn"], 1)
                dve.wait_ge(s["yn"], b + 1)
            for b in range(NB):
                a = acc[b][:, :]
                for o in mine:
                    dve.wait_ge(s["hid"], b * O + o + 1)
                    for k in range(K):
                        x, w = hid[b][:, o, k:k + N], w2[:, o * K + k:o * K + k + 1]
                        if o == 0 and k == 0:
                            y = hp[b][:, 2:2 + N]
                        else:
                            y = a
                        ch.link(dve.scalar_tensor_tensor(out=a, in0=x, scalar=w, in1=y, op0=ALU.mult, op1=ALU.add))
                dve.wait_ge(s["accp"], b + 1)
                dve.tensor_tensor(a, a, accp[b][:, :], ALU.add).then_inc(s["acc"], 1)
                if b:
                    norm(b - 1)
            norm(NB - 1)


def feed_forward(c):
    nc = c.nc
    UN, C = 2, 4
    w1 = c.sb("f_w1", [D, C * D])
    w2 = c.sb("f_w2", [D, C, D])
    cols = c.sb("f_cols", [D, C + 3])
    hh = [c.sb(f"f_hh{u}", [D, C, N]) for u in range(UN)]
    y = [c.sb(f"f_y{u}", [D, N]) for u in range(UN)]
    yn = [c.sb(f"f_yn{u}", [128, TILES, D]) for u in range(UN)]
    ya = [c.sb(f"f_ya{u}", [D, N]) for u in range(UN)]
    stats = [c.sb(f"f_stats{u}", [128, TILES, 6]) for u in range(UN)]
    mv = [c.sb(f"f_mv{u}", [128, TILES, 2]) for u in range(UN)]
    rs = [c.sb(f"f_rs{u}", [128, 3, TILES]) for u in range(UN)]
    psC = [c.ps(f"f_psC{j}") for j in range(2)]
    psY = [c.ps(f"f_psY{u}") for u in range(UN)]
    s = {k: c.sem("f_s_" + k) for k in ("w", "c1", "hh", "o", "y", "tr", "yn", "back", "ya", "x")}
    s_ch = c.sem("f_s_dve")
    with nc.Block() as block:
        @block.sync
        def _(sp):
            sp.dma_start(w1[:, :], c.ins["w_ff0a"]).then_inc(s["w"], 16)
            sp.dma_start(w2[:, :, :], c.ins["w_ff0b"]).then_inc(s["w"], 16)
            sp.dma_start(cols[:, :], c.ins["cols_ff0"]).then_inc(s["w"], 16)

        @block.tensor
        def _(pe):
            pe.wait_ge(s["w"], 48)
            for pair in range(NB // UN):
                it = pair * UN
                for u in range(UN):
                    for j in range(C):
                        if u == 0 and j < 2:
                            wait(pe, s["hh"], it * C)
                        else:
                            wait(pe, s["hh"], (it + u) * C + j - 1)
                        pe.matmul(psC[j % 2][:, :], w1[:, j * D:(j + 1) * D], c.H[:, ds((it + u) * N, N)], start=True,
                                  stop=True).then_inc(s["c1"], 1)
                for u in range(UN):
                    wait(pe, s["hh"], (it + u + 1) * C)
                    wait(pe, s["ya"], it)
                    for j in range(C):
                        last = pe.matmul(psY[u][:, :], w2[:, j, :], hh[u][:, j, :], start=(j == 0), stop=(j == C - 1))
                    last.then_inc(s["o"], 1)
                for u in range(UN):
                    pe.wait_ge(s["y"], it + u + 1)
                    for t in range(TILES):
                        tt = slice(128 * t, 128 * t + 128)
                        last = pe.transpose(psY[u][:, tt], y[u][:, tt], c.ident[:, :])
                    last.then_inc(s["tr"], 1)
                for u in range(UN):
                    pe.wait_ge(s["yn"], it + u + 1)
                    for t in range(TILES):
                        last = pe.transpose(psY[u][:, 128 * t:128 * t + 128], yn[u][:, t, :], c.ident[:, :])
                    last.then_inc(s["back"], 1)

        @block.scalar
        def _(act):
            act.wait_ge(s["w"], 48)
            for pair in range(NB // UN):
                it = pair * UN
                for u in range(UN):
                    wait(act, s["o"], it)
                    for j in range(C):
                        act.wait_ge(s["c1"], (it + u) * C + j + 1)
                        act.activation(hh[u][:, j, :], psC[j % 2][:, :], ACT.Gelu, bias=cols[:, j:j + 1]).then_inc(s["hh"], 1)
                for u in range(UN):
                    act.wait_ge(s["back"], it + u + 1)
                    wait(act, s["x"], it)
                    act.activation(ya[u][:, :], psY[u][:, :], ACT.Identity, bias=cols[:, C + 2:C + 3],
                                   scale=cols[:, C + 1:C + 2]).then_inc(s["ya"], 1)

        @block.vector
        def _(dve):
            for pair in range(NB // UN):
                it = pair * UN
                ch = Chain(dve, s_ch, 40, pair)
                for u in range(UN):
                    dve.wait_ge(s["o"], it + u + 1)
                    dve.scalar_tensor_tensor(out=y[u][:, :], in0=psY[u][:, :], scalar=cols[:, C:C + 1],
                                             in1=c.H[:, ds((it + u) * N, N)], op0=ALU.add, op1=ALU.add).then_inc(s["y"], 1)
                for u in range(UN):
                    dve.wait_ge(s["tr"], it + u + 1)
                    norm_tokens(c, dve, ch, yn[u], psY[u][:, :].rearrange("p (t c) -> p t c", t=TILES), stats[u], mv[u],
                                rs[u], 1e-12).then_inc(s["yn"], 1)
                for u in range(UN):
                    b = it + u
                    dve.wait_ge(s["ya"], b + 1)
                    dve.scalar_tensor_tensor(out=c.X[:, ds(b * N, N)], in0=ya[u][:, :], scalar=c.mods[:, 0, 2, ds(b, 1)],
                                             in1=c.X[:, ds(b * N, N)], op0=ALU.mult, op1=ALU.add).then_inc(s["x"], 1)
                ch.end()


def linear_attention(c):
    nc = c.nc
    LAYERS, NH, HD = 4, 16, 8
    UN = 2
    hs = [c.sb(f"la_hs{u}", [D, N]) for u in range(UN)]
    qg = [c.sb(f"la_qg{u}", [D, N]) for u in range(UN)]
    qp = [c.sb(f"la_qp{u}", [D, N]) for u in range(UN)]
    qc = [c.sb(f"la_qc{u}", [D, N]) for u in range(UN)]
    qs = [c.sb(f"la_qs{u}", [D, N]) for u in range(UN)]
    kg = [c.sb(f"la_kg{u}", [128, TILES, D]) for u in range(UN)]
    kc = [c.sb(f"la_kc{u}", [128, TILES, D]) for u in range(UN)]
    ks = [c.sb(f"la_ks{u}", [128, TILES, D]) for u in range(UN)]
    vv = [c.sb(f"la_v{u}", [128, TILES, D]) for u in range(UN)]
    a12 = [c.sb(f"la_a12_{u}", [D, 3, D]) for u in range(UN)]
    kvm = [c.sb(f"la_kvm{u}", [D, 2, D]) for u in range(UN)]
    kmm = [c.sb(f"la_kmm{u}", [D, D]) for u in range(UN)]
    z = [c.sb(f"la_z{u}", [128, TILES * NH]) for u in range(UN)]
    y = [c.sb(f"la_y{u}", [128, TILES, D]) for u in range(UN)]
    yn = [c.sb(f"la_yn{u}", [128, TILES, D]) for u in range(UN)]
    stats = [c.sb(f"la_stats{u}", [128, TILES, 6]) for u in range(UN)]
    mv = [c.sb(f"la_mv{u}", [128, TILES, 2]) for u in range(UN)]
    rs = [c.sb(f"la_rs{u}", [128, 3, TILES]) for u in range(UN)]
    wqkv = c.sb("la_wqkv", [D, 3 * D])
    lcols = c.sb("la_cols", [D, 3, LAYERS])
    bias = c.sb("la_bias", [3, LAYERS * 2 * D])
    rest = c.sb("la_rest", [3, LAYERS * 2 * D])
    part = c.sb("la_part", [3, 3, LAYERS * 2 * D], BF16)
    bias3 = c.sb("la_bias3", [3, LAYERS * 2 * D], BF16)
    ones3 = c.sb("la_ones3", [3, D], BF16)
    psQ = [c.ps(f"la_psQ{u}") for u in range(UN)]
    psK = [c.ps(f"la_psK{u}", (128, 2, 512)) for u in range(UN)]
    psA = [c.ps(f"la_psA{u}") for u in range(UN)]

    names = ("w", "c", "b3", "hs", "q", "kv", "qg", "kg", "v", "qc", "kc", "a", "a12", "kmm", "r", "kvm", "o", "yn", "t",
             "h", "x", "y")
    s = {k: c.sem("la_s_" + k) for k in names}
    s_bias, s_k, s_q, s_y, s_n = (c.sem("la_s_chain_" + k) for k in ("bias", "k", "q", "y", "norm"))

    ORDER = {
        "pe": "q0 r3- kv0 t2- o3- x0 a0 kv1 r0 q1 t3- o0 x1 a1 kv2 r1 q2 t0 o1 x2 a2 kv3 r2 q3 t1 o2 a3 x3",
        "act": "hs0 a123- qg0 kg0 H2- v0 hs1 a120 kg1 v1 qg1 hs2 H3- hs3 a121 kg2 v2 qg2 H0 a122 kg3 qg3 H1 v3",
        "dve": "n2- kmm3- kvm3- qc0 kc0 y3- n3- kmm0 kvm0 kc1 qc1 y0 n0 kmm1 kvm1 kc2 qc2 y1 n1 kmm2 kvm2 kc3 qc3 y2",
    }

    def layers(eng, name, step):
        def turn(i):
            for word in ORDER[name].split():
                before = word[-1] == "-"
                word = word.rstrip("-")
                layer = i - 1 if before else i
                if not isinstance(i, int) or 0 <= layer < LAYERS:
                    b = int(word[-1])
                    step(word[:-1], b, layer * NB + b, layer)
        turn(0)
        turn(1)
        with eng.Fori(2, LAYERS) as i:
            turn(i)
        turn(LAYERS)

    with nc.Block() as block:
        @block.sync
        def _(sp):
            sp.dma_start(lcols[:, :, :], c.ins["cols_la"]).then_inc(s["c"], 16)
            sp.dma_start(bias[:, :], c.ins["b_kv0"].to_broadcast([3, LAYERS * 2 * D])).then_inc(s["c"], 16)
            for layer in range(LAYERS):
                wait(sp, s["kv"], layer * NB)
                wait(sp, s["q"], layer * NB)
                sp.dma_start(wqkv[:, :], c.ins["w_qkv0"][layer]).then_inc(s["w"], 16)

        @block.tensor
        def _(pe):
            def step(kind, b, g, layer):
                u = b % UN
                if kind in ("q", "kv"):
                    pe.wait_ge(s["w"], (layer + 1) * 16)
                    pe.wait_ge(s["hs"], g + 1)
                    wait(pe, s["y"], g - 1)
                if kind == "q":
                    pe.matmul(psQ[u][:, :], wqkv[:, 0:D], hs[u][:, :], start=True, stop=True).then_inc(s["q"], 1)
                elif kind == "kv":
                    for t in range(TILES):
                        o = psK[u][:, t // 2, (t % 2) * 256:(t % 2 + 1) * 256]
                        pe.matmul(o, hs[u][:, t * 128:(t + 1) * 128], wqkv[:, D:3 * D], start=True, stop=False)
                        last = pe.matmul(o, ones3[:, :], bias3[:, ds(layer * 2 * D, 2 * D)], start=False, stop=True)
                    last.then_inc(s["kv"], 1)
                elif kind == "a":
                    pe.wait_ge(s["kc"], g + 1)
                    pe.wait_ge(s["v"], g + 1)
                    wait(pe, s["h"], g - 1)
                    for j, kk in enumerate((kc, ks)):
                        for t in range(TILES):
                            pe.matmul(psA[u][:, j * D:(j + 1) * D], kk[u][:, t, :], vv[u][:, t, :],
                                      start=(t == 0), stop=(t == TILES - 1))
                    for t in range(TILES):
                        last = pe.matmul(psA[u][:, 2 * D:3 * D], kg[u][:, t, :], c.ones_n[:, :],
                                         start=(t == 0), stop=(t == TILES - 1))
                    last.then_inc(s["a"], 1)
                elif kind == "x":
                    pe.wait_ge(s["v"], g + 1)
                    for t in range(TILES):
                        last = pe.transpose(psK[u][:, 0, t * 128:(t + 1) * 128], hs[u][:, t * 128:(t + 1) * 128],
                                            c.ident[:, :])
                    last.then_inc(s["x"], 1)
                elif kind == "r":
                    pe.wait_ge(s["a12"], g + 1)
                    pe.matmul(psA[u][:, 0:D], c.ident[:, :], a12[u][:, 0, :], start=True, stop=False)
                    pe.matmul(psA[u][:, 0:D], c.rot_t[:, :], a12[u][:, 1, :], start=False, stop=True)
                    pe.matmul(psA[u][:, D:2 * D], c.rot[:, :], a12[u][:, 0, :], start=True, stop=False)
                    pe.matmul(psA[u][:, D:2 * D], c.ident[:, :], a12[u][:, 1, :], start=False,
                              stop=True).then_inc(s["r"], 1)
                elif kind == "o":
                    pe.wait_ge(s["qc"], g + 1)
                    pe.wait_ge(s["kvm"], g + 1)
                    for t in range(TILES):
                        tt = slice(t * 128, (t + 1) * 128)
                        pe.matmul(psQ[u][:, tt], qc[u][:, tt], kvm[u][:, 0, :], start=True, stop=False)
                        pe.matmul(psQ[u][:, tt], qs[u][:, tt], kvm[u][:, 1, :], start=False, stop=True)
                        last = pe.matmul(psK[u][:, 1, tt], qp[u][:, tt], kmm[u][:, :], start=True, stop=True)
                    last.then_inc(s["o"], 1)
                else:
                    pe.wait_ge(s["yn"], g + 1)
                    for t in range(TILES):
                        last = pe.transpose(psA[u][:, t * 128:(t + 1) * 128], yn[u][:, t, :], c.ident[:, :])
                    last.then_inc(s["t"], 1)
            pe.wait_ge(s["b3"], 1)
            layers(pe, "pe", step)

        @block.scalar
        def _(act):
            def step(kind, b, g, layer):
                u = b % UN
                if kind == "hs":
                    wait(act, s["x"], g - 1)
                    wait(act, s["kv"], g - 1)
                    wait(act, s["q"], g - 1)
                    wait(act, s["h"], g - 3)
                    act.activation(hs[u][:, :], c.H[:, b * N:(b + 1) * N], ACT.Copy).then_inc(s["hs"], 1)
                elif kind == "qg":
                    wait(act, s["o"], g - 1)
                    c.wait_apart(act, s["q"], g + 1)
                    act.activation(qg[u][:, :], psQ[u][:, :], ACT.Gelu,
                                   bias=lcols[:, 0, ds(layer, 1)]).then_inc(s["qg"], 1)
                elif kind == "kg":
                    wait(act, s["a"], g - 1)
                    act.wait_ge(s["kv"], g + 1)
                    for j in range(2):
                        pk = psK[u][:, j, :].rearrange("p (t k c) -> p t k c", t=2, k=2)
                        last = act.activation(kg[u][:, 2 * j:2 * j + 2, :], pk[:, :, 0, :], ACT.Gelu)
                    last.then_inc(s["kg"], 1)
                elif kind == "v":
                    wait(act, s["a"], g - 1)
                    act.wait_ge(s["kv"], g + 1)
                    for j in range(2):
                        pk = psK[u][:, j, :].rearrange("p (t k c) -> p t k c", t=2, k=2)
                        last = act.activation(vv[u][:, 2 * j:2 * j + 2, :], pk[:, :, 1, :], ACT.Copy)
                    last.then_inc(s["v"], 1)
                elif kind == "a12":
                    wait(act, s["kvm"], g - 1)
                    act.wait_ge(s["a"], g + 1)
                    act.activation(a12[u][:, :, :], psA[u][:, 0:3 * D].rearrange("p (j c) -> p j c", j=3),
                                   ACT.Copy).then_inc(s["a12"], 1)
                else:
                    c.wait_apart(act, s["t"], g + 1)
                    act.activation(c.H[:, b * N:(b + 1) * N], psA[u][:, :], ACT.Identity,
                                   bias=lcols[:, 2, ds(layer, 1)], scale=lcols[:, 1, ds(layer, 1)]).then_inc(s["h"], 1)
            act.wait_ge(s["c"], 32)
            layers(act, "act", step)

        @block.vector
        def _(dve):
            def step(kind, b, g, layer):
                u = b % UN
                if kind == "kc":
                    kk = kg[u][:, :, :]
                    ch = Chain(dve, s_k, 1, g)
                    dve.wait_ge(s["kg"], g + 1)
                    wait(dve, s["a"], g - 1)
                    ch.inc(dve.scalar_tensor_tensor(out=kc[u][:, :, :], in0=kk, scalar=0.21, in1=c.cos_tok[:, :, :],
                                                    op0=ALU.add, op1=ALU.mult))
                    dve.scalar_tensor_tensor(out=ks[u][:, :, :], in0=kk, scalar=0.21, in1=c.sin_tok[:, :, :],
                                             op0=ALU.add, op1=ALU.mult).then_inc(s["kc"], 1)
                elif kind == "qc":
                    ch = Chain(dve, s_q, 2, g)
                    dve.wait_ge(s["qg"], g + 1)
                    wait(dve, s["o"], g - 1)
                    ch.inc(dve.tensor_scalar(qp[u][:, :], qg[u][:, :], 0.21, None, ALU.add))
                    ch.inc(dve.scalar_tensor_tensor(out=qc[u][:, :], in0=qg[u][:, :], scalar=0.21, in1=c.cos_feat[:, :],
                                                    op0=ALU.add, op1=ALU.mult))
                    dve.scalar_tensor_tensor(out=qs[u][:, :], in0=qg[u][:, :], scalar=0.21, in1=c.sin_feat[:, :],
                                             op0=ALU.add, op1=ALU.mult).then_inc(s["qc"], 1)
                elif kind == "kmm":
                    dve.wait_ge(s["a12"], g + 1)
                    wait(dve, s["o"], g - 1)
                    dve.scalar_tensor_tensor(out=kmm[u][:, :], in0=a12[u][:, 2, :], scalar=0.21,
                                             in1=c.headmask[:, 0, :], op0=ALU.add, op1=ALU.mult).then_inc(s["kmm"], 1)
                elif kind == "kvm":
                    dve.wait_ge(s["r"], g + 1)
                    dve.scalar_tensor_tensor(out=kvm[u][:, :, :], in0=psA[u][:, 0:2 * D].rearrange(
                        "p (j c) -> p j c", j=2), scalar=1.0 / N, in1=c.headmask[:, :, :],
                        op0=ALU.mult, op1=ALU.mult).then_inc(s["kvm"], 1)
                elif kind == "y":
                    ch = Chain(dve, s_y, 3, g)
                    dve.wait_ge(s["o"], g + 1)
                    wait(dve, s["yn"], g - 1)
                    den = psK[u][:, 1, :].rearrange("p (h e) -> p h e", e=HD)[:, :, 0]
                    ch.link(dve.tensor_scalar(z[u][:, :], den, 1e-6, None, ALU.add))
                    ch.link(dve.reciprocal(z[u][:, :], z[u][:, :]))
                    o3 = psQ[u][:, :].rearrange("p (h e) -> p h e", e=HD)
                    y3 = y[u][:, :, :].rearrange("p t (h e) -> p (t h) e", e=HD)
                    ch.link(dve.tensor_tensor(y3, o3, z[u][:, :].unsqueeze(2).to_broadcast([128, TILES * NH, HD]),
                                              ALU.mult))
                    dve.wait_ge(s["x"], g + 1)
                    dve.tensor_tensor(y[u][:, :, :], y[u][:, :, :],
                                      psK[u][:, 0, :].rearrange("p (t c) -> p t c", t=TILES), ALU.add).then_inc(s["y"], 1)
                else:
                    ch = Chain(dve, s_n, 20, g)
                    dve.wait_ge(s["y"], g + 1)
                    wait(dve, s["t"], g - 1)
                    norm_tokens(c, dve, ch, yn[u], y[u], stats[u], mv[u], rs[u], 1e-12).then_inc(s["yn"], 1)
                    ch.end()
            ch = Chain(dve, s_bias)
            dve.wait_ge(s["c"], 32)
            ch.inc(dve.tensor_copy(ones3[:, :], c.ones[0:3, :]))
            src = bias
            for n in range(3):
                ch.link(dve.tensor_copy(part[:, n, :], src[:, :]))
                if n < 2:
                    ch.link(dve.tensor_tensor(rest[:, :], src[:, :], part[:, n, :], ALU.subtract))
                    src = rest
            ch.link(dve.tensor_scalar(bias3[:, :], part[:, 0, :], c.ident[0:3, 0:1], None, ALU.mult))
            for n in (1, 2):
                last = dve.scalar_tensor_tensor(out=bias3[:, :], in0=part[:, n, :], scalar=c.ident[0:3, n:n + 1],
                                                in1=bias3[:, :], op0=ALU.mult, op1=ALU.add)
                if n == 1:
                    ch.link(last)
            last.then_inc(s["b3"], 1)
            layers(dve, "dve", step)


def experts(c):
    nc = c.nc
    E, TOPK, C, NT = 16, 4, 4, T // 128
    R32 = mybir.dt.float32r
    ROWS = 3 * 32
    raw = [c.sb(f"e_raw{u}", [D, 2, C * D]) for u in range(2)]
    whi = [c.sb(f"e_whi{u}", [D, 2, C * D], R32) for u in range(2)]
    wlo = [c.sb(f"e_wlo{u}", [D, 2, C * D], R32) for u in range(2)]
    b1 = [c.sb(f"e_b1_{u}", [D, C]) for u in range(2)]
    b2 = c.sb("e_b2", [ROWS, D])
    Hhi, Hlo = c.sb("e_Hhi", [D, T], R32), c.sb("e_Hlo", [D, T], R32)
    keys = c.sb("e_keys", [D, 2, E])
    rbias = c.sb("e_rb", [1, E])
    kr = c.sb("e_kr", [D, E])
    ksq = c.sb("e_ksq", [D, E])
    crow = c.sb("e_crow", [128, E])
    nones = c.sb("e_nones", [D, D])
    hsq = [c.sb(f"e_hsq{u}", [D, N]) for u in range(2)]
    lg = c.sb("e_lg", [128, NT, E])
    m8 = c.sb("e_m8", [128, NT, 8])
    gt = c.sb("e_gt", [128, NT, E])
    eq = c.sb("e_eq", [128, NT, E])
    run = c.sb("e_run", [128, NT, E])
    zero = c.sb("e_zero", [128, E])
    left = c.sb("e_left", [128, NT])
    gate = c.sb("e_gate", [128, NT, E])
    gpart = c.sb("e_gpart", [128, NT, E], BF16)
    gate3 = c.sb("e_gate3", [128, NT, ROWS])
    gT = [c.sb(f"e_gT{j}", [ROWS, N]) for j in range(2)]
    gT3 = c.sb("e_gT3", [ROWS, T], BF16)
    pick = c.sb("e_pick", [ROWS, E])
    sel = [c.sb(f"e_sel{u}", [ROWS, D], BF16) for u in range(2)]
    hh = [c.sb(f"e_hh{j}", [D, C, N]) for j in range(2)]
    hg = [c.sb(f"e_hg{j}", [D, C, N]) for j in range(2)]
    ghi = [c.sb(f"e_ghi{j}", [D, C, N], R32) for j in range(2)]
    glo = [c.sb(f"e_glo{j}", [D, C, N], R32) for j in range(2)]
    psH = [c.ps(f"e_psH{j}") for j in range(2)]
    psR = [c.ps(f"e_psR{j}") for j in range(2)]
    psY = [c.ps(f"e_psY{b}") for b in range(NB)]
    names = ("w", "we0", "we1", "k", "crow", "hsq", "l", "lg", "gate", "gt", "gTe", "b2", "z", "h", "hh", "g", "hg",
             "ghi", "glo", "glo3", "whi", "wlo", "hhi", "hlo", "y", "ksq", "tab")
    s = {k: c.sem("e_s_" + k) for k in names}
    s_ch, s_act = c.sem("e_s_dve"), c.sem("e_s_act")
    with nc.Block() as block:
        @block.sync
        def _(sp):
            sp.dma_start(keys[:, :, :], c.ins["keys_rw"]).then_inc(s["w"], 16)
            sp.dma_start(rbias[:, :], c.ins["rb"]).then_inc(s["w"], 16)
            sp.wait_ge(s["z"], 1)
            for n in range(3):
                sp.dma_start(b2[32 * n:32 * n + E, :], c.ins["b2_moe"]).then_inc(s["w"], 16)
            sp.dma_start(c.tables_1, c.ins["tables_1_in"]).then_inc(s["tab"], 16)

            def load_pair(ep):
                for u in range(2):
                    e = ep * 2 + u
                    c.wait_apart(sp, s["y"], (e - 1) * NB)
                    sp.dma_start(raw[u][:, 0, :], c.ins["w1_moe"][e]).then_inc(s[f"we{u}"], 16)
                    sp.dma_start(raw[u][:, 1, :], c.ins["w2_moe"][e]).then_inc(s[f"we{u}"], 16)
                    sp.dma_start(b1[u][:, :], c.ins["b1_moe"][e]).then_inc(s[f"we{u}"], 16)
            load_pair(0)
            with sp.Fori(1, E // 2) as ep:
                load_pair(ep)
            sp.wait_ge(s["tab"], 16)

        @block.tensor
        def _(pe):
            pe.wait_ge(s["k"], 1)
            pe.matmul(psR[0][:, 0:E], nones[:, :], ksq[:, :], start=True, stop=False)
            pe.matmul(psR[0][:, 0:E], c.ones[0:1, :], rbias[:, :], start=False, stop=True).then_inc(s["crow"], 1)
            for b in range(NB):
                u = b % 2
                pe.wait_ge(s["hsq"], b + 1)
                wait(pe, s["lg"], b - 1)
                if b == 0:
                    pe.wait_ge(s["ksq"], 1)
                for t in range(TILES):
                    tt = slice(128 * t, 128 * t + 128)
                    o = psR[u][:, E * t:E * t + E]
                    pe.matmul(o, c.H[:, b * N + 128 * t:b * N + 128 * t + 128], kr[:, :], start=True, stop=False)
                    last = pe.matmul(o, hsq[u][:, tt], nones[:, 0:E], start=False, stop=True)
                last.then_inc(s["l"], 1)
            pe.wait_ge(s["gate"], 1)
            pe.wait_ge(s["w"], 80)
            for b in range(NB + 1):
                if b < NB:
                    wait(pe, s["gTe"], b - 1)
                    for t in range(TILES):
                        last = pe.transpose(psR[b % 2][0:ROWS, 128 * t:128 * t + 128], gate3[:, b * TILES + t, :],
                                            c.ident[:, :])
                    last.then_inc(s["gt"], 1)
                if b:
                    pe.wait_ge(s["gTe"], b)
                    pe.matmul(psY[b - 1][:, :], b2[:, :], gT[(b - 1) % 2][:, :], start=True, stop=False,
                              skip_group_check=True).then_inc(s["b2"], 1)

            def split_product(out, hi, lo, mov_hi, mov_lo, start, stop):
                pe.matmul(out, hi, mov_hi, start=start, stop=False, skip_group_check=True)
                pe.matmul(out, hi, mov_lo, start=False, stop=False, skip_group_check=True)
                return pe.matmul(out, lo, mov_hi, start=False, stop=stop, skip_group_check=True)

            def hidden(e, u, b, n):
                if b == 0:
                    pe.wait_ge(s["whi"], e + 1)
                    pe.wait_ge(s["wlo"], e + 1)
                for j in range(C):
                    wait(pe, s["hh"], n * C + j - 1)
                    split_product(psH[j % 2][:, :], whi[u][:, 0, j * D:(j + 1) * D], wlo[u][:, 0, j * D:(j + 1) * D],
                                  Hhi[:, b * N:(b + 1) * N], Hlo[:, b * N:(b + 1) * N], True, True).then_inc(s["h"], 1)
                    if j == 1:
                        wait(pe, s["hg"], (n - 1) * C)
                        pe.matmul(psR[b % 2][:, :], sel[u][:, :], gT3[:, b * N:(b + 1) * N], start=True,
                                  stop=True).then_inc(s["g"], 1)

            def outputs(u, b, n, end=False):
                for j in range(C):
                    pe.wait_ge(s["ghi"], n * C + j + 1)
                    if j < C - 1:
                        pe.wait_ge(s["glo"], n * (C - 1) + j + 1)
                    else:
                        pe.wait_ge(s["glo3"], n + 1)
                    last = split_product(psY[b][:, :], whi[u][:, 1, j * D:(j + 1) * D], wlo[u][:, 1, j * D:(j + 1) * D],
                                         ghi[b % 2][:, j, :], glo[b % 2][:, j, :], False, end and j == C - 1)
                last.then_inc(s["y"], 1)

            def expert_pair(ep):
                for u in range(2):
                    for b in range(NB):
                        e = ep * 2 + u
                        n = e * NB + b
                        hidden(e, u, b, n)
                        if not (isinstance(n, int) and n == 0):
                            outputs(u if b else 1 - u, (b - 1) % NB, n - 1, isinstance(n, int) and n > (E - 1) * NB)
            pe.wait_ge(s["hlo"], 1)
            expert_pair(0)
            with pe.Fori(1, E // 2 - 1) as ep:
                expert_pair(ep)
            expert_pair(E // 2 - 1)
            outputs(1, NB - 1, E * NB - 1, True)

        @block.scalar
        def _(act):
            act.activation(Hhi[:, :], c.H[:, :], ACT.Copy).then_inc(s["hhi"], 1)
            for b in range(NB):
                wait(act, s["l"], b - 1)
                act.activation(hsq[b % 2][:, :], c.H[:, b * N:(b + 1) * N], ACT.Square).then_inc(s["hsq"], 1)
            def split_weights(u, e):
                act.wait_ge(s[f"we{u}"], (e // 2 + 1) * 48)
                wait(act, s["y"], (e - 1) * NB)
                act.activation(whi[u][:, :, :], raw[u][:, :, :], ACT.Copy).then_inc(s["whi"], 1)
            split_weights(0, 0)
            act.wait_ge(s["lg"], NB + 1)
            act.activation(gate[:, :, :], lg[:, :, :], ACT.Exp).then_inc(s_act, 1)
            for b in range(NB):
                act.wait_ge(s["gt"], b + 1)
                wait(act, s["b2"], b - 1)
                act.activation(gT[b % 2][:, :], psR[b % 2][0:ROWS, :], ACT.Copy)
                act.activation(gT3[:, b * N:(b + 1) * N], psR[b % 2][0:ROWS, :], ACT.Copy).then_inc(s["gTe"], 1)
            def expert_pair(ep):
                for u in range(2):
                    e = ep * 2 + u
                    for b in range(NB):
                        n = e * NB + b
                        for j in range(C):
                            wait(act, s["hg"], (n - 2) * C + j + 1)
                            act.wait_ge(s["h"], n * C + j + 1)
                            act.activation(hh[b % 2][:, j, :], psH[j % 2][:, :], ACT.Gelu,
                                           bias=b1[u][:, j:j + 1]).then_inc(s["hh"], 1)
                        wait(act, s["y"], n - 1)
                        for j in range(C):
                            act.wait_ge(s["hg"], n * C + j + 1)
                            act.activation(ghi[b % 2][:, j, :], hg[b % 2][:, j, :], ACT.Copy).then_inc(s["ghi"], 1)
                        if b == 2 and not (isinstance(e, int) and e == E - 1):
                            split_weights(1 - u, e + 1)
            expert_pair(0)
            with act.Fori(1, E // 2 - 1) as ep:
                expert_pair(ep)
            expert_pair(E // 2 - 1)

        @block.gpsimd
        def _(pool):
            pool.memset(b2[:, :], 0.0).then_inc(s["z"], 1)
            pool.wait_ge(s["hhi"], 1)
            pool.tensor_tensor(Hlo[:, :], c.H[:, :], Hhi[:, :], ALU.subtract).then_inc(s["hlo"], 1)

            def expert_pair(ep):
                for u in range(2):
                    for b in range(NB):
                        n = (ep * 2 + u) * NB + b
                        wait(pool, s["y"], n - 1)
                        for j in range(C - 1):
                            pool.wait_ge(s["ghi"], n * C + j + 1)
                            pool.tensor_tensor(glo[b % 2][:, j, :], hg[b % 2][:, j, :], ghi[b % 2][:, j, :],
                                               ALU.subtract).then_inc(s["glo"], 1)
            expert_pair(0)
            with pool.Fori(1, E // 2) as ep:
                expert_pair(ep)

        @block.vector
        def _(dve):
            ch = Chain(dve, s_ch)
            dve.wait_ge(s["w"], 80)
            ch.inc(dve.memset(gate3[:, :, :], 0.0))
            ch.inc(dve.memset(nones[:, :], -1.0))
            ch.inc(dve.memset(zero[:, :], 0.0))
            ch.inc(dve.scalar_tensor_tensor(out=kr[:, :], in0=keys[:, 0, :], scalar=2.0, in1=keys[:, 1, :], op0=ALU.mult,
                                            op1=ALU.add))
            dve.tensor_tensor(ksq[:, :], keys[:, 0, :], keys[:, 0, :], ALU.mult).then_inc(s["k"], 1)
            dve.wait_ge(s["crow"], 1)
            dve.tensor_copy(crow[:, :], psR[0][:, 0:E]).then_inc(s["ksq"], 1)
            dve.wait_ge(s["ksq"], 1)
            ch.link(dve.tensor_tensor(pick[:, :], c.ident[0:ROWS, 0:E], c.ident[0:ROWS, 32:32 + E], ALU.add))
            ch.link(dve.tensor_tensor(pick[:, :], pick[:, :], c.ident[0:ROWS, 64:64 + E], ALU.add))

            def split_weights(u, e):
                dve.wait_ge(s["whi"], e + 1)
                dve.tensor_scalar(sel[u][:, :], c.ones[0:ROWS, :], pick[:, ds(e, 1)], None, ALU.mult)
                dve.tensor_tensor(wlo[u][:, :, :], raw[u][:, :, :], whi[u][:, :, :], ALU.subtract).then_inc(s["wlo"], 1)
            split_weights(0, 0)
            for b in range(NB):
                dve.wait_ge(s["l"], b + 1)
                dve.tensor_tensor(lg[:, b * TILES:(b + 1) * TILES, :],
                                  psR[b % 2][:, 0:TILES * E].rearrange("p (t e) -> p t e", e=E),
                                  crow[:, :].unsqueeze(1).to_broadcast([128, TILES, E]), ALU.add).then_inc(s["lg"], 1)
            wait(dve, s["lg"], NB)
            for t in range(NT):
                m = ch.inc(dve.max(m8[:, t, :], lg[:, t, :]))
            ch.wait(m)
            kth = m8[:, :, TOPK - 1].unsqueeze(2).to_broadcast([128, NT, E])
            ch.inc(dve.tensor_tensor(gt[:, :, :], lg[:, :, :], kth, ALU.is_gt))
            ch.link(dve.tensor_tensor(eq[:, :, :], lg[:, :, :], kth, ALU.is_equal))
            ch.link(dve.tensor_reduce(left[:, :], gt[:, :, :], AX_X, ALU.add))
            ch.link(dve.tensor_scalar(left[:, :], left[:, :], -1.0, float(TOPK), ALU.mult, ALU.add))
            for t in range(NT):
                m = ch.inc(dve.tensor_tensor_scan(run[:, t, :], eq[:, t, :], zero[:, :], 0.0, ALU.add, ALU.add))
            ch.wait(m)
            ch.link(dve.tensor_tensor(run[:, :, :], run[:, :, :], left[:, :].unsqueeze(2).to_broadcast([128, NT, E]),
                                      ALU.is_le))
            ch.link(dve.tensor_tensor(run[:, :, :], run[:, :, :], eq[:, :, :], ALU.mult))
            ch.link(dve.tensor_tensor(gt[:, :, :], gt[:, :, :], run[:, :, :], ALU.add))
            dve.tensor_tensor(lg[:, :, :], lg[:, :, :], m8[:, :, 0].unsqueeze(2).to_broadcast([128, NT, E]),
                              ALU.subtract).then_inc(s["lg"], 1)
            dve.wait_ge(s_act, 1)
            ch.link(dve.tensor_tensor(gate[:, :, :], gate[:, :, :], gt[:, :, :], ALU.mult))
            ch.link(dve.tensor_reduce(left[:, :], gate[:, :, :], AX_X, ALU.add))
            ch.link(dve.reciprocal(left[:, :], left[:, :]))
            ch.link(dve.tensor_tensor(gate[:, :, :], gate[:, :, :], left[:, :].unsqueeze(2).to_broadcast([128, NT, E]),
                                      ALU.mult))
            for n in range(3):
                ch.link(dve.tensor_copy(gpart[:, :, :], gate[:, :, :]))
                last = dve.tensor_copy(gate3[:, :, 32 * n:32 * n + E], gpart[:, :, :])
                if n < 2:
                    ch.inc(last)
                    ch.link(dve.tensor_tensor(gate[:, :, :], gate[:, :, :], gpart[:, :, :], ALU.subtract))
            last.then_inc(s["gate"], 1)
            def expert_pair(ep):
                for u in range(2):
                    e = ep * 2 + u
                    for b in range(NB):
                        n = e * NB + b
                        dve.wait_ge(s["g"], n + 1)
                        wait(dve, s["glo"], (n - 1) * (C - 1))
                        wait(dve, s["glo3"], n - 1)
                        for j in range(C):
                            dve.wait_ge(s["hh"], n * C + j + 1)
                            dve.tensor_tensor(hg[b % 2][:, j, :], hh[b % 2][:, j, :], psR[b % 2][:, :],
                                              ALU.mult).then_inc(s["hg"], 1)
                        dve.wait_ge(s["ghi"], n * C + C)
                        wait(dve, s["y"], n - 1)
                        dve.tensor_tensor(glo[b % 2][:, C - 1, :], hg[b % 2][:, C - 1, :], ghi[b % 2][:, C - 1, :],
                                          ALU.subtract).then_inc(s["glo3"], 1)
                        if b == 2 and not (isinstance(e, int) and e == E - 1):
                            split_weights(1 - u, e + 1)
            expert_pair(0)
            with dve.Fori(1, E // 2 - 1) as ep:
                expert_pair(ep)
            expert_pair(E // 2 - 1)
            for b in range(NB):
                dve.wait_ge(s["y"], (E - 1) * NB + b + 1)
                dve.scalar_tensor_tensor(out=c.X[:, b * N:(b + 1) * N], in0=psY[b][:, :], scalar=c.mods[:, 0, 5, b:b + 1],
                                         in1=c.X[:, b * N:(b + 1) * N], op0=ALU.mult, op1=ALU.add)


def causal_attention(c):
    nc = c.nc
    DQ, UN = 32, 2
    LOWEST = float(np.finfo(np.float32).min)
    wqk = c.sb("a_wqk", [D, 2, DQ])
    wvd = c.sb("a_wvd", [DQ, D])
    wvu = c.sb("a_wvu", [DQ, D])
    wv = c.sb("a_wv", [D, D])
    hst = [c.sb(f"a_hst{u}", [D, N]) for u in range(UN)]
    qk = [c.sb(f"a_qk{u}", [DQ, 2, N]) for u in range(UN)]
    v = [c.sb(f"a_v{u}", [128, TILES, D]) for u in range(UN)]
    sc = [c.sb(f"a_sc{u}", [128, N]) for u in range(UN)]
    zz = [c.sb(f"a_zz{u}", [128, N]) for u in range(UN)]
    pr = [c.sb(f"a_pr{u}", [128, N]) for u in range(UN)]
    pT = [c.sb(f"a_pT{u}", [128, TILES, 128]) for u in range(UN)]
    mx = [c.sb(f"a_mx{u}", [128, 1]) for u in range(UN)]
    sm = [c.sb(f"a_sm{u}", [128, 1]) for u in range(UN)]
    psA = [c.ps(f"a_psA{u}") for u in range(UN)]
    psS = [c.ps(f"a_psS{u}") for u in range(UN)]
    psT = [c.ps(f"a_psT{u}") for u in range(UN)]
    psO = [c.ps(f"a_psO{u}") for u in range(UN)]
    s = {k: c.sem("a_s_" + k) for k in ("w", "wv", "wve", "h", "qk", "qke", "v", "ve", "sc", "z", "mx", "e", "pr", "t", "te",
                                        "o", "x")}
    s_ch = c.sem("a_s_dve")
    with nc.Block() as block:
        @block.sync
        def _(sp):
            sp.dma_start(wqk[:, :, :], c.ins["w_qk1"]).then_inc(s["w"], 16)
            sp.dma_start(wvd[:, :], c.ins["w_vdT"]).then_inc(s["w"], 16)
            sp.dma_start(wvu[:, :], c.ins["w_vu"]).then_inc(s["w"], 16)

        @block.tensor
        def _(pe):
            pe.wait_ge(s["w"], 48)
            pe.matmul(psA[0][:, 0:D], wvd[:, :], wvu[:, :], start=True, stop=True).then_inc(s["wv"], 1)
            pe.wait_ge(s["wve"], 1)
            for pair in range(NB // UN):
                it = pair * UN
                for j in range(2):
                    for u in range(UN):
                        pe.wait_ge(s["h"], it + u + 1)
                        if j == 0:
                            wait(pe, s["ve"], it)
                        else:
                            wait(pe, s["qke"], 2 * (it + u) + 1 - u)
                            pe.wait_ge(s["qke"], 2 * it + 1 + u)
                        pe.matmul(psA[u][0:DQ, :], wqk[:, j, :], hst[u][:, :], start=True, stop=True).then_inc(s["qk"], 1)
                for u in range(UN):
                    pe.wait_ge(s["qke"], 2 * it + 3 + u)
                    for t in range(TILES):
                        last = pe.matmul(psA[u][:, 128 * t:128 * t + 128], hst[u][:, 128 * t:128 * t + 128], wv[:, :],
                                         start=True, stop=True)
                    last.then_inc(s["v"], 1)
                def attend(t, u):
                    if t == 0:
                        wait(pe, s["x"], it)
                        pe.wait_ge(s["ve"], it + u + 1)
                    pe.wait_ge(s["pr"], it * TILES + UN * t + u + 1)
                    wait(pe, s["te"], it * TILES + UN * t)
                    for k in range(TILES):
                        kk = slice(128 * k, 128 * k + 128)
                        last = pe.transpose(psT[u][:, kk], pr[u][:, kk], c.ident[:, :])
                    last.then_inc(s["t"], 1)
                    pe.wait_ge(s["te"], it * TILES + UN * t + u + 1)
                    for k in range(TILES):
                        last = pe.matmul(psO[u][:, 128 * t:128 * t + 128], v[u][:, k, :], pT[u][:, k, :],
                                         start=(k == 0), stop=(k == TILES - 1))
                    last.then_inc(s["o"], 1)
                for t in range(TILES + 1):
                    for u in range(UN):
                        if t < TILES:
                            wait(pe, s["z"], it * TILES + UN * t)
                            pe.matmul(psS[u][:, :], qk[u][:, 0, 128 * t:128 * t + 128], qk[u][:, 1, :], start=True,
                                      stop=True).then_inc(s["sc"], 1)
                    if t:
                        for u in range(UN):
                            attend(t - 1, u)

        @block.scalar
        def _(act):
            act.wait_ge(s["wv"], 1)
            act.activation(wv[:, :], psA[0][:, 0:D], ACT.Copy).then_inc(s["wve"], 1)
            for pair in range(NB // UN):
                it = pair * UN
                for u in range(UN):
                    wait(act, s["v"], it)
                    act.activation(hst[u][:, :], c.H[:, ds((it + u) * N, N)], ACT.Copy).then_inc(s["h"], 1)
                for j in range(2):
                    for u in range(UN):
                        act.wait_ge(s["qk"], 2 * it + 2 * j + u + 1)
                        wait(act, s["sc"], it * TILES)
                        act.activation(qk[u][:, j, :], psA[u][0:DQ, :], ACT.Copy).then_inc(s["qke"], 1)
                for u in range(UN):
                    act.wait_ge(s["v"], it + u + 1)
                    wait(act, s["o"], it * TILES)
                    act.activation(v[u][:, :, :], psA[u][:, :].rearrange("p (t c) -> p t c", t=TILES),
                                   ACT.Copy).then_inc(s["ve"], 1)
                def evac(t, u):
                    n = it * TILES + UN * t
                    act.wait_ge(s["t"], n + u + 1)
                    wait(act, s["o"], n)
                    act.activation(pT[u][:, :, :], psT[u][:, :].rearrange("p (t c) -> p t c", t=TILES),
                                   ACT.Copy).then_inc(s["te"], 1)
                for t in range(TILES + 1):
                    for u in range(UN):
                        if t:
                            evac(t - 1, u)
                        if t < TILES:
                            n = it * TILES + UN * t
                            act.wait_ge(s["mx"], n + u + 1)
                            wait(act, s["pr"], n)
                            act.activation(pr[u][:, :], sc[u][:, :], ACT.Exp, bias=mx[u][:, :],
                                           accum_out=sm[u][:, :]).then_inc(s["e"], 1)

        @block.vector
        def _(dve):
            for pair in range(NB // UN):
                it = pair * UN
                ch = Chain(dve, s_ch, 32, pair)
                for t in range(TILES):
                    n = it * TILES + UN * t
                    for u in range(UN):
                        dve.wait_ge(s["sc"], n + u + 1)
                        wait(dve, s["e"], n)
                        dve.scalar_tensor_tensor(out=sc[u][:, :], in0=psS[u][:, :], scalar=DQ ** -0.5,
                                                 in1=c.causal[:, t, :], op0=ALU.mult, op1=ALU.mult).then_inc(s["z"], 1)
                        dve.wait_ge(s["z"], n + u + 1)
                        ch.link(dve.tensor_scalar(zz[u][:, :], sc[u][:, :], 0.0, LOWEST, ALU.is_equal, ALU.mult))
                        ch.link(dve.tensor_tensor(sc[u][:, :], sc[u][:, :], zz[u][:, :], ALU.add))
                        ch.link(dve.tensor_reduce(mx[u][:, :], sc[u][:, :], AX_X, ALU.max))
                        dve.tensor_scalar(mx[u][:, :], mx[u][:, :], -1.0, None, ALU.mult).then_inc(s["mx"], 1)
                    for u in range(UN):
                        dve.wait_ge(s["e"], n + u + 1)
                        wait(dve, s["t"], n)
                        ch.link(dve.reciprocal(sm[u][:, :], sm[u][:, :]))
                        dve.tensor_scalar(pr[u][:, :], pr[u][:, :], sm[u][:, :], None, ALU.mult).then_inc(s["pr"], 1)
                for u in range(UN):
                    b = it + u
                    dve.wait_ge(s["o"], it * TILES + UN * (TILES - 1) + u + 1)
                    dve.scalar_tensor_tensor(out=c.X[:, ds(b * N, N)], in0=psO[u][:, :], scalar=c.mods[:, 1, 2, ds(b, 1)],
                                             in1=c.X[:, ds(b * N, N)], op0=ALU.mult, op1=ALU.add).then_inc(s["x"], 1)
                ch.end()


def finish(c, out):
    s_y, s_o = c.sem("o_s_y"), c.sem("o_s_out")
    with c.nc.Block() as block:
        @block.vector
        def _(dve):
            for b in range(NB):
                bb = slice(b * N, (b + 1) * N)
                dve.scalar_tensor_tensor(out=c.X[:, bb], in0=c.H[:, bb], scalar=c.mods[:, 1, 5, b:b + 1], in1=c.X[:, bb],
                                         op0=ALU.mult, op1=ALU.add).then_inc(s_y, 1)

        @block.sync
        def _(sp):
            for b in range(NB):
                sp.wait_ge(s_y, b + 1)
                sp.dma_start(out[:, b * N:(b + 1) * N], c.X[:, b * N:(b + 1) * N]).then_inc(s_o, 16)
            wait(sp, s_o, 16 * NB)


def windowed_layers(c):
    nc = c.nc
    DEPTH, HEADS, DH, WIN = 6, 16, 64, 32
    PAIRS, BLK = HEADS // 2, 64
    KEYS = WIN + BLK
    NBLK = N // BLK
    FF = 341
    CH = [(0, 128), (128, 128), (256, FF - 256)]
    ROUNDS = DEPTH * NB
    QKV = 3 * HEADS * DH
    UP, UT, UA = 24, 16, 2 * NBLK

    w_qkv = c.sb("w_qkv", [D, 2, QKV])
    w_o = c.sb("w_o", [D, PAIRS, D])
    w_1 = c.sb("w_1", [D, 2 * FF])
    w_2 = c.sb("w_2", [D, 3, D])
    cols = c.sb("w_cols", [D, 9])
    xs = c.sb("w_xs", [D, N])
    raw = [c.sb(f"w_raw{j}", [128, 4, 512]) for j in range(2)]
    sq = c.sb("w_sq", [128, 4, 512])
    qr = c.sb("w_qr", [128, 4, 512])
    t2 = c.sb("w_t2", [128, 512])
    nrm = [c.sb(f"w_nrm{j}", [128, 4, 32]) for j in range(2)]
    qb = [c.sb(f"w_qb{j}", [128, PAIRS, 2, 2, BLK]) for j in range(2)]
    kT = c.sb("w_kT", [128, PAIRS, WIN + N])
    v = [c.tables_1[:, 1024 * t:1024 * (t + 1)] for t in range(3)] + [c.sb("w_v3", [128, HEADS * DH])]
    v_even = c.sb("w_v_even", [KEYS, HEADS * DH])
    pb = [c.sb(f"w_pb{j}", [128, PAIRS, KEYS + WIN * j]) for j in range(2)]
    mx = c.sb("w_mx", [128, PAIRS])
    sm = [c.sb(f"w_sm{j}", [128, PAIRS]) for j in range(2)]
    pT = c.sb("w_pT", [128, PAIRS, 128])
    oT = c.sb("w_oT", [128, PAIRS, N])
    xsf = c.sb("w_xsf", [D, N])
    yn = c.sb("w_yn", [128, TILES, D])
    xn = c.sb("w_xn", [D, N])
    gg = yn[:, :, :].rearrange("p t c -> p (t c)")
    hh = c.sb("w_hh", [D, 3, N])
    stats = c.sb("w_stats", [128, TILES, 6])
    mv = c.sb("w_mv", [128, TILES, 2])
    rs = c.sb("w_rs", [128, 3, TILES])
    tabs = c.sb("w_tabs", [128, DEPTH, 4, TILES, DH])
    scl = sq[:, 0:3, :].rearrange("p a b -> p (a b)").rearrange("p (l k d) -> p l k d", l=DEPTH, k=4)

    psP = [c.ps(f"w_psP{j}") for j in range(2)]
    psT = c.ps("w_psT")
    psA = c.ps("w_psA")
    psS = [c.ps(f"w_psS{j}") for j in range(2)]
    psO = c.ps("w_psO")
    psF = c.ps("w_psF")

    names = ("wa", "wf", "tab", "z", "xs", "p", "pe", "sr", "rn", "t1", "qr", "t", "te", "s", "x1", "e", "r", "pn", "pt",
             "pte", "ve", "av", "ot", "f", "xf", "xsf", "yn", "xn", "gg", "hh", "out", "scl")
    s = {k: c.sem("w_s_" + k) for k in names}
    s_norm, s_max, s_sum, s_f, s_pool = (c.sem("w_s_chain_" + k) for k in ("norm", "max", "sum", "tail", "pool"))

    def proj_use(kind, t, j):
        return 6 * t + (j if kind == "P" else 4 + j)

    ORDER = {
        "pe": """P2.0 P2.1 S0.0 At7.0- P2.2 P2.3 At7.1- T1.0 S0.1 S1.0 V2.0 T1.1 Av7.0- V2.1 Av7.1- T1.2 S1.1
            wo0- T1.3 At0.0 P3.0 wo1- T2.0 P3.1 P3.2 At0.1 S2.0 S2.1 P3.3 T2.1 Av0.0 Av0.1 At1.0 V3.0
            T2.2 S3.0 V3.1 Av1.0 At1.1 T2.3 tr- S3.1 P0.0+ Av1.1 T3.0 S4.0 At2.0 P0.1+ P0.2+ At2.1 S4.1
            back- P0.3+ Av2.0 Av2.1 g0- S5.0 V0.0+ T3.1 At3.0 a0- V0.1+ P1.0+ At3.1 Av3.0 g1- Av3.1
            At4.0 P1.1+ a1- T3.2 S5.1 At4.1 T3.3 g2- P1.2+ S6.0 T0.0+ Av4.0 Av4.1 S6.1 P1.3+ a2- S7.0
            At5.0 T0.1+ S7.1 At5.1 Av5.0 V1.0+ Av5.1 At6.0 T0.2+ w2- At6.1 V1.1+ Av6.0 Av6.1 T0.3+""",
        "act": """P2.0 P2.1 At7.0- P2.2 T1.0 At7.1- P2.3 T1.1 Xb0.0 Av7.1- V2.0 T1.2 V2.1 Xb1.0 T1.3 P3.0
            At0.0 P3.1 T2.0 P3.2 At0.1 P3.3 T2.1 Av0.1 T2.2 At1.0 tr- stage+ Xb2.0 V3.0 At1.1 T2.3 V3.1
            Av1.1 Xb3.0 P0.0+ At2.0 T3.0 P0.1+ At2.1 back- P0.2+ Xb4.0 g0- P0.3+ At3.0 V0.0+ Av2.1 V0.1+
            T3.1 At3.1 g1- Av3.1 At4.0 T3.2 P1.0+ T3.3 At4.1 g2- Xb5.0 P1.1+ Av4.1 P1.2+ T0.0+ Xb6.0
            At5.0 P1.3+ At5.1 T0.1+ Av5.1 Xb7.0 At6.0 At6.1 T0.2+ V1.0+ V1.1+ Av6.1 T0.3+""",
        "dve": """Xa0.0 Rb1.2 Rs2.0 Rs2.1 Xa0.1 Rs2.2 Xa1.0 Rb1.3 Rs2.3 Xb0.0 Ra2.0 Rb2.0 Xa1.1 Rb2.1 Xb1.0
            Rb2.2 wo- Rb2.3 Rs3.0 Rs3.1 Xa2.0 Xa2.1 Rs3.2 Rs3.3 Ra3.0 Rb3.0 Rb3.1 Xa3.0 Xb2.0 Xa3.1 tr-
            Xa4.0 Xa4.1 Xb3.0 Rs0.0+ Rb3.2 Rs0.1+ Xb4.0 Rs0.2+ Rb3.3 a0- Rs0.3+ Ra0.0+ Rb0.0+ Xa5.0 a1-
            Rb0.1+ Xa5.1 Rb0.2+ Xa6.0 Xb5.0 Rs1.0+ Xa6.1 Rs1.1+ a2- Xb6.0 Rb0.3+ Xa7.0 Xa7.1 Rs1.2+
            Rs1.3+ Xb7.0 w2- Ra1.0+ Rb1.0+ Rb1.1+""",
        "pool": """Rb1.2 Rb1.3 Xb0.0 Rb2.0 Rb2.1 Xb1.0 Rb2.2 Rb2.3 Rb3.0 Xb2.0 Rb3.1 Xb3.0 Xb4.0 Rb3.2 Rb3.3
            Rb0.0+ Rb0.1+ Xb5.0 Rb0.2+ Xb6.0 Rb0.3+ Xb7.0 Rb1.0+ Rb1.1+""",
    }

    def unit(word):
        dr = {"+": 1, "-": -1}.get(word[-1], 0)
        word = word.rstrip("+-")
        if "." in word:
            at = next(n for n, ch in enumerate(word) if ch.isdigit() and word[n + 1] == ".")
            return word[:at], int(word[at]), int(word[at + 2]), dr
        return ("stage", 0, 0, dr) if word == "stage" else ("F", word, 0, dr)

    order = {name: [unit(word) for word in text.split()] for name, text in ORDER.items()}

    def turns(eng, name, step):
        def turn(i):
            for kind, k, j, dr in order[name]:
                r = i + dr
                if not isinstance(i, int) or 0 <= r < ROUNDS:
                    step(kind, k, j, r, r % NB, r // NB)
        for i in range(-1, 2):
            turn(i)
        with eng.Fori(2, ROUNDS - 1) as i:
            turn(i)
        turn(ROUNDS - 1)
        turn(ROUNDS)

    def make_tables(eng, of_layers):
        for layer in of_layers:
            for k, base in enumerate((c.rope_cos_q, c.rope_sin_q, c.rope_cos_k, c.rope_sin_k)):
                eng.tensor_tensor(tabs[:, layer, k, :, :], base[:, :, :],
                                  scl[:, layer, ds(k, 1), :].to_broadcast([128, TILES, DH]), ALU.mult).then_inc(s["tab"], 1)

    with nc.Block() as block:
        @block.sync
        def _(sp):
            sp.dma_start(sq[:, 0:3, :].rearrange("p a b -> p (a b)"),
                         c.ins["qk_scales"].to_broadcast([128, DEPTH * 4 * DH])).then_inc(s["scl"], 16)

            def load_qkv(layer):
                c.wait_apart(sp, s["p"], (layer - 1) * (NB * UP))
                sp.dma_start(w_qkv[:, ds(layer % 2, 1), :], c.ins["w_qkv1"][layer]).then_inc(s["wa"], 16)

            def load_tail(layer):
                c.wait_apart(sp, s["out"], layer * NB)
                sp.dma_start(w_o[:, :, :], c.ins["w_o1"][layer]).then_inc(s["wf"], 16)
                sp.dma_start(w_1[:, :], c.ins["w_ff1"][layer]).then_inc(s["wf"], 16)
                sp.dma_start(w_2[:, :, :], c.ins["w_ff2"][layer]).then_inc(s["wf"], 16)
                sp.dma_start(cols[:, :], c.ins["cols_w"][layer]).then_inc(s["wf"], 16)

            def rounds_of(layer, more):
                for b in range(NB):
                    r = layer * NB + b
                    for t in range(TILES):
                        c.wait_apart(sp, s["pe"], r * UP + proj_use("V", t, 1) + 1)
                        c.wait_apart(sp, s["av"], r * UA + 4 * t - 2)
                        sp.dma_start(v_even[WIN:KEYS, :], v[t][0:BLK, :]).then_inc(s["ve"], 16)
                        if t:
                            sp.dma_start(v_even[0:WIN, :], v[t - 1][128 - WIN:128, :]).then_inc(s["ve"], 16)
                    if b == 0:
                        if more:
                            load_qkv(layer + 1)
                        if not isinstance(layer, int) or layer > 0:
                            load_tail(layer)
            load_qkv(0)
            load_tail(0)
            sp.wait_ge(s["z"], 3)
            rounds_of(0, True)
            with sp.Fori(1, DEPTH - 1) as layer:
                rounds_of(layer, True)
            rounds_of(DEPTH - 1, False)

        VE = 16 * (2 * TILES - 1)

        def mm_tail(pe, f, r, layer):
            if f[:2] == "wo":
                half = int(f[2])
                if half == 0:
                    pe.wait_ge(s["wf"], (layer + 1) * 64)
                    pe.wait_ge(s["ot"], (r + 1) * NBLK)
                    wait(pe, s["out"], r)
                for pair in range(4 * half, 4 * half + 4):
                    last = pe.matmul(psF[:, :], w_o[:, pair, :], oT[:, pair, :], start=(pair == 0),
                                     stop=(pair == PAIRS - 1), skip_group_check=True)
                if half == 0:
                    return
            elif f == "tr":
                pe.wait_ge(s["xsf"], r + 1)
                for t in range(TILES):
                    last = pe.transpose(psF[:, 128 * t:128 * (t + 1)], xsf[:, 128 * t:128 * (t + 1)], c.ident[:, :])
            elif f == "back":
                pe.wait_ge(s["yn"], r + 1)
                for t in range(TILES):
                    last = pe.transpose(psF[:, 128 * t:128 * (t + 1)], yn[:, t, :], c.ident[:, :])
            elif f[0] in "ga":
                k = int(f[1])
                at, m = CH[k]
                if f[0] == "g":
                    pe.wait_ge(s["xn"], r + 1)
                    wait(pe, s["hh"], 3 * r + k)
                    at += FF
                else:
                    pe.wait_ge(s["gg"], 3 * r + k + 1)
                last = pe.matmul(psF[0:m, :], w_1[:, at:at + m], xn[:, :], start=True, stop=True)
            else:
                pe.wait_ge(s["hh"], 3 * r + 3)
                for k, (at, m) in enumerate(CH):
                    last = pe.matmul(psF[:, :], w_2[0:m, k, :], hh[0:m, k, :], start=(k == 0), stop=(k == 2))
            last.then_inc(s["f"], 1)

        @block.tensor
        def _(pe):
            def step(kind, k, j, r, b, layer):
                if kind in "PV":
                    u = proj_use(kind, k, j)
                    if u == 0:
                        pe.wait_ge(s["wa"], (layer + 1) * 16)
                        pe.wait_ge(s["xs"], r + 1)
                    wait(pe, s["pe"], r * UP + u - 1)
                    at = 512 * (j if kind == "P" else 4 + j)
                    pe.matmul(psP[u % 2][:, :], xs[:, 128 * k:128 * (k + 1)],
                              w_qkv[:, ds(layer % 2, 1), at:at + 512], start=True, stop=True).then_inc(s["p"], 1)
                elif kind == "T":
                    wait(pe, s["te"], r * UT + 4 * k + j)
                    pe.wait_ge(s["qr"], r * UT + 4 * k + j + 1)
                    for q in range(4):
                        last = pe.transpose(psT[:, 128 * q:128 * (q + 1)], qr[:, j, 128 * q:128 * (q + 1)], c.ident[:, :])
                    last.then_inc(s["t"], 1)
                elif kind == "S":
                    if k % 2 == 0 and j == 0:
                        pe.wait_ge(s["te"], r * UT + 4 * (k // 2) + 4)
                    wait(pe, s["x1"], r * UA + 2 * (k - 1) + j + 1)
                    pe.matmul(psS[j][:, 0:4 * KEYS], c.ident_bf[:, :], c.band_bf[:, min(k, 1), :], start=True, stop=False,
                              skip_group_check=True)
                    for q in range(4):
                        last = pe.matmul(psS[j][:, q * KEYS:(q + 1) * KEYS], qb[(k // 2) % 2][:, 4 * j + q, k % 2, :, :],
                                         kT[:, 4 * j + q, BLK * k:BLK * k + KEYS], start=False, stop=True,
                                         skip_group_check=True)
                    last.then_inc(s["s"], 1)
                elif kind == "At":
                    rows = KEYS + WIN * (k % 2)
                    pe.wait_ge(s["pn"], r * NBLK + k + 1)
                    wait(pe, s["pte"], r * UA + 2 * k + j)
                    for q in range(4):
                        last = pe.transpose(psA[0:rows, 128 * q:128 * (q + 1)], pb[k % 2][:, 4 * j + q, :], c.ident[:, :])
                    last.then_inc(s["pt"], 1)
                elif kind == "Av":
                    t, odd = k // 2, k % 2
                    rows = KEYS + WIN * odd
                    if odd:
                        pe.wait_ge(s["pe"], r * UP + proj_use("V", t, 1) + 1)
                        vals = v[t]
                    else:
                        pe.wait_ge(s["ve"], r * VE + 16 * (2 * t + 1))
                        vals = v_even
                    if j == 0:
                        wait(pe, s["ot"], r * NBLK + k)
                    pe.wait_ge(s["pte"], r * UA + 2 * k + j + 1)
                    for pair in range(4 * j, 4 * j + 4):
                        for h in range(2):
                            last = pe.matmul(psO[64 * h:64 * h + 64, BLK * pair:BLK * (pair + 1)],
                                             vals[0:rows, (2 * pair + h) * DH:(2 * pair + h + 1) * DH],
                                             pT[0:rows, pair, BLK * h:BLK * (h + 1)], start=True, stop=True)
                    last.then_inc(s["av"], 1)
                else:
                    mm_tail(pe, k, r, layer)
            pe.wait_ge(s["z"], 3)
            turns(pe, "pe", step)

        @block.scalar
        def _(act):
            def step(kind, k, j, r, b, layer):
                if kind == "stage":
                    wait(act, s["p"], r * UP)
                    c.wait_apart(act, s["out"], r - 2)
                    act.activation(xs[0:64, :], c.H[0:64, ds(b * N, N)], ACT.Copy)
                    act.activation(xs[64:128, 1:N], c.H[64:128, ds(b * N, N - 1)], ACT.Copy).then_inc(s["xs"], 1)
                elif kind == "P":
                    u = proj_use("P", k, j)
                    wait(act, s["qr"], r * UT + 4 * (k - 2) + j + 1)
                    wait(act, s["sr"], r * UT + 4 * (k - 1) + j + 1)
                    act.wait_ge(s["p"], r * UP + u + 1)
                    act.activation(raw[k % 2][:, j, :], psP[u % 2][:, :], ACT.Copy)
                    act.activation(sq[:, j, :], psP[u % 2][:, :], ACT.Square).then_inc(s["pe"], 1)
                elif kind == "V":
                    u = proj_use("V", k, j)
                    wait(act, s["av"], (r - 1) * UA + 4 * k + 4)
                    if k == TILES - 1:
                        wait(act, s["ve"], r * VE)
                    else:
                        wait(act, s["ve"], (r - 1) * VE + 16 * (2 * k + 3))
                    act.wait_ge(s["p"], r * UP + u + 1)
                    act.activation(v[k][:, 512 * j:512 * (j + 1)], psP[u % 2][:, :], ACT.Copy).then_inc(s["pe"], 1)
                elif kind == "T":
                    act.wait_ge(s["t"], r * UT + 4 * k + j + 1)
                    src = psT[:, :].rearrange("p (a b) -> p a b", a=4)
                    if j < 2:
                        for h in range(2):
                            rows = slice(64 * h, 64 * h + 64)
                            last = act.activation(qb[k % 2][rows, 4 * j:4 * j + 4, :, h, :],
                                                  src[rows].rearrange("p a (b q) -> p a b q", b=2), ACT.Copy)
                    else:
                        last = act.activation(kT[:, 4 * (j - 2):4 * (j - 2) + 4, WIN + 128 * k:WIN + 128 * (k + 1)],
                                              src, ACT.Copy)
                    last.then_inc(s["te"], 1)
                elif kind == "Xb":
                    act.wait_ge(s["x1"], r * UA + 2 * k + 2)
                    p = pb[k % 2][:, :, WIN * (k % 2):]
                    act.activation(p, p, ACT.Exp, scale=8.0).then_inc(s["e"], 1)
                elif kind == "At":
                    rows = KEYS + WIN * (k % 2)
                    wait(act, s["av"], r * UA + 2 * (k - 1) + j + 1)
                    act.wait_ge(s["pt"], r * UA + 2 * k + j + 1)
                    act.activation(pT[0:rows, 4 * j:4 * j + 4, :], psA[0:rows, :].rearrange("p (a b) -> p a b", a=4),
                                   ACT.Copy).then_inc(s["pte"], 1)
                elif kind == "Av":
                    if k == 0:
                        wait(act, s["f"], (r - 1) * 10 + 1)
                    act.wait_ge(s["av"], r * UA + 2 * k + 2)
                    act.activation(oT[:, :, BLK * k:BLK * (k + 1)], psO[:, :].rearrange("p (a b) -> p a b", b=BLK),
                                   ACT.Copy).then_inc(s["ot"], 1)
                elif k == "tr":
                    wait(act, s["yn"], r)
                    c.wait_apart(act, s["xf"], r + 1)
                    act.activation(xsf[0:64, :], c.H[0:64, ds(b * N, N)], ACT.Copy)
                    act.activation(xsf[64:128, 1:N], c.H[64:128, ds(b * N, N - 1)], ACT.Copy).then_inc(s["xsf"], 1)
                elif k == "back":
                    act.wait_ge(s["f"], r * 10 + 3)
                    act.activation(xn[:, :], psF[:, :], ACT.Identity, bias=cols[:, 1:2],
                                   scale=cols[:, 0:1]).then_inc(s["xn"], 1)
                else:
                    n, (at, m) = int(k[1]), CH[int(k[1])]
                    act.wait_ge(s["f"], r * 10 + 4 + 2 * n)
                    wait(act, s["hh"], 3 * r + n)
                    act.activation(gg[0:m, :], psF[0:m, :], ACT.Gelu, bias=cols[0:m, 5 + n:6 + n]).then_inc(s["gg"], 1)
            act.wait_ge(s["tab"], 4 * DEPTH)
            act.wait_ge(s["z"], 1)
            turns(act, "act", step)

        @block.vector
        def _(dve):
            def step(kind, k, j, r, b, layer):
                if kind == "Rs":
                    dve.wait_ge(s["pe"], r * UP + proj_use("P", k, j) + 1)
                    wait(dve, s["rn"], r * UT + 4 * (k - 2) + 4)
                    dve.tensor_reduce(nrm[k % 2][:, 0, 8 * j:8 * j + 8], sq[:, j, :].rearrange(
                        "p (h d) -> p h d", d=DH), AX_X, ALU.add).then_inc(s["sr"], 1)
                elif kind == "Ra":
                    nn = nrm[k % 2]
                    ch = Chain(dve, s_norm, 9, r * TILES + k)
                    dve.wait_ge(s["sr"], r * UT + 4 * k + 4)
                    rsqrt(dve, ch, nn[:, 1, :], nn[:, 0, :], nn[:, 2, :], nn[:, 3, :], 1e-24, ALU.max)
                    ch.end()
                elif kind == "Rb":
                    u = r * UT + 4 * k + j
                    xv = raw[k % 2][:, j, :].rearrange("p (h d) -> p h d", d=DH)
                    dve.tensor_tensor(xv, xv, nrm[k % 2][:, 1, 8 * j:8 * j + 8].unsqueeze(2).to_broadcast(
                        [128, 8, DH]), ALU.mult).then_inc(s["rn"], 1)
                    dve.wait_ge(s["rn"], u + 1)
                    wait(dve, s["t"], u - 3)
                    tab = tabs[:, ds(layer, 1), 2 * (j // 2), k, :].to_broadcast([128, 8, DH])
                    dve.tensor_tensor(qr[:, j, :].rearrange("p (h d) -> p h d", d=DH), xv, tab,
                                      ALU.mult).then_inc(s["t1"], 1)
                elif kind == "Xa":
                    wait(dve, s["pt"], r * UA + 2 * (k - 2) + 2)
                    ch = Chain(dve, s_max, 1, r * UA + 2 * k + j)
                    half = slice(4 * j, 4 * j + 4)
                    sc = psS[j][:, 0:4 * KEYS].rearrange("p (a b) -> p a b", a=4)
                    dve.wait_ge(s["s"], r * UA + 2 * k + j + 1)
                    ch.link(dve.tensor_reduce(mx[:, half], sc, AX_X, ALU.max))
                    dve.tensor_tensor(pb[k % 2][:, half, WIN * (k % 2):], sc, mx[:, half].unsqueeze(2).to_broadcast(
                        [128, 4, KEYS]), ALU.subtract).then_inc(s["x1"], 1)
                elif kind == "Xb":
                    ch = Chain(dve, s_sum, 1, r * NBLK + k)
                    dve.wait_ge(s["e"], r * NBLK + k + 1)
                    wait(dve, s["pn"], r * NBLK + k - 1)
                    ch.link(dve.tensor_reduce(sm[k % 2][:, :], pb[k % 2][:, :, WIN * (k % 2):], AX_X, ALU.add))
                    dve.reciprocal(sm[k % 2][:, :], sm[k % 2][:, :]).then_inc(s["r"], 1)
                elif k == "wo":
                    dve.wait_ge(s["f"], r * 10 + 1)
                    wait(dve, s["out"], r)
                    dve.tensor_tensor(c.H[:, ds(b * N, N)], psF[:, :], c.H[:, ds(b * N, N)], ALU.add).then_inc(s["xf"], 1)
                elif k == "tr":
                    cf = Chain(dve, s_f, 20, r)
                    dve.wait_ge(s["f"], r * 10 + 2)
                    norm_tokens(c, dve, cf, yn, psF[:, :].rearrange("p (t c) -> p t c", t=TILES), stats, mv, rs,
                                1e-5).then_inc(s["yn"], 1)
                    cf.end()
                elif k[0] == "a":
                    n, (at, m) = int(k[1]), CH[int(k[1])]
                    dve.wait_ge(s["f"], r * 10 + 5 + 2 * n)
                    dve.scalar_tensor_tensor(out=hh[0:m, n, :], in0=psF[0:m, :], scalar=cols[0:m, 2 + n:3 + n],
                                             in1=gg[0:m, :], op0=ALU.add, op1=ALU.mult).then_inc(s["hh"], 1)
                else:
                    dve.wait_ge(s["f"], r * 10 + 10)
                    dve.scalar_tensor_tensor(out=c.H[:, ds(b * N, N)], in0=psF[:, :], scalar=cols[:, 8:9],
                                             in1=c.H[:, ds(b * N, N)], op0=ALU.add, op1=ALU.add).then_inc(s["out"], 1)
            dve.wait_ge(s["scl"], 16)
            make_tables(dve, range(2, DEPTH))
            dve.wait_ge(s["tab"], 4 * DEPTH)
            turns(dve, "dve", step)

        @block.gpsimd
        def _(pool):
            pool.memset(xs[:, 0:1], 0.0)
            pool.memset(xsf[:, 0:1], 0.0).then_inc(s["z"], 1)
            for j in range(2):
                pool.memset(qb[j][:, :, :, :, :], 0.0)
            pool.memset(kT[:, :, 0:WIN], 0.0)
            pool.memset(pb[1][:, :, 0:WIN], 0.0).then_inc(s["z"], 1)
            pool.memset(v_even[:, :], 0.0).then_inc(s["z"], 1)
            pool.wait_ge(s["scl"], 16)
            make_tables(pool, range(0, 2))

            def step(kind, k, j, r, b, layer):
                if kind == "Rb":
                    u = r * UT + 4 * k + j
                    xv = raw[k % 2][:, j, :].rearrange("p (h x d) -> p h x d", x=2, d=32)
                    tv = t2[:, :].rearrange("p (h x d) -> p h x d", x=2, d=32)
                    wait(pool, s["qr"], u)
                    c.wait_apart(pool, s["rn"], u + 1)
                    for x in range(2):
                        tab = tabs[:, ds(layer, 1), 2 * (j // 2) + 1, k, 32 * x:32 * x + 32].to_broadcast([128, 8, 32])
                        last = pool.tensor_tensor(tv[:, :, x, :], xv[:, :, 1 - x, :], tab, ALU.mult)
                    last.then_inc(s_pool, 1)
                    pool.wait_ge(s_pool, u + 1)
                    pool.wait_ge(s["t1"], u + 1)
                    pool.tensor_tensor(qr[:, j, :], qr[:, j, :], t2[:, :], ALU.add).then_inc(s["qr"], 1)
                else:
                    pool.wait_ge(s["r"], r * NBLK + k + 1)
                    p = pb[k % 2][:, :, WIN * (k % 2):]
                    pool.tensor_tensor(p, p, sm[k % 2][:, :].unsqueeze(2).to_broadcast([128, PAIRS, KEYS]),
                                       ALU.mult).then_inc(s["pn"], 1)
            pool.wait_ge(s["tab"], 4 * DEPTH)
            turns(pool, "pool", step)


def program(nc, ins, out):
    with ExitStack() as stack:
        c = Core(nc, ins, stack)
        place_tables(c)
        stages = [lambda: setup(c), lambda: adaln(c, 0, 0), lambda: convolutions(c), lambda: linear_attention(c),
                  lambda: feed_forward(c), lambda: adaln(c, 0, 1), lambda: experts(c), lambda: adaln(c, 1, 0),
                  lambda: causal_attention(c), lambda: adaln(c, 1, 1), lambda: windowed_layers(c),
                  lambda: finish(c, out)]
        for stage in stages:
            with ExitStack() as c.stage:
                stage()


def layouts(i):
    A = lambda n: np.asarray(i["L0_attn_" + n])
    E = lambda n: np.asarray(i["L0_ffn_" + n])
    B = lambda n: np.asarray(i["L1_attn_" + n])
    W = lambda n: np.asarray(i["L1_ffn_" + n])
    col = lambda a: a.reshape(-1, D).T
    swap = lambda a: np.concatenate([a[:, 32:], a[:, :32]], 1)
    FF, DEPTH = 341, 6

    def ff_cols(a):
        return np.pad(a, ((0, 0), (0, 3 * D - FF))).reshape(DEPTH, 3, D).transpose(0, 2, 1)

    return {
        "x": np.asarray(i["L0_attn_x"]).reshape(T, D).T,
        "c_cols": np.stack([np.asarray(i["L0_c"]).T, np.asarray(i["L1_c"]).T], 1),
        "w_mod": np.stack([np.asarray(i["L0_wmod"]), np.asarray(i["L1_wmod"])]),
        "tables_all_in": group_array("all"),
        "tables_0_in": group_array("L0"),
        "tables_1_in": group_array("L1"),
        "cols_conv": np.concatenate([A("conv1_w").reshape(D, 20), A("conv2_w").reshape(D, 20), A("conv1_b").reshape(D, 4),
                                     col(A("conv2_b")), col(A("ln0_g")), col(A("ln0_b"))], 1),
        "w_qkv0": np.concatenate([A("Wq"), A("Wk"), A("Wv")], 2),
        "b_kv0": np.concatenate([A("bk"), A("bv")], 1).reshape(1, -1),
        "cols_la": np.stack([A("bq"), A("lnA_g"), A("lnA_b")]).transpose(2, 0, 1),
        "w_ff0a": A("W1"),
        "w_ff0b": A("W2").reshape(4, D, D).transpose(1, 0, 2),
        "cols_ff0": np.concatenate([col(A("b1")), col(A("b2")), col(A("ln2_g")), col(A("ln2_b"))], 1),
        "keys_rw": np.stack([E("keys").T, E("rw").T], 1),
        "rb": E("rb").reshape(1, 16),
        "b2_moe": E("b2"),
        "w1_moe": E("w1").transpose(0, 2, 1),
        "w2_moe": E("w2").reshape(16, D, 4, D).transpose(0, 3, 2, 1),
        "b1_moe": E("b1").reshape(16, 4, D).transpose(0, 2, 1),
        "w_qk1": np.stack([B("Wq"), B("Wk")], 1),
        "w_vdT": B("Wvdown").T,
        "w_vu": B("Wvup"),
        "qk_scales": np.stack([W("q_scale"), swap(W("q_scale")), W("k_scale"), swap(W("k_scale"))], 1).reshape(1, -1),
        "w_qkv1": W("Wqkv"),
        "w_o1": W("Wo").reshape(DEPTH, 8, D, D).transpose(0, 2, 1, 3),
        "w_ff1": W("W1"),
        "w_ff2": np.pad(W("W2"), ((0, 0), (0, 3 * D - FF), (0, 0))).reshape(DEPTH, 3, D, D).transpose(0, 2, 1, 3),
        "cols_w": np.concatenate([W("ln_g")[:, :, None], W("ln_b")[:, :, None], ff_cols(W("b1")[:, :FF]),
                                  ff_cols(W("b1")[:, FF:]), W("b2")[:, :, None]], 2),
    }


def kernel(**inputs):
    import concourse.bacc as _bacc
    from concourse.bass_utils import run_bass_kernel_spmd as _run

    nc = _bacc.Bacc("TRN2", target_bir_lowering=False, num_devices=1)
    arrays, ins = {}, {}
    for name, a in layouts(inputs).items():
        a = np.ascontiguousarray(a)
        arrays[f"in_{name}"] = a
        ins[name] = nc.dram_tensor(f"in_{name}", a.shape, mybir.dt.from_np(a.dtype), kind="ExternalInput").ap()
    out = nc.dram_tensor("out_x", (D, T), F32, kind="ExternalOutput").ap()
    program(nc, ins, out)
    r = _run(nc, [arrays], core_ids=[0])
    return np.ascontiguousarray(r.results[0]["out_x"].T.reshape(NB, N, D))
```
